# Optimizing a Trainium2 kernel written in Bass

```python
import numpy as np
import jax
import jax.numpy as jnp

def _softmax(x, axis=-1):
    return jax.nn.softmax(x, axis=axis)

def _gelu(x):
    return jax.nn.gelu(x, approximate=True)

def _silu(x):
    return jax.nn.silu(x)

def _sigmoid(x):
    return jax.nn.sigmoid(x)

def _layernorm(x, axis=-1, eps=1e-05):
    m = jnp.mean(x, axis=axis, keepdims=True)
    v = jnp.var(x, axis=axis, keepdims=True)
    return (x - m) / jnp.sqrt(v + eps)

def _scatter_add(tgt, idx, src, axis=0):
    return tgt.at[idx].add(src)

def _segment_sum(src, seg, n):
    return jax.ops.segment_sum(src, seg, n)
kernel_name = 'mk_perceiver_d1_seqx_r4_e4efa0'

def setup_inputs(seed: int=0):
    np.random.seed(seed)
    _w = jnp.asarray

    def _rec_inputs():
        import jax
        import jax.numpy as jnp
        _rk = jax.random.key(seed)
        x = 0.002226 + 0.9996 * jax.random.normal(jax.random.fold_in(_rk, 1), (8, 64, 256), jnp.float32)
        _lenS = 64 - jax.random.randint(jax.random.fold_in(_rk, 7), (8,), 0, max(1, 64 // 4) + 1, jnp.int32)
        _lenS2 = 1024 - jax.random.randint(jax.random.fold_in(_rk, 8), (8,), 0, max(1, 1024 // 4) + 1, jnp.int32)
        _ctx_1024P = jax.random.normal(jax.random.fold_in(_rk, 11), (8, 16, 256), jnp.float32)
        _ctx_1024c = jax.random.dirichlet(jax.random.fold_in(_rk, 511), 0.3 * jnp.ones((16,), jnp.float32), (8, 1024))
        _ctx_1024t = jnp.einsum('bsk,bkd->bsd', _ctx_1024c, _ctx_1024P)
        _ctx_1024t = _ctx_1024t * jax.lax.rsqrt(jnp.mean(jnp.square(_ctx_1024t)) + 1e-12) * 0.953939
        ctx_1024 = -0.000125008 + 0.999885 * (_ctx_1024t + 0.3 * jax.random.normal(jax.random.fold_in(_rk, 611), (8, 1024, 256), jnp.float32))
        return (x, ctx_1024)
    x, ctx_1024 = _rec_inputs()

    def _L0_xattn_setup():
        import jax, jax.numpy as jnp
        import numpy as np
        DIM = 256
        HEADS = 16
        DIM_HEAD = 64
        INNER = HEADS * DIM_HEAD
        EPS = 1e-05

        def _layernorm(x, w, b):
            m = jnp.mean(x, axis=-1, keepdims=True)
            v = jnp.mean(jnp.square(x - m), axis=-1, keepdims=True)
            return (x - m) * jax.lax.rsqrt(v + EPS) * w + b
        key = jax.random.key(seed)
        ks = jax.random.split(key, 9)
        B, N, L = (8, 1024, 64)
        x = jax.random.normal(ks[0], (B, N, DIM), dtype=jnp.float32)
        latents = jax.random.normal(ks[1], (B, L, DIM), dtype=jnp.float32)
        s = 1.0 / np.sqrt(DIM)
        Wq = jax.random.normal(ks[2], (DIM, INNER), dtype=jnp.float32) * s
        Wkv = jax.random.normal(ks[3], (DIM, 2 * INNER), dtype=jnp.float32) * s
        Wo = jax.random.normal(ks[4], (INNER, DIM), dtype=jnp.float32) * (1.0 / np.sqrt(INNER))
        ln1_w = jnp.ones((DIM,), jnp.float32)
        ln1_b = jnp.zeros((DIM,), jnp.float32)
        ln2_w = jnp.ones((DIM,), jnp.float32)
        ln2_b = jnp.zeros((DIM,), jnp.float32)
        return {'x': x, 'latents': latents, 'Wq': Wq, 'Wkv': Wkv, 'Wo': Wo, 'ln1_w': ln1_w, 'ln1_b': ln1_b, 'ln2_w': ln2_w, 'ln2_b': ln2_b}
    _L0_xattn_all = _L0_xattn_setup()
    _L0_xattn_in = {k: v for k, v in _L0_xattn_all.items() if k in ('Wq', 'Wkv', 'Wo', 'ln1_w', 'ln1_b', 'ln2_w', 'ln2_b')}
    del _L0_xattn_all

    def _L0_attn_setup():
        import jax, jax.numpy as jnp
        import numpy as np
        D_MODEL = 256
        D_STATE = 16
        D_CONV = 4
        EXPAND = 2
        D_INNER = D_MODEL * EXPAND
        B, L = (4, 512)

        def _forward(x, norm_w, norm_b, W_in, conv_w, conv_b, x_proj_w, dt_w, dt_b, A_log, D, W_out):
            Bsz, Lln, _ = x.shape
            residual = x
            mu = jnp.mean(x, -1, keepdims=True)
            var = jnp.var(x, -1, keepdims=True)
            xn = (x - mu) * jax.lax.rsqrt(var + 1e-05) * norm_w + norm_b
            xz = xn @ W_in
            xc, z = jnp.split(xz, 2, axis=-1)
            x_pad = jnp.pad(xc, ((0, 0), (D_CONV - 1, 0), (0, 0)))
            xc = sum((x_pad[:, k:k + Lln, :] * conv_w[:, k] for k in range(D_CONV))) + conv_b
            xc = jax.nn.silu(xc)
            A = -jnp.exp(A_log)
            dbc = xc @ x_proj_w
            dt = jax.nn.softplus(dbc[..., :1] * dt_w + dt_b)
            Bp = dbc[..., 1:1 + D_STATE]
            Cp = dbc[..., 1 + D_STATE:]

            def step(h, inp):
                x_t, dt_t, B_t, C_t = inp
                A_bar = jnp.exp(dt_t[..., None] * A)
                h = A_bar * h + dt_t[..., None] * B_t[:, None, :] * x_t[..., None]
                y_t = jnp.einsum('bdn,bn->bd', h, C_t)
                return (h, y_t)
            h0 = jnp.zeros((Bsz, D_INNER, D_STATE), xc.dtype)
            xs = (jnp.moveaxis(xc, 1, 0), jnp.moveaxis(dt, 1, 0), jnp.moveaxis(Bp, 1, 0), jnp.moveaxis(Cp, 1, 0))
            _, ys = jax.lax.scan(step, h0, xs)
            y = jnp.moveaxis(ys, 0, 1) + xc * D
            y = y * jax.nn.silu(z)
            return y @ W_out + residual
        key = jax.random.key(seed)
        ks = jax.random.split(key, 12)
        s = lambda k, shape, fan: jax.random.normal(k, shape, jnp.float32) / np.sqrt(fan)
        return {'x': jax.random.normal(ks[0], (B, L, D_MODEL), jnp.float32), 'norm_w': jnp.ones((D_MODEL,), jnp.float32), 'norm_b': jnp.zeros((D_MODEL,), jnp.float32), 'W_in': s(ks[1], (D_MODEL, 2 * D_INNER), D_MODEL), 'conv_w': s(ks[2], (D_INNER, D_CONV), D_CONV), 'conv_b': jnp.zeros((D_INNER,), jnp.float32), 'x_proj_w': s(ks[3], (D_INNER, 2 * D_STATE + 1), D_INNER), 'dt_w': s(ks[4], (D_INNER,), 1), 'dt_b': jnp.zeros((D_INNER,), jnp.float32), 'A_log': jax.random.normal(ks[5], (D_INNER, D_STATE), jnp.float32) * 0.5, 'D': jnp.ones((D_INNER,), jnp.float32), 'W_out': s(ks[6], (D_INNER, D_MODEL), D_INNER)}
    _L0_attn_all = _L0_attn_setup()
    _L0_attn_in = {k: v for k, v in _L0_attn_all.items() if k in ('norm_w', 'norm_b', 'W_in', 'conv_w', 'conv_b', 'x_proj_w', 'dt_w', 'dt_b', 'A_log', 'D', 'W_out')}
    del _L0_attn_all

    def _L0_ffn_setup():
        import jax, jax.numpy as jnp
        import numpy as np
        S, B, D, E, C, FF = (512, 4, 256, 8, 512, 1024)
        N = S * B
        key = jax.random.key(seed)
        ks = jax.random.split(key, 7)
        return {'hidden_states': jax.random.normal(ks[0], (S, B, D), dtype=jnp.float32), 'combine_weights': jax.random.uniform(ks[1], (N, E), dtype=jnp.float32), 'top_idx': jax.random.randint(ks[2], (C, E), 0, N, dtype=jnp.int64), 'W1': jax.random.normal(ks[3], (E, D, FF), dtype=jnp.float32) * (1.0 / np.sqrt(D)), 'b1': jnp.zeros((E, FF), dtype=jnp.float32), 'W2': jax.random.normal(ks[4], (E, FF, D), dtype=jnp.float32) * (1.0 / np.sqrt(FF)), 'b2': jnp.zeros((E, D), dtype=jnp.float32)}
    _L0_ffn_all = _L0_ffn_setup()
    _L0_ffn_in = {k: v for k, v in _L0_ffn_all.items() if k in ('combine_weights', 'top_idx', 'W1', 'b1', 'W2', 'b2')}
    del _L0_ffn_all
    return {'x': x, 'ctx_1024': ctx_1024, 'L0_xattn_Wq': _L0_xattn_in['Wq'], 'L0_xattn_Wkv': _L0_xattn_in['Wkv'], 'L0_xattn_Wo': _L0_xattn_in['Wo'], 'L0_xattn_ln1_w': _L0_xattn_in['ln1_w'], 'L0_xattn_ln1_b': _L0_xattn_in['ln1_b'], 'L0_xattn_ln2_w': _L0_xattn_in['ln2_w'], 'L0_xattn_ln2_b': _L0_xattn_in['ln2_b'], 'L0_attn_norm_w': _L0_attn_in['norm_w'], 'L0_attn_norm_b': _L0_attn_in['norm_b'], 'L0_attn_W_in': _L0_attn_in['W_in'], 'L0_attn_conv_w': _L0_attn_in['conv_w'], 'L0_attn_conv_b': _L0_attn_in['conv_b'], 'L0_attn_x_proj_w': _L0_attn_in['x_proj_w'], 'L0_attn_dt_w': _L0_attn_in['dt_w'], 'L0_attn_dt_b': _L0_attn_in['dt_b'], 'L0_attn_A_log': _L0_attn_in['A_log'], 'L0_attn_D': _L0_attn_in['D'], 'L0_attn_W_out': _L0_attn_in['W_out'], 'L0_ffn_combine_weights': _L0_ffn_in['combine_weights'], 'L0_ffn_top_idx': _L0_ffn_in['top_idx'], 'L0_ffn_W1': _L0_ffn_in['W1'], 'L0_ffn_b1': _L0_ffn_in['b1'], 'L0_ffn_W2': _L0_ffn_in['W2'], 'L0_ffn_b2': _L0_ffn_in['b2']}

def reference(x, ctx_1024, L0_xattn_Wq, L0_xattn_Wkv, L0_xattn_Wo, L0_xattn_ln1_w, L0_xattn_ln1_b, L0_xattn_ln2_w, L0_xattn_ln2_b, L0_attn_norm_w, L0_attn_norm_b, L0_attn_W_in, L0_attn_conv_w, L0_attn_conv_b, L0_attn_x_proj_w, L0_attn_dt_w, L0_attn_dt_b, L0_attn_A_log, L0_attn_D, L0_attn_W_out, L0_ffn_combine_weights, L0_ffn_top_idx, L0_ffn_W1, L0_ffn_b1, L0_ffn_W2, L0_ffn_b2):
    import jax
    import jax.numpy as jnp

    def _L0_xattn_ref(x, latents, Wq, Wkv, Wo, ln1_w, ln1_b, ln2_w, ln2_b):
        import jax, jax.numpy as jnp
        import numpy as np
        DIM = 256
        HEADS = 16
        DIM_HEAD = 64
        INNER = HEADS * DIM_HEAD
        EPS = 1e-05

        def _layernorm(x, w, b):
            m = jnp.mean(x, axis=-1, keepdims=True)
            v = jnp.mean(jnp.square(x - m), axis=-1, keepdims=True)
            return (x - m) * jax.lax.rsqrt(v + EPS) * w + b
        B, L, _ = latents.shape
        xn = _layernorm(x, ln1_w, ln1_b)
        ln = _layernorm(latents, ln2_w, ln2_b)
        q = ln @ Wq
        kv_input = jnp.concatenate([xn, ln], axis=-2)
        kv = kv_input @ Wkv
        k, v = jnp.split(kv, 2, axis=-1)

        def heads(t):
            b, s, _ = t.shape
            return t.reshape(b, s, HEADS, DIM_HEAD).transpose(0, 2, 1, 3)
        q, k, v = (heads(q), heads(k), heads(v))
        scale = 1.0 / np.sqrt(np.sqrt(DIM_HEAD))
        logits = jnp.einsum('bhld,bhsd->bhls', q * scale, k * scale)
        w = jax.nn.softmax(logits.astype(jnp.float32), axis=-1).astype(logits.dtype)
        out = jnp.einsum('bhls,bhsd->bhld', w, v)
        out = out.transpose(0, 2, 1, 3).reshape(B, L, INNER)
        return out @ Wo

    def _L0_attn_ref(x, norm_w, norm_b, W_in, conv_w, conv_b, x_proj_w, dt_w, dt_b, A_log, D, W_out):
        import jax, jax.numpy as jnp
        import numpy as np
        D_MODEL = 256
        D_STATE = 16
        D_CONV = 4
        EXPAND = 2
        D_INNER = D_MODEL * EXPAND
        B, L = (4, 512)

        def _forward(x, norm_w, norm_b, W_in, conv_w, conv_b, x_proj_w, dt_w, dt_b, A_log, D, W_out):
            Bsz, Lln, _ = x.shape
            residual = x
            mu = jnp.mean(x, -1, keepdims=True)
            var = jnp.var(x, -1, keepdims=True)
            xn = (x - mu) * jax.lax.rsqrt(var + 1e-05) * norm_w + norm_b
            xz = xn @ W_in
            xc, z = jnp.split(xz, 2, axis=-1)
            x_pad = jnp.pad(xc, ((0, 0), (D_CONV - 1, 0), (0, 0)))
            xc = sum((x_pad[:, k:k + Lln, :] * conv_w[:, k] for k in range(D_CONV))) + conv_b
            xc = jax.nn.silu(xc)
            A = -jnp.exp(A_log)
            dbc = xc @ x_proj_w
            dt = jax.nn.softplus(dbc[..., :1] * dt_w + dt_b)
            Bp = dbc[..., 1:1 + D_STATE]
            Cp = dbc[..., 1 + D_STATE:]

            def step(h, inp):
                x_t, dt_t, B_t, C_t = inp
                A_bar = jnp.exp(dt_t[..., None] * A)
                h = A_bar * h + dt_t[..., None] * B_t[:, None, :] * x_t[..., None]
                y_t = jnp.einsum('bdn,bn->bd', h, C_t)
                return (h, y_t)
            h0 = jnp.zeros((Bsz, D_INNER, D_STATE), xc.dtype)
            xs = (jnp.moveaxis(xc, 1, 0), jnp.moveaxis(dt, 1, 0), jnp.moveaxis(Bp, 1, 0), jnp.moveaxis(Cp, 1, 0))
            _, ys = jax.lax.scan(step, h0, xs)
            y = jnp.moveaxis(ys, 0, 1) + xc * D
            y = y * jax.nn.silu(z)
            return y @ W_out + residual
        return _forward(x, norm_w, norm_b, W_in, conv_w, conv_b, x_proj_w, dt_w, dt_b, A_log, D, W_out)

    def _L0_ffn_ref(hidden_states, combine_weights, top_idx, W1, b1, W2, b2):
        import jax, jax.numpy as jnp
        import numpy as np
        S, B, D, E, C, FF = (512, 4, 256, 8, 512, 1024)
        N = S * B
        s, b, d = hidden_states.shape
        x = hidden_states.reshape(-1, d)
        tok = top_idx.T
        gathered = x[tok]
        h = jax.nn.gelu(jnp.einsum('ecd,edf->ecf', gathered, W1) + b1[:, None, :])
        out_e = jnp.einsum('ecf,efd->ecd', h, W2) + b2[:, None, :]
        e_ids = jnp.arange(tok.shape[0])[:, None]
        w = combine_weights[tok, e_ids]
        weighted = (out_e * w[..., None]).reshape(-1, d)
        out = jnp.zeros_like(x).at[tok.reshape(-1)].add(weighted)
        return out.reshape(s, b, d)
    x = x + _L0_xattn_ref(ctx_1024, _layernorm(x, axis=-1), L0_xattn_Wq, L0_xattn_Wkv, L0_xattn_Wo, L0_xattn_ln1_w, L0_xattn_ln1_b, L0_xattn_ln2_w, L0_xattn_ln2_b)
    x = x + _L0_attn_ref(_layernorm(x, axis=-1), L0_attn_norm_w, L0_attn_norm_b, L0_attn_W_in, L0_attn_conv_w, L0_attn_conv_b, L0_attn_x_proj_w, L0_attn_dt_w, L0_attn_dt_b, L0_attn_A_log, L0_attn_D, L0_attn_W_out)
    x = x + _L0_ffn_ref(_layernorm(x, axis=-1), L0_ffn_combine_weights, L0_ffn_top_idx, L0_ffn_W1, L0_ffn_b1, L0_ffn_W2, L0_ffn_b2)
    return x

_drawn_inputs = setup_inputs


def setup_inputs(seed=0):
    import zlib

    import numpy as np

    out = dict(_drawn_inputs(seed))
    spreads = {'L0_xattn_ln1_w': (1.0, 0.2),
     'L0_xattn_ln1_b': (0.0, 0.1),
     'L0_xattn_ln2_w': (1.0, 0.2),
     'L0_xattn_ln2_b': (0.0, 0.344),
     'L0_attn_norm_w': (1.0, 0.2),
     'L0_attn_norm_b': (0.0, 0.1),
     'L0_attn_conv_b': (0.0, 0.1),
     'L0_attn_dt_b': (0.0, 0.504),
     'L0_attn_D': (1.0, 0.2),
     'L0_ffn_b1': (0.0, 0.313),
     'L0_ffn_b2': (0.0, 0.1)}
    factors = {}
    for name, (base, spread) in spreads.items():
        noise = np.random.default_rng([zlib.crc32(name.encode()), seed]).standard_normal(out[name].shape)
        drawn = base * np.exp(spread * noise) if base else spread * noise
        out[name] = jnp.asarray(drawn.astype(out[name].dtype))
    for name, factor in factors.items():
        out[name] = (out[name] * factor).astype(out[name].dtype)
    return out
```

```python
from contextlib import ExitStack

import concourse.bass as bass
from concourse import mybir

F32 = mybir.dt.float32
F32R = mybir.dt.float32r
BF16 = mybir.dt.bfloat16
I32 = mybir.dt.int32
ALU = mybir.AluOpType
ACT = mybir.ActivationFunctionType
X = mybir.AxisListType.X
ds = bass.ds

P = 128
EPS = 1e-5


def perceiver_kernel(nc, x, ctx_in, Wq, Wkv, Wo, ln1_w, ln1_b, ln2_w, ln2_b,
                     norm_w, norm_b, W_in, conv_w, conv_b, x_proj_w, dt_w, dt_b, A_log, D_skip, W_out,
                     combine_w, top_idx, W1, b1, W2, b2, out):
    B, L, C = x.shape
    S = ctx_in.shape[1]
    INNER = Wq.shape[1]
    DH = 64
    HP = INNER // (2 * DH)
    CK = C // P
    SJ = S // P
    T = B * L
    TT = T // P
    BP = P // L
    DI = conv_w.shape[0]
    DT = DI // P
    TAPS = conv_w.shape[1]
    NS = A_log.shape[1]
    NX = x_proj_w.shape[1]
    E, _, FF = W1.shape
    FT = FF // P
    SLOTS = top_idx.shape[0]
    SC = SLOTS // P
    SCALE = float(DH) ** -0.5
    GT = 4
    MISC = 8
    assert HP == MISC and C == 2 * P and P == 2 * L and SJ == 8 and TT * P == T == 512

    top = ExitStack()
    with top:
        def sem(name):
            return top.enter_context(nc.semaphore(name))

        def sb(stack, name, shape, dt=F32):
            return stack.enter_context(nc.sbuf_tensor(name, shape, dt))

        def row(v):
            return v.rearrange("(a d) -> a d", a=1)

        ident = sb(top, "ident", [P, P])
        x1 = sb(top, "x1", [P, TT, C])
        iota_t = None

        bank = [top.enter_context(nc.psum_tensor(f"bank{i}", [P, 512], F32)) for i in range(8)] if False else None
        psum = top.enter_context(nc.psum_tensor("psum", [P, 8, 512], F32))

        att = ExitStack()
        ctx_nat = sb(att, "ctx_nat", [P, SJ, C])
        kvn_hi = [sb(att, "kvn_hi0", [P, SJ, C], F32R), None]
        kvn_lo = [sb(att, "kvn_lo0", [P, SJ, C], F32R), None]
        kvt_hi = [sb(att, f"kvt_hi{i}", [P, CK, S], F32R) for i in range(2)]
        kvt_lo = [sb(att, f"kvt_lo{i}", [P, CK, S], F32R) for i in range(2)]
        qk_hi = [sb(att, f"qk_hi{i}", [P, CK, HP, 2, L], F32R) for i in range(2)]
        qk_lo = [sb(att, f"qk_lo{i}", [P, CK, HP, 2, L], F32R) for i in range(2)]
        lat_hi = sb(att, "lat_hi", [L, B, C], F32R)
        lat_lo = sb(att, "lat_lo", [L, B, C], F32R)
        latt_hi = sb(att, "latt_hi", [P, CK, T], F32R)
        latt_lo = sb(att, "latt_lo", [P, CK, T], F32R)
        q_t = sb(att, "q_t", [P, HP, T])
        q_cur = sb(att, "q_cur", [P, HP, L])
        wk_t = sb(att, "wk_t", [P, HP, C])
        wv = sb(att, "wv", [P, CK, INNER])
        wo = sb(att, "wo", [P, HP, C])
        prob = sb(att, "prob", [P, S])
        prob_lat = [sb(att, f"prob_lat{i}", [P, L]) for i in range(2)]
        y_n = sb(att, "y_n", [P, C])
        y_t = sb(att, "y_t", [P, CK, P])
        o_t = sb(att, "o_t", [P, HP, P])
        ln1wb = sb(att, "ln1wb", [P, 2, C])
        cstat = sb(att, "cstat", [P, SJ, 6])
        cmv = sb(att, "cmv", [P, SJ, 2])
        cvar = sb(att, "cvar", [P, SJ])
        crstd = sb(att, "crstd", [P, SJ])
        cnm = sb(att, "cnm", [P, SJ])
        cshift = sb(att, "cshift", [P, SJ])
        mhalf = sb(att, "mhalf", [P, SJ])
        rowmax = [sb(att, f"rowmax{i}", [P, HP]) for i in range(2)]
        latmax = [sb(att, f"latmax{i}", [P, HP]) for i in range(2)]
        nbias = [sb(att, f"nbias{i}", [P, HP]) for i in range(2)]
        den_ctx = [sb(att, f"den_ctx{i}", [P, HP]) for i in range(2)]
        den_lat = [sb(att, f"den_lat{i}", [P, HP]) for i in range(2)]
        den = [sb(att, f"den{i}", [P, HP]) for i in range(2)]
        rden = [sb(att, f"rden{i}", [P, HP]) for i in range(2)]
        pro = ExitStack()
        wq_sb = sb(pro, "wq_sb", [P, CK, INNER])
        wk_nat = sb(pro, "wk_nat", [P, CK, INNER])
        x_lat = sb(pro, "x_lat", [L, B, C])
        latt = sb(pro, "latt", [P, CK, T])
        ln2wb = sb(pro, "ln2wb", [L, 2, C])
        pro.close()
        kvn_hi[1] = sb(att, "kvn_hi1", [P, SJ, C], F32R)
        kvn_lo[1] = sb(att, "kvn_lo1", [P, SJ, C], F32R)
        pt_hi = [sb(att, f"pt_hi{i}", [P, SJ + 1, P], F32R) for i in range(2)]
        pt_lo = [sb(att, f"pt_lo{i}", [P, SJ + 1, P], F32R) for i in range(2)]
        att.close()

        mam = ExitStack()
        win = sb(mam, "win", [P, CK, 2 * DI])
        wout = sb(mam, "wout", [P, DT, C])
        wxp = sb(mam, "wxp", [P, DT, NX])
        convw = sb(mam, "convw", [P, DT, TAPS])
        dvec = sb(mam, "dvec", [P, 4, DT])
        a_neg = sb(mam, "a_neg", [P, DT, NS])
        nwb = sb(mam, "nwb", [P, 2, C])
        mres = sb(mam, "mres", [P, TT, C])
        xn = sb(mam, "xn", [P, TT, C])
        xn_t = sb(mam, "xn_t", [P, CK, T])
        xpad = sb(mam, "xpad", [P, DT, B, L + TAPS - 1])
        conv = sb(mam, "conv", [P, DT, T])
        xc = sb(mam, "xc", [P, DT, T])
        zs = sb(mam, "zs", [P, DT, T])
        dts = sb(mam, "dts", [P, DT, T])
        dtx = sb(mam, "dtx", [P, DT, T])
        sel = sb(mam, "sel", [NX, NX, P], F32R)
        dbc_hi = sb(mam, "dbc_hi", [NX, T], F32R)
        dbc_lo = sb(mam, "dbc_lo", [NX, T], F32R)
        bmat = [sb(mam, f"bmat{i}", [P, T]) for i in range(2)]
        dec = [sb(mam, f"dec{i}", [P, DT, T]) for i in range(2)]
        drive = [sb(mam, f"drive{i}", [P, DT, T]) for i in range(2)]
        state = [sb(mam, f"state{i}", [P, DT, T]) for i in range(2)]
        read = [sb(mam, f"read{i}", [P, DT, T]) for i in range(2)]
        tstat = sb(mam, "tstat", [P, TT, 6])
        tmv = sb(mam, "tmv", [P, TT, 2])
        tvar = sb(mam, "tvar", [P, TT])
        trstd = sb(mam, "trstd", [P, TT])
        tnm = sb(mam, "tnm", [P, TT])
        tshift = sb(mam, "tshift", [P, TT])
        thalf = sb(mam, "thalf", [P, TT])
        mam.close()

        ffn = ExitStack()
        ffn.enter_context(nc.sbuf_tensor("hold", [P, 2048], F32)) if False else None
        w1 = [sb(ffn, f"w1_{i}", [P, CK, FF]) for i in range(2)]
        w2 = [sb(ffn, f"w2_{i}", [P, FT, C]) for i in range(2)]
        hid = sb(ffn, "hid", [P, FT, T])
        f_nat = sb(ffn, "f_nat", [P, TT, C])
        f_t = sb(ffn, "f_t", [P, CK, T])
        acc = sb(ffn, "acc", [P, TT, C])
        b1_rows = sb(ffn, "b1_rows", [E * FT, P])
        b1_t = sb(ffn, "b1_t", [P, E * FT])
        b2_sb = sb(ffn, "b2_sb", [E, C])
        idx_i = sb(ffn, "idx_i", [P, SC, E], I32)
        idx_f = sb(ffn, "idx_f", [P, SC, E])
        iota_i = sb(ffn, "iota_i", [P, T], I32)
        iota_f = sb(ffn, "iota_f", [P, T])
        onehot = [sb(ffn, f"onehot{i}", [P, SC, T], BF16) for i in range(2)]
        ones = sb(ffn, "ones", [P, 2], BF16)
        comb = sb(ffn, "comb", [P, TT, E])
        coef = sb(ffn, "coef", [P, TT, E])
        coef_t = sb(ffn, "coef_t", [E, T])
        fstat = sb(ffn, "fstat", [P, TT, 6])
        fmv = sb(ffn, "fmv", [P, TT, 2])
        fvar = sb(ffn, "fvar", [P, TT])
        frstd = sb(ffn, "frstd", [P, TT])
        fnm = sb(ffn, "fnm", [P, TT])
        fshift = sb(ffn, "fshift", [P, TT])
        fhalf = sb(ffn, "fhalf", [P, TT])
        ffn.close()

        LG, TP, PV, LAT, OC, MB = psum[:, 0:2, :], [psum[:, 2, :], psum[:, 3, :]], psum[:, 4, 0:C], \
            psum[:, 5, :], psum[:, 6, :], psum[:, 7, :]

        ld_xlat, ld_vec, ld_wq, ld_wk, ld_wvo, ld_ctx = (sem(n) for n in (
            "ld_xlat", "ld_vec", "ld_wq", "ld_wk", "ld_wvo", "ld_ctx"))
        ld_mam, ld_ffn, ld_out = sem("ld_mam"), sem("ld_ffn"), sem("ld_out")
        ld_e = [sem(f"ld_e{i}") for i in range(2)]
        s_dve, s_pool, s_act, s_pe = sem("s_dve"), sem("s_pool"), sem("s_act"), sem("s_pe")
        s_apart = sem("s_apart")
        s_id, s_pstat, s_pln, s_platt, s_pevac, s_pq, s_pqe, s_pwk, s_pwke, s_plo = (sem(n) for n in (
            "s_id", "s_pstat", "s_pln", "s_platt", "s_pevac", "s_pq", "s_pqe", "s_pwk", "s_pwke", "s_plo"))
        s_cst, s_cmv, s_cvar, s_crs, s_cnm, s_csh, s_cz, s_cw, s_cn, s_khi, s_klo, s_qcur = (sem(n) for n in (
            "s_cst", "s_cmv", "s_cvar", "s_crs", "s_cnm", "s_csh", "s_cz", "s_cw", "s_cn", "s_khi", "s_klo",
            "s_qcur"))
        s_misc, s_mhi, s_mlo = sem("s_misc"), sem("s_mhi"), sem("s_mlo")
        s_latl, s_latm = sem("s_latl"), sem("s_latm")
        (s_lg, s_mx, s_nb, s_exp, s_expl, s_tA, s_tB, s_tC, s_hA, s_hB, s_hC, s_lA, s_lB, s_lC,
         s_den, s_rd, s_pv, s_y, s_yt, s_yte, s_o, s_oe) = (sem(n) for n in (
             "s_lg", "s_mx", "s_nb", "s_exp", "s_expl", "s_tA", "s_tB", "s_tC", "s_hA", "s_hB", "s_hC",
             "s_lA", "s_lB", "s_lC", "s_den", "s_rd", "s_pv", "s_y", "s_yt", "s_yte", "s_o", "s_oe"))
        s_wo, s_woe = sem("s_wo"), sem("s_woe")
        (m_stat, m_ln, m_xt, m_xte, m_xz, m_xze, m_zz, m_conv, m_xc, m_dbc, m_dhi, m_dlo, m_dt0, m_dtu, m_dta,
         m_dtx, m_sel, m_aneg, m_b, m_bs, m_c, m_dec, m_z0, m_drv, m_scan, m_rd, m_acc, m_y, m_out) = (
            sem("m_" + n) for n in (
                "stat ln xt xte xz xze zz conv xc dbc dhi dlo dt0 dtu dta dtx sel aneg b bs c dec z0 drv scan rd "
                "acc y out").split())
        (f_stat, f_ln, f_x, f_xe, f_b1, f_cast, f_iota, f_oh, f_cnt, f_coef, f_ct, f_cte, f_b2, f_h, f_he, f_o,
         f_oe, f_done) = (sem("f_" + n) for n in (
             "stat ln x xe b1 cast iota oh cnt coef ct cte b2 h he o oe done").split())

        def count(b, hp):
            return HP * b + hp + 1

        def back(b, slot, hp, n):
            if hp >= n:
                return b, slot, hp - n
            if isinstance(b, int) and b == 0:
                return None
            return b - 1, 1 - slot, hp - n + HP

        def apart(eng):
            eng.sem_inc(s_apart, 1)

        def misc_count(b, m):
            return MISC * b + m + 1

        def misc_dst(slot, m, hi):
            k, h = m % 4 // 2, m % 2
            if m < 4:
                return (qk_hi if hi else qk_lo)[slot][:, k, :, h, :]
            return (kvt_hi if hi else kvt_lo)[slot][:, k, h * 512:(h + 1) * 512]

        def misc_src(m):
            return MB.rearrange("p (a l) -> p a l", l=L) if m < 4 else MB

        def all_steps(loops, body, drain):
            body(0, 0, True, None)
            with loops.Fori(0, B // 2 - 1) as p:
                body(2 * p + 1, 1, True, None)
                body(2 * p + 2, 0, True, p)
            body(B - 1, 1, False, None)
            drain(B, 0, B // 2 - 1)

        block = top.enter_context(nc.Block())

        @block.sync
        def _(sp):
            sp.dma_start(x_lat[:], x.rearrange("b l c -> l b c")).then_inc(ld_xlat, 16)
            sp.dma_start(ctx_nat[:], ctx_in[0].rearrange("(p j) c -> p j c", j=SJ)).then_inc(ld_ctx, 16)
            for i, v in enumerate((ln1_w, ln1_b)):
                sp.dma_start(ln1wb[:, i, :], row(v).to_broadcast((P, C))).then_inc(ld_vec, 16)
            for i, v in enumerate((ln2_w, ln2_b)):
                sp.dma_start(ln2wb[:, i, :], row(v).to_broadcast((L, C))).then_inc(ld_vec, 16)
            sp.dma_start(wq_sb[:], Wq.rearrange("(k p) n -> p k n", p=P)).then_inc(ld_wq, 16)
            wkv = Wkv.rearrange("(k p) n -> p k n", p=P)
            sp.dma_start(wk_nat[:], wkv[:, :, 0:INNER]).then_inc(ld_wk, 16)
            sp.dma_start(wv[:], wkv[:, :, INNER:2 * INNER]).then_inc(ld_wvo, 16)
            sp.dma_start(wo[:], Wo.rearrange("(h p) n -> p h n", p=P)).then_inc(ld_wvo, 16)
            sp.dma_start(x1[:], x.rearrange("(t b) l c -> (b l) t c", b=BP)).then_inc(ld_wvo, 16)
            with sp.Fori(1, B) as b:
                sp.wait_ge(s_misc, MISC * b)
                sp.wait_ge(s_klo, b)
                sp.dma_start(ctx_nat[:], ctx_in[ds(b, 1)].rearrange("a (p j) c -> p (a j) c", j=SJ))\
                    .then_inc(ld_ctx, 16)
            sp.wait_ge(s_woe, B // 2)
            sp.wait_ge(s_pool, 1)
            sp.dma_start(win[:], W_in.rearrange("(k p) n -> p k n", p=P)).then_inc(ld_mam, 16)
            sp.dma_start(wout[:], W_out.rearrange("(k p) n -> p k n", p=P)).then_inc(ld_mam, 16)
            sp.dma_start(wxp[:], x_proj_w.rearrange("(k p) n -> p k n", p=P)).then_inc(ld_mam, 16)
            sp.dma_start(convw[:], conv_w.rearrange("(k p) n -> p k n", p=P)).then_inc(ld_mam, 16)
            with nc.allow_non_contiguous_dma(reason="four short vectors"):
                for i, v in enumerate((conv_b, dt_w, dt_b, D_skip)):
                    sp.dma_start(dvec[:, i, :], v.rearrange("(k p) -> p k", p=P)).then_inc(ld_mam, 16)
            sp.dma_start(a_neg[:], A_log.rearrange("(k p) n -> p k n", p=P)).then_inc(ld_mam, 16)
            for i, v in enumerate((norm_w, norm_b)):
                sp.dma_start(nwb[:, i, :], row(v).to_broadcast((P, C))).then_inc(ld_mam, 16)
            sp.wait_ge(m_out, TT)
            sp.dma_start(idx_i[:], top_idx.rearrange("(j p) e -> p j e", p=P)).then_inc(ld_ffn, 16)
            sp.dma_start(comb[:], combine_w[0:T, :].rearrange("(t p) e -> p t e", p=P)).then_inc(ld_ffn, 16)
            sp.dma_start(b1_rows[:], b1.rearrange("e (f p) -> (e f) p", p=P)).then_inc(ld_ffn, 16)
            sp.dma_start(b2_sb[:], b2).then_inc(ld_ffn, 16)

            def load_expert(e, i):
                sp.dma_start(w1[i][:], W1[ds(e, 1)].rearrange("a (k p) n -> p (a k) n", p=P)).then_inc(ld_e[i], 16)
                sp.dma_start(w2[i][:], W2[ds(e, 1)].rearrange("a (k p) n -> p (a k) n", p=P)).then_inc(ld_e[i], 16)

            load_expert(0, 0)
            load_expert(1, 1)
            with sp.Fori(1, E // 2) as q:
                for i in range(2):
                    sp.wait_ge(f_o, TT * (2 * q - 1 + i))
                    load_expert(2 * q + i, i)
            for t in range(TT):
                sp.wait_ge(f_done, t + 1)
                sp.dma_start(out.rearrange("(t b) l c -> t (b l) c", b=BP)[t], acc[:, t, :]).then_inc(ld_out, 16)
            sp.wait_ge(ld_out, 16 * TT)

        @block.gpsimd
        def _(pool):
            done = [0]

            def link(ins):
                done[0] += 1
                ins.then_inc(s_pool, 1)
                pool.wait_ge(s_pool, done[0])

            def layernorm(rows, var, rstd, nm, shift, half, mv, src, dst, j_n, wb=None):
                link(pool.tensor_scalar(var[0:rows], mv[0:rows, :, 1], 1.0, EPS, ALU.mult, ALU.add))
                link(pool.tensor_tensor(rstd[0:rows], var[0:rows], half[0:rows], ALU.pow))
                link(pool.tensor_tensor(nm[0:rows], mv[0:rows, :, 0], rstd[0:rows], ALU.mult))
                link(pool.tensor_scalar(shift[0:rows], nm[0:rows], -1.0, 0.0, ALU.mult, ALU.add))
                for j in range(j_n):
                    last = pool.tensor_scalar(dst[:, j, :], src[:, j, :], rstd[0:rows, j:j + 1],
                                              shift[0:rows, j:j + 1], ALU.mult, ALU.add)
                if wb is None:
                    return last
                link(last)
                shape = (rows, j_n, C)
                link(pool.tensor_tensor(dst[:], dst[:], wb[:, 0:1, :].to_broadcast(shape), ALU.mult))
                return pool.tensor_tensor(dst[:], dst[:], wb[:, 1:2, :].to_broadcast(shape), ALU.add)

            link(pool.memset(ident[:], 0.0))
            pool.affine_select(out=ident[:], in_=ident[:], compare_op=ALU.not_equal, fill=1.0, base=0,
                               pattern=[[-1, P]], channel_multiplier=1).then_inc(s_id, 1)
            link(pool.memset(mhalf[:], -0.5))
            pool.wait_ge(s_pstat, 1)
            layernorm(L, cvar, crstd, cnm, cshift, mhalf, cmv[0:L], x_lat, x_lat, B).then_inc(s_pln, 1)
            pool.wait_ge(s_pstat, 2)
            pool.wait_ge(ld_vec, 64)
            link(layernorm(L, cvar, crstd, cnm, cshift, mhalf, cmv[0:L], x_lat, x_lat, B, ln2wb))
            link(pool.tensor_scalar(lat_hi[:], x_lat[:], 1.0, 0.0, ALU.mult, ALU.add))
            pool.sem_inc(s_pln, 1)
            pool.tensor_tensor(lat_lo[:], x_lat[:], lat_hi[:].bitcast(F32), ALU.subtract).then_inc(s_plo, 1)

            def queries(b):
                if not (isinstance(b, int) and b == 0):
                    pool.wait_ge(s_misc, MISC * (b - 1) + 4)
                else:
                    pool.wait_ge(s_pqe, HP)
                apart(pool)
                pool.tensor_copy(q_cur[:], q_t[:, :, ds(b * L, L)])\
                    .then_inc(s_qcur, 1)

            def context(b, slot):
                pool.wait_ge(s_cmv, b + 1)
                apart(pool)
                pool.tensor_scalar(cvar[:], cmv[:, :, 1], 1.0, EPS, ALU.mult, ALU.add).then_inc(s_cvar, 1)
                pool.wait_ge(s_cvar, b + 1)
                pool.tensor_tensor(crstd[:], cvar[:], mhalf[:], ALU.pow).then_inc(s_crs, 1)
                pool.wait_ge(s_crs, b + 1)
                pool.tensor_tensor(cnm[:], cmv[:, :, 0], crstd[:], ALU.mult).then_inc(s_cnm, 1)
                pool.wait_ge(s_cnm, b + 1)
                apart(pool)
                pool.tensor_scalar(cshift[:], cnm[:], -1.0, 0.0, ALU.mult, ALU.add).then_inc(s_csh, 1)
                pool.wait_ge(s_csh, b + 1)
                apart(pool)
                for j in range(SJ):
                    z = pool.tensor_scalar(ctx_nat[:, j, :], ctx_nat[:, j, :], crstd[:, j:j + 1],
                                           cshift[:, j:j + 1], ALU.mult, ALU.add)
                z.then_inc(s_cz, 1)
                pool.wait_ge(s_cz, b + 1)
                shape = (P, SJ, C)
                pool.tensor_tensor(ctx_nat[:], ctx_nat[:], ln1wb[:, 0:1, :].to_broadcast(shape), ALU.mult)\
                    .then_inc(s_cw, 1)
                pool.wait_ge(s_cw, b + 1)
                pool.tensor_tensor(ctx_nat[:], ctx_nat[:], ln1wb[:, 1:2, :].to_broadcast(shape), ALU.add)\
                    .then_inc(s_cn, 1)
                pool.wait_ge(s_cn, b + 1)
                if not (isinstance(b, int) and b < 2):
                    pool.wait_ge(s_pv, HP * (b - 1))
                apart(pool)
                pool.tensor_scalar(kvn_hi[slot][:], ctx_nat[:], 1.0, 0.0, ALU.mult, ALU.add).then_inc(s_khi, 1)
                pool.wait_ge(s_khi, b + 1)
                pool.tensor_tensor(kvn_lo[slot][:], ctx_nat[:], kvn_hi[slot][:].bitcast(F32), ALU.subtract)\
                    .then_inc(s_klo, 1)

            context(0, 0)
            queries(0)
            pool.wait_ge(s_misc, MISC)

            def body(b, slot, more, pair):
                if more:
                    queries(b + 1)
                    context(b + 1, 1 - slot)

            all_steps(pool, body, lambda b, slot, pair: None)

            pool.wait_ge(s_woe, B // 2)
            link(pool.memset(thalf[:], -0.5))
            link(pool.memset(xpad[:], 0.0))
            selw = state[0][0:NX, :, :].rearrange("p a b -> p (a b)")

            half_n = (NX + 2) // 3
            for i in range(3):
                n0, n1 = half_n * i, min(NX, half_n * (i + 1))
                w = (n1 - n0) * P
                view = selw[:, 0:w].rearrange("p (n m) -> p n m", m=P)
                link(pool.memset(selw[:, 0:w], 0.0))
                link(pool.affine_select(out=view, in_=view, compare_op=ALU.not_equal, fill=1.0, base=-n0,
                                        pattern=[[-1, n1 - n0], [0, P]], channel_multiplier=1))
                link(pool.tensor_scalar(sel[:, n0:n1, :], view, 1.0, 0.0, ALU.mult, ALU.add))
            pool.sem_inc(m_sel, 1)
            pool.wait_ge(m_stat, 1)
            layernorm(P, tvar, trstd, tnm, tshift, thalf, tmv, x1, mres, TT).then_inc(m_ln, 1)
            pool.wait_ge(m_stat, 2)
            pool.wait_ge(ld_mam, 16 * 11)
            layernorm(P, tvar, trstd, tnm, tshift, thalf, tmv, mres, xn, TT, nwb).then_inc(m_ln, 1)
            for n in range(NS):
                i = n % 2
                pool.wait_ge(m_dec, n + 1)
                pool.memset(dec[i][:].rearrange("p a (b l) -> p (a b) l", l=L)[:, :, 0:1], 0.0).then_inc(m_z0, 1)
                pool.wait_ge(m_bs, n + 1)
                pool.wait_ge(m_dtx, 1)
                if n >= 2:
                    pool.wait_ge(m_scan, n - 1)
                pool.tensor_tensor(drive[i][:], dtx[:], bmat[i][:].unsqueeze(1).to_broadcast((P, DT, T)),
                                   ALU.mult).then_inc(m_drv, 1)
            pool.wait_ge(m_out, TT)
            link(pool.memset(fhalf[:], -0.5))
            link(pool.memset(ones[:], 1.0))
            link(pool.iota(iota_i[:], pattern=[[1, T]], base=0, channel_multiplier=0))
            pool.sem_inc(f_iota, 1)
            pool.wait_ge(f_stat, 1)
            layernorm(P, fvar, frstd, fnm, fshift, fhalf, fmv, x1, f_nat, TT).then_inc(f_ln, 1)

        @block.vector
        def _(dve):
            done = [0]

            def link(ins):
                done[0] += 1
                ins.then_inc(s_dve, 1)
                dve.wait_ge(s_dve, done[0])

            def stats(src, st, mv, j_n):
                for j in range(j_n):
                    last = dve.bn_stats(st[:, j, :], src[:, j, :])
                link(last)
                for j in range(j_n):
                    last = dve.bn_aggr(mv[:, j, :], st[:, j, :])
                return last

            dve.wait_ge(ld_xlat, 16)
            stats(x_lat, cstat[0:L], cmv[0:L], B).then_inc(s_pstat, 1)
            dve.wait_ge(s_pln, 1)
            stats(x_lat, cstat[0:L], cmv[0:L], B).then_inc(s_pstat, 1)

            def ctx_stats(b, part):
                if part == 0:
                    dve.wait_ge(ld_ctx, 16 * (b + 1))
                for j in range(part * SJ // 2, (part + 1) * SJ // 2):
                    last = dve.bn_stats(cstat[:, j, :], ctx_nat[:, j, :])
                if part == 1:
                    last.then_inc(s_cst, 1)
                    dve.wait_ge(s_cst, b + 1)
                    apart(dve)
                    for j in range(SJ):
                        last = dve.bn_aggr(cmv[:, j, :], cstat[:, j, :])
                    last.then_inc(s_cmv, 1)

            def misc_lo(b, slot, m):
                dve.wait_ge(s_mhi, misc_count(b, m))
                dve.tensor_tensor(misc_dst(slot, m, False), misc_src(m),
                                  misc_dst(slot, m, True).bitcast(F32), ALU.subtract).then_inc(s_mlo, 1)

            for g in range(HP // 2):
                dve.wait_ge(s_pwk, g + 1)
                dve.tensor_copy(wk_t[:, 2 * g:2 * g + 2, :], TP[g % 2].rearrange("p (a c) -> p a c", c=C))\
                    .then_inc(s_pwke, 1)
            dve.wait_ge(s_platt, 1)
            dve.tensor_copy(latt[:], LG).then_inc(s_pevac, 1)
            dve.wait_ge(s_pevac, 2)
            dve.tensor_tensor(latt_lo[:], LG, latt_hi[:].bitcast(F32), ALU.subtract).then_inc(s_plo, 1)
            dve.wait_ge(s_pln, 2)
            ctx_stats(0, 0)
            ctx_stats(0, 1)
            for m in range(MISC):
                misc_lo(0, 0, m)

            def tail_lo(part, now):
                b, slot, hp = now
                u = hp % 2
                high, low, where, t0, t1 = {"A": (s_hA, s_lA, TP[0], 0, 4), "B": (s_hB, s_lB, TP[1], 4, 8),
                                            "C": (s_hC, s_lC, TP[0], 8, 9)}[part]
                dve.wait_ge(high, count(b, hp))
                rows = P if part != "C" else L
                dve.tensor_tensor(pt_lo[u][0:rows, t0:t1, :],
                                  where[0:rows, 0:(t1 - t0) * P].rearrange("p (t m) -> p t m", m=P),
                                  pt_hi[u][0:rows, t0:t1, :].bitcast(F32), ALU.subtract).then_inc(low, 1)

            def step(b, slot, hp, live, more, pair):
                p1, p3 = back(b, slot, hp, 1), back(b, slot, hp, 3)
                if live:
                    if hp == 0:
                        dve.wait_ge(s_latl, b + 1)
                        dve.tensor_reduce(latmax[slot][:], LAT.rearrange("p (h l) -> p h l", l=L), X, ALU.max)\
                            .then_inc(s_latm, 1)
                    dve.wait_ge(s_lg, count(b, hp))
                    dve.tensor_reduce(rowmax[slot][:, hp:hp + 1], LG.rearrange("p a n -> p (a n)"), X, ALU.max)\
                        .then_inc(s_mx, 1)
                    dve.wait_ge(s_mx, count(b, hp))
                    dve.wait_ge(s_latm, b + 1)
                    dve.tensor_scalar(nbias[slot][:, hp:hp + 1], rowmax[slot][:, hp:hp + 1],
                                      latmax[slot][:, hp:hp + 1], -SCALE, ALU.max, ALU.mult).then_inc(s_nb, 1)
                if p1:
                    tail_lo("A", p1)
                    tail_lo("B", p1)
                    b1_, sl1, hp1 = p1
                    dve.wait_ge(s_expl, count(b1_, hp1))
                    dve.tensor_tensor(den[sl1][:, hp1:hp1 + 1], den_ctx[sl1][:, hp1:hp1 + 1],
                                      den_lat[sl1][:, hp1:hp1 + 1], ALU.add).then_inc(s_den, 1)
                    dve.wait_ge(s_den, count(b1_, hp1))
                    dve.reciprocal(rden[sl1][:, hp1:hp1 + 1], den[sl1][:, hp1:hp1 + 1]).then_inc(s_rd, 1)
                if p3:
                    dve.wait_ge(s_yt, count(p3[0], p3[2]))
                    dve.tensor_copy(y_t[:], OC[:, 0:C].rearrange("p (k m) -> p k m", k=CK)).then_inc(s_yte, 1)
                if slot == 0 and hp == 3 and pair is not None:
                    dve.wait_ge(s_wo, pair + 1)
                    dve.tensor_tensor(x1[:, ds(pair, 1), :], x1[:, ds(pair, 1), :], MB[:, 0:C].unsqueeze(1),
                                      ALU.add).then_inc(s_woe, 1)
                if p1:
                    tail_lo("C", p1)
                if more:
                    if hp in (1, 2):
                        ctx_stats(b + 1, hp - 1)
                    misc_lo(b + 1, 1 - slot, hp)

            def body(b, slot, more, pair):
                for hp in range(HP):
                    step(b, slot, hp, True, more, pair)

            def drain(b, slot, pair):
                step(b, slot, 0, False, False, pair)
                for hp in (1, 2, 3):
                    p3 = back(b, slot, hp, 3)
                    if p3[0] is not b:
                        dve.wait_ge(s_yt, count(p3[0], p3[2]))
                        dve.tensor_copy(y_t[:], OC[:, 0:C].rearrange("p (k m) -> p k m", k=CK)).then_inc(s_yte, 1)
                    if hp == 3:
                        dve.wait_ge(s_wo, pair + 1)
                        dve.tensor_tensor(x1[:, ds(pair, 1), :], x1[:, ds(pair, 1), :], MB[:, 0:C].unsqueeze(1),
                                          ALU.add).then_inc(s_woe, 1)

            dve.wait_ge(ld_wvo, 48)
            all_steps(dve, body, drain)

            dve.wait_ge(s_woe, B // 2)
            stats(x1, tstat, tmv, TT).then_inc(m_stat, 1)
            dve.wait_ge(m_ln, 1)
            stats(mres, tstat, tmv, TT).then_inc(m_stat, 1)
            dve.wait_ge(m_xt, 1)
            link(dve.tensor_copy(xn_t[:], LG))
            dve.sem_inc(m_xte, 1)
            for d in range(DT):
                dve.wait_ge(m_xze, d + 1)
                o = conv[:, d, :].rearrange("p (b l) -> p b l", l=L)
                link(dve.tensor_scalar(o, xpad[:, d, :, 0:L], convw[:, d, 0:1], dvec[:, 0, d:d + 1],
                                       ALU.mult, ALU.add))
                for k in range(1, TAPS):
                    ins = dve.scalar_tensor_tensor(out=o, in0=xpad[:, d, :, k:k + L], scalar=convw[:, d, k:k + 1],
                                                   in1=o, op0=ALU.mult, op1=ALU.add)
                    if k < TAPS - 1:
                        link(ins)
                ins.then_inc(m_conv, 1)
            dve.wait_ge(m_dhi, 1)
            dve.tensor_tensor(dbc_lo[:], psum[0:NX, 2, :], dbc_hi[:].bitcast(F32), ALU.subtract).then_inc(m_dlo, 1)
            dve.wait_ge(m_dt0, 1)
            for d in range(DT):
                last = dve.tensor_scalar(state[0][:, d, :], psum[:, 3, :], dvec[:, 1, d:d + 1], dvec[:, 2, d:d + 1],
                                         ALU.mult, ALU.add)
            last.then_inc(m_dtu, 1)
            dve.wait_ge(m_dta, 1)
            link(dve.scalar_tensor_tensor(out=dts[:], in0=state[0][:], scalar=0.0, in1=read[1][:],
                                          op0=ALU.max, op1=ALU.add))
            dve.tensor_tensor(dtx[:], dts[:], xc[:], ALU.mult).then_inc(m_dtx, 1)
            for n in range(NS):
                i = n % 2
                dve.wait_ge(m_z0, n + 1)
                dve.wait_ge(m_drv, n + 1)
                flat = "p a b -> p (a b)"
                dve.tensor_tensor_scan(state[i][:].rearrange(flat), dec[i][:].rearrange(flat),
                                       drive[i][:].rearrange(flat), 0.0, ALU.mult, ALU.add).then_inc(m_scan, 1)
                dve.wait_ge(m_scan, n + 1)
                dve.wait_ge(m_c, n + 1)
                if n >= 2:
                    dve.wait_ge(m_acc, n - 1)
                dve.tensor_tensor(read[i][:], state[i][:], psum[:, 5 + i:6 + i, :].to_broadcast((P, DT, T)),
                                  ALU.mult).then_inc(m_rd, 1)
            dve.wait_ge(m_acc, NS)
            for d in range(DT):
                link(dve.scalar_tensor_tensor(out=conv[:, d, :], in0=xc[:, d, :], scalar=dvec[:, 3, d:d + 1],
                                              in1=psum[:, d, :], op0=ALU.mult, op1=ALU.add))
            dve.tensor_tensor(conv[:], conv[:], zs[:], ALU.mult).then_inc(m_y, 1)
            for t in range(TT):
                dve.wait_ge(m_y, 2 + t)
                link(dve.tensor_tensor(mres[:, t, :], mres[:, t, :], psum[:, 4 + t, 0:C], ALU.add))
                dve.tensor_tensor(x1[:, t, :], x1[:, t, :], mres[:, t, :], ALU.add).then_inc(m_out, 1)

            dve.wait_ge(m_out, TT)
            stats(x1, fstat, fmv, TT).then_inc(f_stat, 1)
            dve.wait_ge(ld_ffn, 64)
            dve.tensor_copy(idx_f[:], idx_i[:]).then_inc(f_cast, 1)
            dve.wait_ge(f_iota, 1)
            dve.tensor_copy(iota_f[:], iota_i[:]).then_inc(f_cast, 1)
            dve.wait_ge(f_cast, 2)
            for e in range(E):
                if e >= 2:
                    dve.wait_ge(f_cnt, e - 1)
                for j in range(SC):
                    last = dve.tensor_scalar(onehot[e % 2][:, j, :], iota_f[:], idx_f[:, j, e:e + 1], None,
                                             ALU.is_equal)
                last.then_inc(f_oh, 1)
            dve.wait_ge(f_cnt, E)
            dve.tensor_tensor(coef[:], psum[:, 4, 0:TT * E].rearrange("p (e t) -> p t e", t=TT), comb[:], ALU.mult)\
                .then_inc(f_coef, 1)
            dve.wait_ge(f_x, 1)
            dve.tensor_copy(f_t[:], LG).then_inc(f_xe, 1)
            dve.wait_ge(f_b1, 1)
            dve.tensor_copy(b1_t[:], psum[:, 5, 0:E * FT]).then_inc(f_xe, 1)
            dve.wait_ge(f_ct, 1)
            dve.tensor_copy(coef_t[:], psum[0:E, 6, :]).then_inc(f_cte, 1)
            for t in range(TT):
                dve.wait_ge(f_b2, t + 1)
                dve.tensor_tensor(acc[:, t, :], x1[:, t, :], psum[:, 4 + t, 0:C], ALU.add).then_inc(f_oe, 1)

            with dve.Fori(0, E // 2) as q:
                for i in range(2):
                    for t in range(TT):
                        dve.wait_ge(f_o, TT * (2 * q + i) + t + 1)
                        dve.wait_ge(f_oe, TT * (2 * q + i + 1) )
                        dve.scalar_tensor_tensor(out=acc[:, t, :], in0=psum[:, 4 + t, 0:C],
                                                 scalar=coef[:, t, ds(2 * q + i, 1)], in1=acc[:, t, :],
                                                 op0=ALU.mult, op1=ALU.add).then_inc(f_oe, 1)
            for t in range(TT):
                dve.wait_ge(f_oe, TT * E + t + 1)
                dve.sem_inc(f_done, 1)

        @block.scalar
        def _(act):
            act.wait_ge(s_pevac, 1)
            act.activation(latt_hi[:], LG, ACT.Copy).then_inc(s_pevac, 1)
            for t in range(HP):
                act.wait_ge(s_pq, t + 1)
                act.activation(q_t[:, t, :], psum[:, t % 2, :], ACT.Copy).then_inc(s_pqe, 1)

            def misc_hi(b, slot, m):
                act.wait_ge(s_misc, misc_count(b, m))
                act.activation(misc_dst(slot, m, True), misc_src(m), ACT.Copy).then_inc(s_mhi, 1)

            for m in range(MISC):
                misc_hi(0, 0, m)

            def tail_hi(part, now):
                b, slot, hp = now
                u = hp % 2
                turned, high, where, t0, t1 = {"A": (s_tA, s_hA, TP[0], 0, 4), "B": (s_tB, s_hB, TP[1], 4, 8),
                                               "C": (s_tC, s_hC, TP[0], 8, 9)}[part]
                act.wait_ge(turned, count(b, hp))
                rows = P if part != "C" else L
                act.activation(pt_hi[u][0:rows, t0:t1, :],
                               where[0:rows, 0:(t1 - t0) * P].rearrange("p (t m) -> p t m", m=P), ACT.Copy)\
                    .then_inc(high, 1)

            def mean_value(now):
                b, slot, hp = now
                act.wait_ge(s_pv, count(b, hp))
                act.wait_ge(s_rd, count(b, hp))
                before = back(b, slot, hp, 1)
                if before:
                    act.wait_ge(s_yt, count(before[0], before[2]))
                act.activation(y_n[:], PV, ACT.Copy, scale=rden[slot][:, hp:hp + 1]).then_inc(s_y, 1)

            def keep_out(now, pair):
                b, slot, hp = now
                act.wait_ge(s_o, count(b, hp))
                if slot == 0 and pair is not None:
                    act.wait_ge(s_wo, pair + 1)
                act.activation(o_t[:, hp, slot * L:(slot + 1) * L], OC[:, C:C + L], ACT.Copy).then_inc(s_oe, 1)

            def step(b, slot, hp, live, more, pair):
                p1, p2, p3 = (back(b, slot, hp, n) for n in (1, 2, 3))
                if p3:
                    mean_value(p3)
                if p1:
                    if p3:
                        act.wait_ge(s_pv, count(p3[0], p3[2]))
                    tail_hi("A", p1)
                    tail_hi("B", p1)
                if live:
                    act.wait_ge(s_nb, count(b, hp))
                    act.activation(prob[:], LG.rearrange("p a n -> p (a n)"), ACT.Exp,
                                   bias=nbias[slot][:, hp:hp + 1], scale=SCALE,
                                   accum_out=den_ctx[slot][:, hp:hp + 1]).then_inc(s_exp, 1)
                    if p2:
                        act.wait_ge(s_tC, count(p2[0], p2[2]))
                    act.activation(prob_lat[hp % 2][:], LAT[:, hp * L:(hp + 1) * L], ACT.Exp,
                                   bias=nbias[slot][:, hp:hp + 1], scale=SCALE,
                                   accum_out=den_lat[slot][:, hp:hp + 1]).then_inc(s_expl, 1)
                if p1:
                    tail_hi("C", p1)
                if p3:
                    keep_out(p3, pair if hp >= 3 else None)
                if more:
                    misc_hi(b + 1, 1 - slot, hp)

            def body(b, slot, more, pair):
                for hp in range(HP):
                    step(b, slot, hp, True, more, pair)

            def drain(b, slot, pair):
                step(b, slot, 0, False, False, None)
                for hp in (1, 2):
                    p3 = back(b, slot, hp, 3)
                    mean_value(p3)
                    keep_out(p3, None)

            all_steps(act, body, drain)

            act.wait_ge(ld_mam, 16 * 11)
            act.activation(a_neg[:], a_neg[:], ACT.Exp).then_inc(m_aneg, 1)
            act.wait_ge(m_aneg, 1)
            act.activation(a_neg[:], a_neg[:], ACT.Copy, scale=-1.0).then_inc(m_aneg, 1)
            act.wait_ge(m_ln, 1)
            for t in range(2 * DT):
                act.wait_ge(m_xz, t + 1)
                if t < DT:
                    act.activation(xpad[:, t, :, TAPS - 1:], psum[:, t % 2, :].rearrange("p (b l) -> p b l", l=L),
                                   ACT.Copy).then_inc(m_xze, 1)
                else:
                    act.activation(zs[:, t - DT, :], psum[:, t % 2, :], ACT.Silu).then_inc(m_xze, 1)
            for d in range(DT):
                act.wait_ge(m_conv, d + 1)
                act.activation(xc[:, d, :], conv[:, d, :], ACT.Silu).then_inc(m_xc, 1)
            act.wait_ge(m_dbc, 1)
            act.activation(dbc_hi[:], psum[0:NX, 2, :], ACT.Copy).then_inc(m_dhi, 1)
            act.wait_ge(m_dtu, 1)
            act.activation(read[0][:], state[0][:], ACT.Abs).then_inc(s_act, 1)
            act.wait_ge(s_act, 1)
            act.activation(read[0][:], read[0][:], ACT.Exp, scale=-1.0).then_inc(s_act, 1)
            act.wait_ge(s_act, 2)
            act.activation(read[1][:], read[0][:], ACT.Ln, bias=1.0).then_inc(m_dta, 1)
            act.wait_ge(m_dtx, 1)
            for n in range(NS):
                i = n % 2
                act.wait_ge(m_b, n + 1)
                if n >= 2:
                    act.wait_ge(m_drv, n - 1)
                act.activation(bmat[i][:], psum[:, 4, :], ACT.Copy).then_inc(m_bs, 1)
                if n >= 2:
                    act.wait_ge(m_scan, n - 1)
                for d in range(DT):
                    last = act.activation(dec[i][:, d, :], dts[:, d, :], ACT.Exp, scale=a_neg[:, d, n:n + 1])
                last.then_inc(m_dec, 1)

            act.wait_ge(f_xe, 2)
            with act.Fori(0, E // 2) as q:
                for i in range(2):
                    e = 2 * q + i
                    for f in range(FT):
                        act.wait_ge(f_h, FT * e + f + 1)
                        act.activation(hid[:, f, :], psum[:, f % 4, :], ACT.Gelu_apprx_tanh,
                                       bias=b1_t[:, ds(FT * e + f, 1)]).then_inc(f_he, 1)

        @block.tensor
        def _(pe):
            pe.wait_ge(s_id, 1)
            pe.wait_ge(ld_wk, 16)
            for g in range(HP // 2):
                if g >= 2:
                    pe.wait_ge(s_pwke, g - 1)
                for a in range(2):
                    for k in range(CK):
                        last = pe.transpose(TP[g % 2][:, (2 * a + k) * P:(2 * a + k + 1) * P],
                                            wk_nat[:, k, (2 * g + a) * P:(2 * g + a + 1) * P], ident[:])
                last.then_inc(s_pwk, 1)
            pe.wait_ge(s_pln, 2)
            for k in range(CK):
                for b in range(B):
                    last = pe.transpose(psum[:, k, b * L:(b + 1) * L], x_lat[:, b, k * P:(k + 1) * P],
                                        ident[0:L, 0:L])
            last.then_inc(s_platt, 1)
            pe.wait_ge(s_pevac, 2)
            pe.wait_ge(s_plo, 2)
            pe.wait_ge(ld_wq, 16)
            for t in range(HP):
                if t >= 2:
                    pe.wait_ge(s_pqe, t - 1)
                for k in range(CK):
                    last = pe.matmul(psum[:, t % 2, :], wq_sb[:, k, t * P:(t + 1) * P], latt[:, k, :],
                                     start=(k == 0), stop=(k == CK - 1))
                last.then_inc(s_pq, 1)

            def misc(b, slot, m, after=None):
                if after is not None:
                    pe.wait_ge(s_woe, after)
                if not (isinstance(b, int) and b == 0 and m == 0):
                    pe.wait_ge(s_mlo, misc_count(b, m) - 1)
                k, h = m % 4 // 2, m % 2
                if m < 4:
                    if m == 0:
                        pe.wait_ge(s_qcur, b + 1)
                    rows = slice(h * DH, (h + 1) * DH)
                    for hp in range(HP):
                        last = pe.matmul(MB[:, hp * L:(hp + 1) * L], wk_t[rows, hp, k * P:(k + 1) * P],
                                         q_cur[rows, hp, :], start=True, stop=True)
                else:
                    if m == 4:
                        pe.wait_ge(s_cn, b + 1)
                    for j in range(4):
                        last = pe.transpose(MB[:, j * P:(j + 1) * P], ctx_nat[:, 4 * h + j, k * P:(k + 1) * P],
                                            ident[:])
                last.then_inc(s_misc, 1)

            pe.wait_ge(s_pwke, HP // 2)
            for m in range(MISC):
                misc(0, 0, m)

            def lat_logits(b, slot):
                if not (isinstance(b, int) and b == 0):
                    pe.wait_ge(s_expl, HP * b)
                cols = ds(b * L, L)
                for hp in range(HP):
                    for k in range(CK):
                        for n, (q, x_) in enumerate(((qk_hi, latt_hi), (qk_hi, latt_lo), (qk_lo, latt_hi))):
                            last = pe.matmul(LAT[:, hp * L:(hp + 1) * L],
                                             q[slot][:, k, hp].rearrange("p a l -> p (a l)"), x_[:, k, cols],
                                             start=(k == 0 and n == 0), stop=(k == CK - 1 and n == 2))
                last.then_inc(s_latl, 1)

            def logits(b, slot, hp):
                for k in range(CK):
                    for q, x_ in ((qk_hi, kvt_hi), (qk_hi, kvt_lo), (qk_lo, kvt_hi)):
                        w = q[slot][:, k, hp].rearrange("p a l -> p (a l)")
                        for n in range(2):
                            last = pe.matmul(psum[:, n, :], w, x_[slot][:, k, n * 512:(n + 1) * 512],
                                             start=(k == 0 and q is qk_hi and x_ is kvt_hi),
                                             stop=(k == CK - 1 and q is qk_lo))
                last.then_inc(s_lg, 1)

            def turn(now, part):
                b, slot, hp = now
                if part == "C":
                    pe.wait_ge(s_lA, count(b, hp))
                    pe.wait_ge(s_expl, count(b, hp))
                    apart(pe)
                    pe.transpose(TP[0][0:L, 0:P], prob_lat[hp % 2][:], ident[:]).then_inc(s_tC, 1)
                    return
                before = back(b, slot, hp, 1)
                if before:
                    pe.wait_ge(s_lC, count(before[0], before[2]))
                for half, done in ((0, s_tA), (1, s_tB)):
                    for j in range(4):
                        last = pe.transpose(TP[half][:, j * P:(j + 1) * P],
                                            prob[:, (4 * half + j) * P:(4 * half + j + 1) * P], ident[:])
                    last.then_inc(done, 1)

            def times_rows(now):
                b, slot, hp = now
                pe.wait_ge(s_lC, count(b, hp))
                if hp == 0:
                    pe.wait_ge(s_klo, b + 1)
                before = back(b, slot, hp, 1)
                if before:
                    pe.wait_ge(s_y, count(before[0], before[2]))
                u = hp % 2
                for j in range(SJ):
                    for w, x_ in ((pt_hi, kvn_hi), (pt_hi, kvn_lo), (pt_lo, kvn_hi)):
                        pe.matmul(PV, w[u][:, j, :], x_[slot][:, j, :],
                                  start=(j == 0 and w is pt_hi and x_ is kvn_hi), stop=False)
                for n, (w, x_) in enumerate(((pt_hi, lat_hi), (pt_hi, lat_lo), (pt_lo, lat_hi))):
                    last = pe.matmul(PV, w[u][0:L, SJ, :], x_[:, ds(b, 1), :].rearrange("p a c -> p (a c)"),
                                     start=False, stop=(n == 2))
                last.then_inc(s_pv, 1)

            def turn_value(now):
                b, slot, hp = now
                pe.wait_ge(s_y, count(b, hp))
                before = back(b, slot, hp, 1)
                if before:
                    pe.wait_ge(s_oe, count(before[0], before[2]))
                for k in range(CK):
                    last = pe.transpose(OC[:, k * P:(k + 1) * P], y_n[:, k * P:(k + 1) * P], ident[:])
                last.then_inc(s_yt, 1)

            def head_out(now):
                b, slot, hp = now
                pe.wait_ge(s_yte, count(b, hp))
                for h in range(2):
                    for k in range(CK):
                        last = pe.matmul(OC[h * DH:(h + 1) * DH, C:C + L],
                                         wv[:, k, (2 * hp + h) * DH:(2 * hp + h + 1) * DH],
                                         y_t[:, k, h * L:(h + 1) * L], start=(k == 0), stop=(k == CK - 1))
                last.then_inc(s_o, 1)

            def out_proj(pair, seen):
                pe.wait_ge(s_oe, HP * 2 * (pair + 1))
                pe.wait_ge(s_mlo, seen)
                for hp in range(HP):
                    last = pe.matmul(MB[:, 0:C], o_t[:, hp, :], wo[:, hp, :], start=(hp == 0), stop=(hp == HP - 1))
                last.then_inc(s_wo, 1)

            def step(b, slot, hp, live, more, pair):
                p1, p2, p3 = (back(b, slot, hp, n) for n in (1, 2, 3))
                if live:
                    if hp == 0:
                        pe.wait_ge(s_mlo, MISC * (b + 1))
                        lat_logits(b, slot)
                    if p1:
                        pe.wait_ge(s_exp, count(p1[0], p1[2]))
                    logits(b, slot, hp)
                if p1:
                    if not live:
                        pe.wait_ge(s_exp, count(p1[0], p1[2]))
                    turn(p1, "AB")
                if p3:
                    turn_value(p3)
                if slot == 0 and hp == 3 and pair is not None:
                    out_proj(pair, misc_count(b + 1, hp) - 1)
                if p2:
                    times_rows(p2)
                if p1:
                    turn(p1, "C")
                if p3:
                    head_out(p3)
                if more:
                    misc(b + 1, 1 - slot, hp, pair + 1 if slot == 0 and hp == 3 and pair is not None else None)

            def body(b, slot, more, pair):
                for hp in range(HP):
                    step(b, slot, hp, True, more, pair)

            def drain(b, slot, pair):
                step(b, slot, 0, False, False, None)
                turn_value(back(b, slot, 1, 3))
                times_rows(back(b, slot, 1, 2))
                head_out(back(b, slot, 1, 3))
                turn_value(back(b, slot, 2, 3))
                head_out(back(b, slot, 2, 3))
                out_proj(pair, MISC * B)

            pe.wait_ge(ld_wvo, 48)
            all_steps(pe, body, drain)

            pe.wait_ge(m_ln, 2)
            for k in range(CK):
                for t in range(TT):
                    last = pe.transpose(psum[:, k, t * P:(t + 1) * P], xn[:, t, k * P:(k + 1) * P], ident[:])
            last.then_inc(m_xt, 1)
            pe.wait_ge(m_xte, 1)
            for t in range(2 * DT):
                if t >= 2:
                    pe.wait_ge(m_xze, t - 1)
                for k in range(CK):
                    last = pe.matmul(psum[:, t % 2, :], win[:, k, t * P:(t + 1) * P], xn_t[:, k, :],
                                     start=(k == 0), stop=(k == CK - 1))
                last.then_inc(m_xz, 1)
            for d in range(DT):
                pe.wait_ge(m_xc, d + 1)
                last = pe.matmul(psum[0:NX, 2, :], wxp[:, d, :], xc[:, d, :], start=(d == 0), stop=(d == DT - 1))
            last.then_inc(m_dbc, 1)
            pe.wait_ge(m_dlo, 1)
            pe.wait_ge(m_sel, 1)

            def spread(where, r):
                pe.matmul(where, sel[:, r, :], dbc_hi[:], start=True, stop=False)
                return pe.matmul(where, sel[:, r, :], dbc_lo[:], start=False, stop=True)

            spread(psum[:, 3, :], 0).then_inc(m_dt0, 1)
            pe.wait_ge(m_xze, 2 * DT)
            pe.wait_ge(m_dtx, 1)
            for n in range(NS):
                if n >= 1:
                    pe.wait_ge(m_bs, n)
                spread(psum[:, 4, :], 1 + n).then_inc(m_b, 1)
                if n >= 2:
                    pe.wait_ge(m_rd, n - 1)
                spread(psum[:, 5 + n % 2, :], 1 + NS + n).then_inc(m_c, 1)
                if n >= 1:
                    m = n - 1
                    pe.wait_ge(m_rd, m + 1)
                    for d in range(DT):
                        last = pe.matmul(psum[:, d, :], ident[:], read[m % 2][:, d, :], start=(m == 0), stop=False)
                    last.then_inc(m_acc, 1)
            pe.wait_ge(m_rd, NS)
            for d in range(DT):
                last = pe.matmul(psum[:, d, :], ident[:], read[(NS - 1) % 2][:, d, :], start=False, stop=True)
            last.then_inc(m_acc, 1)
            pe.wait_ge(m_y, 1)
            for t in range(TT):
                for d in range(DT):
                    last = pe.matmul(psum[:, 4 + t, 0:C], conv[:, d, t * P:(t + 1) * P], wout[:, d, :],
                                     start=(d == 0), stop=(d == DT - 1))
                last.then_inc(m_y, 1)

            pe.wait_ge(m_out, TT)
            pe.wait_ge(f_iota, 1)
            for e in range(E):
                pe.wait_ge(f_oh, e + 1)
                for t in range(TT):
                    for j in range(SC):
                        last = pe.matmul(psum[:, 4, e * TT + t:e * TT + t + 1],
                                         onehot[e % 2][:, j, t * P:(t + 1) * P], ones[:, 0:1],
                                         start=(j == 0), stop=(j == SC - 1))
                last.then_inc(f_cnt, 1)
            pe.wait_ge(f_ln, 1)
            for k in range(CK):
                for t in range(TT):
                    last = pe.transpose(psum[:, k, t * P:(t + 1) * P], f_nat[:, t, k * P:(k + 1) * P], ident[:])
            last.then_inc(f_x, 1)
            pe.wait_ge(ld_ffn, 64)
            pe.transpose(psum[:, 5, 0:E * FT], b1_rows[:], ident[0:E * FT, 0:E * FT]).then_inc(f_b1, 1)
            pe.wait_ge(f_coef, 1)
            for t in range(TT):
                last = pe.transpose(psum[0:E, 6, t * P:(t + 1) * P], coef[:, t, :], ident[:])
            last.then_inc(f_ct, 1)
            pe.wait_ge(f_cte, 1)
            pe.wait_ge(f_xe, 2)
            for t in range(TT):
                pe.matmul(psum[:, 4 + t, 0:C], coef_t[:, t * P:(t + 1) * P], b2_sb[:], start=True, stop=True)\
                    .then_inc(f_b2, 1)
            with pe.Fori(0, E // 2) as q:
                for i in range(2):
                    e = 2 * q + i
                    pe.wait_ge(ld_e[i], 32 * (q + 1))
                    for f in range(FT):
                        if f >= 4:
                            pe.wait_ge(f_he, FT * e + f - 3)
                        elif i == 1:
                            pe.wait_ge(f_he, FT * e)
                        else:
                            pe.wait_ge(f_he, FT * e)
                        for k in range(CK):
                            last = pe.matmul(psum[:, f % 4, :], w1[i][:, k, f * P:(f + 1) * P], f_t[:, k, :],
                                             start=(k == 0), stop=(k == CK - 1))
                        last.then_inc(f_h, 1)
                    pe.wait_ge(f_he, FT * e + FT)
                    for t in range(TT):
                        pe.wait_ge(f_oe, TT * e + t + 1)
                        for f in range(FT):
                            last = pe.matmul(psum[:, 4 + t, 0:C], hid[:, f, t * P:(t + 1) * P], w2[i][:, f, :],
                                             start=(f == 0), stop=(f == FT - 1))
                        last.then_inc(f_o, 1)


_INS = ['x', 'ctx_1024', 'L0_xattn_Wq', 'L0_xattn_Wkv', 'L0_xattn_Wo', 'L0_xattn_ln1_w', 'L0_xattn_ln1_b',
        'L0_xattn_ln2_w', 'L0_xattn_ln2_b', 'L0_attn_norm_w', 'L0_attn_norm_b', 'L0_attn_W_in', 'L0_attn_conv_w',
        'L0_attn_conv_b', 'L0_attn_x_proj_w', 'L0_attn_dt_w', 'L0_attn_dt_b', 'L0_attn_A_log', 'L0_attn_D',
        'L0_attn_W_out', 'L0_ffn_combine_weights', 'L0_ffn_top_idx', 'L0_ffn_W1', 'L0_ffn_b1', 'L0_ffn_W2',
        'L0_ffn_b2']
_OUTS = [((8, 64, 256), 'float32')]


def kernel(**inputs):
    import numpy as _np
    import concourse.bacc as _bacc
    from concourse import mybir as _mybir
    from concourse.bass_utils import run_bass_kernel_spmd as _run

    nc = _bacc.Bacc("TRN2", target_bir_lowering=False, num_devices=1)
    arrays, args = {}, []
    for name in _INS:
        a = _np.ascontiguousarray(inputs[name])
        arrays[f"in_{name}_dram"] = a
        args.append(nc.dram_tensor(f"in_{name}_dram", a.shape, _mybir.dt.from_np(a.dtype), kind="ExternalInput").ap())
    for i, (shape, dtype) in enumerate(_OUTS):
        dt = _mybir.dt.from_np(_np.dtype(dtype))
        args.append(nc.dram_tensor(f"out_{i}_dram", shape, dt, kind="ExternalOutput").ap())
    perceiver_kernel(nc, *args)
    r = _run(nc, [arrays], core_ids=[0])
    got = tuple(r.results[0][f"out_{i}_dram"] for i in range(len(_OUTS)))
    return got[0]
```

```python
from contextlib import ExitStack

import concourse.bass as bass
from concourse import mybir

F32 = mybir.dt.float32
F32R = mybir.dt.float32r
BF16 = mybir.dt.bfloat16
I32 = mybir.dt.int32
ALU = mybir.AluOpType
ACT = mybir.ActivationFunctionType
X = mybir.AxisListType.X
ds = bass.ds

P = 128
EPS = 1e-5


def perceiver_kernel(nc, x, ctx_in, Wq, Wkv, Wo, ln1_w, ln1_b, ln2_w, ln2_b,
                     norm_w, norm_b, W_in, conv_w, conv_b, x_proj_w, dt_w, dt_b, A_log, D_skip, W_out,
                     combine_w, top_idx, W1, b1, W2, b2, out):
    B, L, C = x.shape
    S = ctx_in.shape[1]
    INNER = Wq.shape[1]
    DH = 64
    HP = INNER // (2 * DH)
    CK = C // P
    SJ = S // P
    T = B * L
    TT = T // P
    BP = P // L
    DI = conv_w.shape[0]
    DT = DI // P
    TAPS = conv_w.shape[1]
    NS = A_log.shape[1]
    NX = x_proj_w.shape[1]
    E, _, FF = W1.shape
    FT = FF // P
    SC = top_idx.shape[0] // P
    RING = 4
    EG = E // RING
    ROUNDS = T // P
    SCALE = float(DH) ** -0.5
    GT = 4
    MISC = 8
    assert HP == MISC and C == 2 * P and P == 2 * L and SJ == 8 and TT * P == T == 512

    top = ExitStack()
    with top:
        def sem(name):
            return top.enter_context(nc.semaphore(name))

        def sb(stack, name, shape, dt=F32):
            return stack.enter_context(nc.sbuf_tensor(name, shape, dt))

        def row(v):
            return v.rearrange("(a d) -> a d", a=1)

        ident = sb(top, "ident", [P, P])
        x1 = sb(top, "x1", [P, TT, C])
        q_t = sb(top, "q_t", [P, HP, T])
        psum = top.enter_context(nc.psum_tensor("psum", [P, 8, 512], F32))

        att = ExitStack()
        ctx_nat = sb(att, "ctx_nat", [P, SJ, C])
        kvn_hi = [sb(att, "kvn_hi0", [P, SJ, C], F32R), None]
        kvn_lo = [sb(att, "kvn_lo0", [P, SJ, C], F32R), None]
        kvt_hi = [sb(att, f"kvt_hi{i}", [P, CK, S], F32R) for i in range(2)]
        kvt_lo = [sb(att, f"kvt_lo{i}", [P, CK, S], F32R) for i in range(2)]
        qk_hi = [sb(att, f"qk_hi{i}", [P, CK, HP, 2, L], F32R) for i in range(2)]
        qk_lo = [sb(att, f"qk_lo{i}", [P, CK, HP, 2, L], F32R) for i in range(2)]
        x_lat = sb(att, "x_lat", [P, TT, C])
        lat_cur = sb(att, "lat_cur", [P, C])
        cur_hi = sb(att, "cur_hi", [P, C], F32R)
        cur_lo = sb(att, "cur_lo", [P, C], F32R)
        latt_hi = sb(att, "latt_hi", [P, CK, T], F32R)
        latt_lo = sb(att, "latt_lo", [P, CK, T], F32R)
        q_cur = sb(att, "q_cur", [P, HP, 2, L])
        wk_t = sb(att, "wk_t", [P, HP, C])
        wv = sb(att, "wv", [P, CK, INNER])
        wo = sb(att, "wo", [P, HP, C])
        prob = [sb(att, f"prob{i}", [P, S + L]) for i in range(2)]
        y_n = sb(att, "y_n", [P, C])
        y_t = sb(att, "y_t", [P, CK, P])
        o_t = sb(att, "o_t", [P, HP, P])
        ln1wb = sb(att, "ln1wb", [P, 2, C])
        cstat = sb(att, "cstat", [P, SJ, 6])
        cmv = sb(att, "cmv", [P, SJ, 2])
        cvar = sb(att, "cvar", [P, SJ])
        crstd = sb(att, "crstd", [P, SJ])
        cnm = sb(att, "cnm", [P, SJ])
        cshift = sb(att, "cshift", [P, SJ])
        mhalf = sb(att, "mhalf", [P, SJ])
        lvar = sb(att, "lvar", [P, TT])
        lstat = sb(att, "lstat", [P, TT, 6])
        lmv = sb(att, "lmv", [P, TT, 2])
        lscale = sb(att, "lscale", [P, TT])
        lnm = sb(att, "lnm", [P, TT])
        lshift = sb(att, "lshift", [P, TT])
        rowmax = [sb(att, f"rowmax{i}", [P, HP]) for i in range(2)]
        nbias = [sb(att, f"nbias{i}", [P, HP]) for i in range(2)]
        den = [sb(att, f"den{i}", [P, HP]) for i in range(2)]
        rden = [sb(att, f"rden{i}", [P, HP]) for i in range(2)]
        pro = ExitStack()
        wq_sb = sb(pro, "wq_sb", [P, CK, INNER])
        wk_nat = sb(pro, "wk_nat", [P, CK, INNER])
        latt = sb(pro, "latt", [P, CK, T])
        ln2wb = sb(pro, "ln2wb", [P, 2, C])
        pro.close()
        kvn_hi[1] = sb(att, "kvn_hi1", [P, SJ, C], F32R)
        kvn_lo[1] = sb(att, "kvn_lo1", [P, SJ, C], F32R)
        pt_hi = [sb(att, f"pt_hi{i}", [P, SJ + 1, P], F32R) for i in range(2)]
        pt_lo = [sb(att, f"pt_lo{i}", [P, SJ + 1, P], F32R) for i in range(2)]
        att.close()

        mam = ExitStack()
        room = q_t[:].rearrange("p h t -> p (h t)")
        used = [0]

        def part(*shape):
            size = 1
            for n in shape:
                size *= n
            view = room[:, used[0]:used[0] + size]
            used[0] += size
            return view.rearrange("p (a b) -> p a b", b=shape[-1])

        win = part(CK, 2 * DI)
        wout = part(DT, C)
        wxp = part(DT, NX)
        convw = part(DT, TAPS)
        dvec = part(4, DT)
        a_neg = part(DT, NS)
        nwb = part(2, C)
        idx_rows = part(3, SC * E)
        pick = sb(mam, "pick", [P, TT, E, P], F32R)
        w1, w2 = [sb(mam, "w1_0", [P, CK, FF])], [sb(mam, "w2_0", [P, FT, C])]
        onehot = sb(mam, "onehot", [P, SC * E, P], BF16)
        onetile = sb(mam, "onetile", [P, SC * E, TT], BF16)
        place_f = sb(mam, "place_f", [P, SC * E])
        tile_f = sb(mam, "tile_f", [P, SC * E])
        iota_i = sb(mam, "iota_i", [P, P], I32)
        iota_f = sb(mam, "iota_f", [P, P])
        before = sb(mam, "before", [P, P], BF16)
        ones = sb(mam, "ones", [P, P], BF16)
        valid = sb(mam, "valid", [P, TT, E], BF16)
        slot_of = sb(mam, "slot_of", [P, TT, E])
        most = sb(mam, "most", [P, 1])
        most_i = sb(mam, "most_i", [P, 1], I32)
        comb = sb(mam, "comb", [P, TT, E])
        coef = sb(mam, "coef", [P, TT, E])
        coef_hl = sb(mam, "coef_hl", [P, TT, E, 2], F32R)
        b1_rows = sb(mam, "b1_rows", [E * FT, P])
        b1_t = sb(mam, "b1_t", [P, E * FT])
        mres = sb(mam, "mres", [P, TT, C])
        conv = sb(mam, "conv", [P, DT, T])
        ident_r = sb(mam, "ident_r", [NX, NX], F32R)
        dbc_hi = sb(mam, "dbc_hi", [NX, T], F32R)
        dbc_lo = sb(mam, "dbc_lo", [NX, T], F32R)
        bmat = [sb(mam, f"bmat{i}", [P, T]) for i in range(2)]
        tstat = sb(mam, "tstat", [P, TT, 6])
        tmv = sb(mam, "tmv", [P, TT, 2])
        tvar = sb(mam, "tvar", [P, TT])
        trstd = sb(mam, "trstd", [P, TT])
        tvar2 = sb(mam, "tvar2", [P, TT])
        trstd2 = sb(mam, "trstd2", [P, TT])
        thalf = sb(mam, "thalf", [P, TT])
        front = ExitStack()
        xn = sb(front, "xn", [P, TT, C])
        xn_t = sb(front, "xn_t", [P, CK, T])
        xpad = sb(front, "xpad", [P, DT, B, L + TAPS - 1])
        front.close()
        w1.append(sb(mam, "w1_1", [P, CK, FF]))
        w2.append(sb(mam, "w2_1", [P, FT, C]))
        sb(mam, "rest_of_front", [P, DT * B * (L + TAPS - 1) + TT * C + CK * T - CK * FF - FT * C])
        steps = ExitStack()
        dec = [sb(steps, f"dec{i}", [P, DT, T]) for i in range(2)]
        drive = [sb(steps, f"drive{i}", [P, DT, T]) for i in range(2)]
        steps.close()
        for i in (2, 3):
            w1.append(sb(mam, f"w1_{i}", [P, CK, FF]))
            w2.append(sb(mam, f"w2_{i}", [P, FT, C]))
        res = ExitStack()
        read = [sb(res, f"read{i}", [P, DT, T]) for i in range(2)]
        state = [sb(res, f"state{i}", [P, DT, T]) for i in range(2)]
        res.close()
        pick_t = sb(mam, "pick_t", [P, E, T], F32R)
        xg_t = sb(mam, "xg_t", [P, CK, E, P])
        hid = sb(mam, "hid", [P, FT, P])
        acc_t = sb(mam, "acc_t", [P, CK, T])
        oper = ExitStack()
        dts = sb(oper, "dts", [P, DT, T])
        dtx = sb(oper, "dtx", [P, DT, T])
        xc = sb(oper, "xc", [P, DT, T])
        zs = sb(oper, "zs", [P, DT, T])
        oper.close()
        coef_t = sb(mam, "coef_t", [E, T])
        b2_sb = sb(mam, "b2_sb", [E, C])
        coef_slot = sb(mam, "coef_slot", [P, E])
        o_s = sb(mam, "o_s", [P, C])
        o_hi = sb(mam, "o_hi", [P, C], F32R)
        o_lo = sb(mam, "o_lo", [P, C], F32R)
        f_nat = sb(mam, "f_nat", [P, TT, C])
        f_hi = sb(mam, "f_hi", [P, TT, C], F32R)
        f_lo = sb(mam, "f_lo", [P, TT, C], F32R)
        res_nat = sb(mam, "res_nat", [P, TT, C])
        fstat = sb(mam, "fstat", [P, TT, 6])
        fmv = sb(mam, "fmv", [P, TT, 2])
        fvar = sb(mam, "fvar", [P, TT])
        frstd = sb(mam, "frstd", [P, TT])
        fhalf = sb(mam, "fhalf", [P, TT])
        mam.close()

        TWO, LG = psum[:, 0:2, :], psum[:, 0:3, :].rearrange("p a n -> p (a n)")[:, 0:S + L]
        TP, PV, OC, MB = [psum[:, 3, :], psum[:, 4, :]], psum[:, 5, 0:C], psum[:, 6, :], psum[:, 7, :]

        ld_xlat, ld_vec, ld_wq, ld_wk, ld_wvo, ld_ctx = (sem(n) for n in (
            "ld_xlat", "ld_vec", "ld_wq", "ld_wk", "ld_wvo", "ld_ctx"))
        ld_vec2 = sem("ld_vec2")
        ld_mam, ld_idx, ld_comb, ld_b2, ld_out = (sem(n) for n in ("ld_mam", "ld_idx", "ld_comb", "ld_b2", "ld_out"))
        ld_e = [sem(f"ld_e{i}") for i in range(RING)]
        s_dve, s_pool, s_act, s_pe = sem("s_dve"), sem("s_pool"), sem("s_act"), sem("s_pe")
        s_apart, s_psc, s_lcur, m_rs, f_rs = (sem(n) for n in ("s_apart", "s_psc", "s_lcur", "m_rs", "f_rs"))
        s_id, s_pstat, s_pln, s_platt, s_pevac, s_pq, s_pqe, s_pwk, s_pwke, s_plo = (sem(n) for n in (
            "s_id", "s_pstat", "s_pln", "s_platt", "s_pevac", "s_pq", "s_pqe", "s_pwk", "s_pwke", "s_plo"))
        s_cst, s_cmv, s_cvar, s_crs, s_cnm, s_csh, s_cz, s_cw, s_cn, s_khi, s_klo, s_qcur = (sem(n) for n in (
            "s_cst", "s_cmv", "s_cvar", "s_crs", "s_cnm", "s_csh", "s_cz", "s_cw", "s_cn", "s_khi", "s_klo",
            "s_qcur"))
        s_misc, s_mhi, s_mlo = sem("s_misc"), sem("s_mhi"), sem("s_mlo")
        (s_lg, s_mx, s_nb, s_exp, s_tA, s_tB, s_tC, s_hA, s_hB, s_hC, s_lA, s_lB, s_lC,
         s_rd, s_pv, s_y, s_yt, s_yte, s_o, s_oe) = (sem("s_" + n) for n in (
             "lg mx nb exp tA tB tC hA hB hC lA lB lC rd pv y yt yte o oe").split())
        s_wo, s_woe = sem("s_wo"), sem("s_woe")
        (m_stat, m_ln, m_xt, m_xte, m_xz, m_xze, m_zz, m_conv, m_xc, m_dbc, m_dhi, m_dlo, m_dt0, m_dtu, m_dta,
         m_dtx, m_sel, m_aneg, m_b, m_bs, m_c, m_dec, m_z0, m_drv, m_scan, m_rd, m_acc, m_y, m_out) = (
            sem("m_" + n) for n in (
                "stat ln xt xte xz xze zz conv xc dbc dhi dlo dt0 dtu dta dtx sel aneg b bs c dec z0 drv scan rd "
                "acc y out").split())
        r_idx, r_tab, r_oh, r_cnt, r_val, r_pre, r_pos, r_b1, r_b1e = (sem("r_" + n) for n in (
            "idx tab oh cnt val pre pos b1 b1e").split())
        (f_stat, f_ln, f_hi_done, f_lo_done, f_hl, f_ct, f_cte, f_pick, f_turn, f_turned, f_cs, f_cse, f_gat, f_gate,
         f_h, f_he, f_o, f_os, f_oh, f_ol, f_sc, f_sce, f_b2, f_shift, f_all, f_fin, f_done) = (sem("f_" + n) for n in (
             "stat ln hi lo hl ct cte pick turn turned cs cse gat gate h he o os oh ol sc sce b2 shift all fin done").split())

        def count(b, hp):
            return HP * b + hp + 1

        def back(b, slot, hp, n):
            if hp >= n:
                return b, slot, hp - n
            if isinstance(b, int) and b == 0:
                return None
            return b - 1, 1 - slot, hp - n + HP

        def apart(eng):
            eng.sem_inc(s_apart, 1)

        def misc_count(b, m):
            return MISC * b + m + 1

        def misc_dst(slot, m, hi):
            if m < 4:
                k, a = m // 2, m % 2
                return (qk_hi if hi else qk_lo)[slot][:, k, a * HP // 2:(a + 1) * HP // 2]\
                    .rearrange("p h a l -> p (h a l)")
            h, k = m % 4 // 2, m % 2
            return (kvt_hi if hi else kvt_lo)[slot][:, k, h * 512:(h + 1) * 512]

        def half(slot):
            return slice(slot * L, (slot + 1) * L)

        def all_steps(loops, body, drain):
            body(0, 0, True, None)
            with loops.Fori(0, B // 2 - 1) as p:
                body(2 * p + 1, 1, True, None)
                body(2 * p + 2, 0, True, p)
            body(B - 1, 1, False, None)
            drain(B, 0, B // 2 - 1)

        def further_rounds(eng, do_round):
            eng.wait_ge(r_pos, 2)
            longest = eng.value_load(most_i[0:1, 0:1], min_val=0, max_val=T)
            with eng.If(longest > P):
                with eng.Fori(1, ROUNDS) as r:
                    do_round(r)

        block = top.enter_context(nc.Block())

        @block.sync
        def _(sp):
            sp.dma_start(x_lat[:], x.rearrange("(t b) l c -> (b l) t c", b=BP)).then_inc(ld_xlat, 16)
            sp.dma_start(ctx_nat[:], ctx_in[0].rearrange("(p j) c -> p j c", j=SJ)).then_inc(ld_ctx, 16)
            for i, v in enumerate((ln2_w, ln2_b)):
                sp.dma_start(ln2wb[:, i, :], row(v).to_broadcast((P, C))).then_inc(ld_vec2, 16)
            wkv = Wkv.rearrange("(k p) n -> p k n", p=P)
            sp.dma_start(wk_nat[:], wkv[:, :, 0:INNER]).then_inc(ld_wk, 16)
            for i, v in enumerate((ln1_w, ln1_b)):
                sp.dma_start(ln1wb[:, i, :], row(v).to_broadcast((P, C))).then_inc(ld_vec, 16)
            sp.dma_start(wq_sb[:], Wq.rearrange("(k p) n -> p k n", p=P)).then_inc(ld_wq, 16)
            sp.dma_start(wv[:], wkv[:, :, INNER:2 * INNER]).then_inc(ld_wvo, 16)
            sp.dma_start(wo[:], Wo.rearrange("(h p) n -> p h n", p=P)).then_inc(ld_wvo, 16)
            sp.dma_start(x1[:], x.rearrange("(t b) l c -> (b l) t c", b=BP)).then_inc(ld_wvo, 16)
            with sp.Fori(1, B) as b:
                sp.wait_ge(s_misc, MISC * b)
                sp.wait_ge(s_klo, b)
                sp.dma_start(ctx_nat[:], ctx_in[ds(b, 1)].rearrange("a (p j) c -> p (a j) c", j=SJ))\
                    .then_inc(ld_ctx, 16)
            sp.wait_ge(s_qcur, 2 * B)
            sp.dma_start(win[:], W_in.rearrange("(k p) n -> p k n", p=P)).then_inc(ld_mam, 16)
            sp.dma_start(wout[:], W_out.rearrange("(k p) n -> p k n", p=P)).then_inc(ld_mam, 16)
            sp.dma_start(wxp[:], x_proj_w.rearrange("(k p) n -> p k n", p=P)).then_inc(ld_mam, 16)
            sp.dma_start(convw[:], conv_w.rearrange("(k p) n -> p k n", p=P)).then_inc(ld_mam, 16)
            with nc.allow_non_contiguous_dma(reason="four short vectors"):
                for i, v in enumerate((conv_b, dt_w, dt_b, D_skip)):
                    sp.dma_start(dvec[:, i, :], v.rearrange("(k p) -> p k", p=P)).then_inc(ld_mam, 16)
            sp.dma_start(a_neg[:], A_log.rearrange("(k p) n -> p k n", p=P)).then_inc(ld_mam, 16)
            for i, v in enumerate((norm_w, norm_b)):
                sp.dma_start(nwb[:, i, :], row(v).to_broadcast((P, C))).then_inc(ld_mam, 16)
            with nc.allow_non_contiguous_dma(reason="a short table"):
                sp.dma_start(idx_rows[:, 0, :].bitcast(I32).rearrange("p (j e) -> p j e", e=E),
                             top_idx.rearrange("(j p) e -> p j e", p=P)).then_inc(ld_idx, 16)

            def load_expert(e, i):
                sp.dma_start(w1[i][:], W1[ds(e, 1)].rearrange("a (k p) n -> p (a k) n", p=P)).then_inc(ld_e[i], 16)
                sp.dma_start(w2[i][:], W2[ds(e, 1)].rearrange("a (k p) n -> p (a k) n", p=P)).then_inc(ld_e[i], 16)

            sp.wait_ge(s_woe, B // 2)
            sp.dma_start(comb[:], combine_w[0:T, :].rearrange("(t p) e -> p t e", p=P)).then_inc(ld_comb, 16)
            sp.dma_start(b1_rows[:], b1.rearrange("e (f p) -> (e f) p", p=P)).then_inc(ld_comb, 16)
            load_expert(0, 0)
            sp.wait_ge(m_conv, DT)
            sp.wait_ge(m_xz, 2 * DT)
            load_expert(1, 1)
            sp.wait_ge(m_scan, NS)
            load_expert(2, 2)
            load_expert(3, 3)
            sp.wait_ge(m_y, 1)
            sp.dma_start(b2_sb[:], b2).then_inc(ld_b2, 16)
            for e in range(RING, E):
                sp.wait_ge(f_o, e - RING + 1)
                load_expert(e, e % RING)

            def more_loads(r):
                for e in range(E):
                    sp.wait_ge(f_o, E * r + e - RING + 1)
                    load_expert(e, e % RING)

            further_rounds(sp, more_loads)
            for t in range(TT):
                sp.wait_ge(f_done, t + 1)
                sp.dma_start(out.rearrange("(t b) l c -> t (b l) c", b=BP)[t], res_nat[:, t, :]).then_inc(ld_out, 16)
            sp.wait_ge(ld_out, 16 * TT)

        @block.gpsimd
        def _(pool):
            done = [0]

            def link(ins):
                done[0] += 1
                ins.then_inc(s_pool, 1)
                pool.wait_ge(s_pool, done[0])

            link(pool.memset(ident[:], 0.0))
            link(pool.memset(q_cur[:], 0.0))
            pool.affine_select(out=ident[:], in_=ident[:], compare_op=ALU.not_equal, fill=1.0, base=0,
                               pattern=[[-1, P]], channel_multiplier=1).then_inc(s_id, 1)
            link(pool.memset(mhalf[:], -0.5))
            pool.wait_ge(s_pstat, 1)
            link(pool.tensor_scalar(lvar[:], lmv[:, :, 1], 1.0 + EPS, EPS * EPS, ALU.mult, ALU.add))
            link(pool.tensor_tensor(lscale[:], lvar[:], mhalf[:, 0:TT], ALU.pow))
            link(pool.tensor_tensor(lnm[:], lmv[:, :, 0], lscale[:], ALU.mult))
            pool.tensor_scalar(lshift[:], lnm[:], -1.0, 0.0, ALU.mult, ALU.add).then_inc(s_psc, 1)

            def queries(b):
                pool.wait_ge(s_misc, MISC * (b - 1) + 4)
                apart(pool)
                pool.wait_ge(s_lcur, 3 * b)
                apart(pool)
                for h in range(2):
                    rows = slice(h * DH, (h + 1) * DH)
                    pool.tensor_copy(q_cur[rows, :, h, :], q_t[rows, :, ds(b * L, L)]).then_inc(s_qcur, 1)
                    pool.wait_ge(s_qcur, 2 * b + h + 1)

            def latents(b, slot):
                rows = half(slot)
                flat = x_lat[:].rearrange("p t c -> p (t c)")
                pool.wait_ge(s_klo, b + 1)
                apart(pool)
                pool.tensor_copy(lat_cur[rows], flat[rows, ds((b - slot) * (C // BP), C)]).then_inc(s_lcur, 1)
                pool.wait_ge(s_lcur, 3 * b + 1)
                apart(pool)
                pool.tensor_scalar(cur_hi[rows], lat_cur[rows], 1.0, 0.0, ALU.mult, ALU.add).then_inc(s_lcur, 1)
                pool.wait_ge(s_lcur, 3 * b + 2)
                pool.tensor_tensor(cur_lo[rows], lat_cur[rows], cur_hi[rows].bitcast(F32), ALU.subtract)\
                    .then_inc(s_lcur, 1)

            def context(b, slot):
                pool.wait_ge(s_cmv, b + 1)
                apart(pool)
                pool.tensor_scalar(cvar[:], cmv[:, :, 1], 1.0, EPS, ALU.mult, ALU.add).then_inc(s_cvar, 1)
                pool.wait_ge(s_cvar, b + 1)
                pool.tensor_tensor(crstd[:], cvar[:], mhalf[:], ALU.pow).then_inc(s_crs, 1)
                pool.wait_ge(s_crs, b + 1)
                pool.tensor_tensor(cnm[:], cmv[:, :, 0], crstd[:], ALU.mult).then_inc(s_cnm, 1)
                pool.wait_ge(s_cnm, b + 1)
                apart(pool)
                pool.tensor_scalar(cshift[:], cnm[:], -1.0, 0.0, ALU.mult, ALU.add).then_inc(s_csh, 1)
                pool.wait_ge(s_cz, b + 1)
                if isinstance(b, int) and b == 0:
                    pool.wait_ge(ld_vec, 32)
                shape = (P, SJ // 2, C)
                for h in range(2):
                    rows = ctx_nat[:, h * SJ // 2:(h + 1) * SJ // 2, :]
                    pool.tensor_tensor(rows, rows, ln1wb[:, 0:1, :].to_broadcast(shape), ALU.mult).then_inc(s_cw, 1)
                    pool.wait_ge(s_cw, 2 * b + h + 1)
                    pool.tensor_tensor(rows, rows, ln1wb[:, 1:2, :].to_broadcast(shape), ALU.add).then_inc(s_cn, 1)
                pool.wait_ge(s_cn, 2 * b + 2)
                if not (isinstance(b, int) and b < 2):
                    pool.wait_ge(s_pv, HP * (b - 1))
                apart(pool)
                pool.tensor_scalar(kvn_hi[slot][:], ctx_nat[:], 1.0, 0.0, ALU.mult, ALU.add).then_inc(s_khi, 1)
                pool.wait_ge(s_khi, b + 1)
                pool.tensor_tensor(kvn_lo[slot][:], ctx_nat[:], kvn_hi[slot][:].bitcast(F32), ALU.subtract)\
                    .then_inc(s_klo, 1)

            context(0, 0)
            pool.wait_ge(s_pln, 1)
            latents(0, 0)
            pool.wait_ge(s_misc, MISC)

            def body(b, slot, more, pair):
                if more:
                    queries(b + 1)
                    context(b + 1, 1 - slot)
                    latents(b + 1, 1 - slot)
                    pool.wait_ge(s_lcur, 3 * (b + 2))

            all_steps(pool, body, lambda b, slot, pair: None)

            pool.wait_ge(s_woe, B // 2)
            link(pool.memset(thalf[:], -0.5))
            link(pool.memset(xpad[:], 0.0))
            pool.tensor_scalar(ident_r[:], ident[0:NX, 0:NX], 1.0, 0.0, ALU.mult, ALU.add).then_inc(m_sel, 1)
            pool.wait_ge(m_stat, 1)
            pool.tensor_scalar(tvar[:], tmv[:, :, 1], 1.0, EPS, ALU.mult, ALU.add)
            link(pool.tensor_scalar(tvar2[:], tmv[:, :, 1], 1.0 + EPS, EPS * EPS, ALU.mult, ALU.add))
            pool.tensor_tensor(trstd[:], tvar[:], thalf[:], ALU.pow)
            pool.tensor_tensor(trstd2[:], tvar2[:], thalf[:], ALU.pow).then_inc(m_rs, 1)
            link(pool.memset(ones[:], 1.0))
            link(pool.affine_select(out=before[:], in_=ones[:], compare_op=ALU.is_ge, fill=0.0, base=0,
                                    pattern=[[1, P]], channel_multiplier=-1))
            link(pool.iota(iota_i[:], pattern=[[1, P]], base=0, channel_multiplier=0))
            link(pool.tensor_copy(iota_f[:], iota_i[:]))
            pool.sem_inc(r_tab, 1)
            pool.wait_ge(r_pos, 2)
            link(pool.tensor_scalar(coef_hl[:, :, :, 0], coef[:], 1.0, 0.0, ALU.mult, ALU.add))
            pool.tensor_tensor(coef_hl[:, :, :, 1], coef[:], coef_hl[:, :, :, 0].bitcast(F32), ALU.subtract)\
                .then_inc(f_hl, 1)
            for n in range(NS):
                i = n % 2
                pool.wait_ge(m_bs, n + 1)
                pool.wait_ge(m_dtx, 1)
                if n >= 2:
                    pool.wait_ge(m_scan, n - 1)
                pool.tensor_tensor(drive[i][:], dtx[:], bmat[i][:].unsqueeze(1).to_broadcast((P, DT, T)),
                                   ALU.mult).then_inc(m_drv, 1)
                pool.wait_ge(m_dec, n + 1)
                pool.memset(dec[i][:].rearrange("p a (b l) -> p (a b) l", l=L)[:, :, 0:1], 0.0).then_inc(m_z0, 1)
            pool.wait_ge(m_out, TT)
            link(pool.memset(fhalf[:], -0.5))
            pool.wait_ge(f_stat, 1)
            link(pool.tensor_scalar(fvar[:], fmv[:, :, 1], 1.0, EPS, ALU.mult, ALU.add))
            pool.tensor_tensor(frstd[:], fvar[:], fhalf[:], ALU.pow).then_inc(f_rs, 1)

        @block.vector
        def _(dve):
            done = [0]

            def link(ins):
                done[0] += 1
                ins.then_inc(s_dve, 1)
                dve.wait_ge(s_dve, done[0])

            def stats(src, st, mv, j_n):
                for j in range(j_n):
                    last = dve.bn_stats(st[:, j, :], src[:, j, :])
                link(last)
                for j in range(j_n):
                    last = dve.bn_aggr(mv[:, j, :], st[:, j, :])
                return last

            def ctx_stats(b, part):
                if part == 0:
                    dve.wait_ge(ld_ctx, 16 * (b + 1))
                for j in range(part * SJ // 2, (part + 1) * SJ // 2):
                    last = dve.bn_stats(cstat[:, j, :], ctx_nat[:, j, :])
                if part == 1:
                    last.then_inc(s_cst, 1)
                    dve.wait_ge(s_cst, b + 1)
                    apart(dve)
                    for j in range(SJ):
                        last = dve.bn_aggr(cmv[:, j, :], cstat[:, j, :])
                    last.then_inc(s_cmv, 1)

            def misc_lo(b, slot, m):
                dve.wait_ge(s_mhi, misc_count(b, m))
                dve.tensor_tensor(misc_dst(slot, m, False), MB,
                                  misc_dst(slot, m, True).bitcast(F32), ALU.subtract).then_inc(s_mlo, 1)

            def ctx_scale(b):
                dve.wait_ge(s_csh, b + 1)
                for j in range(SJ):
                    last = dve.tensor_scalar(ctx_nat[:, j, :], ctx_nat[:, j, :], crstd[:, j:j + 1],
                                             cshift[:, j:j + 1], ALU.mult, ALU.add)
                last.then_inc(s_cz, 1)

            dve.wait_ge(ld_xlat, 16)
            stats(x_lat, lstat, lmv, TT).then_inc(s_pstat, 1)
            ctx_stats(0, 0)
            ctx_stats(0, 1)
            dve.wait_ge(s_psc, 1)
            for t in range(TT):
                last = dve.tensor_scalar(x_lat[:, t, :], x_lat[:, t, :], lscale[:, t:t + 1], lshift[:, t:t + 1],
                                         ALU.mult, ALU.add)
            link(last)
            dve.wait_ge(ld_vec2, 32)
            link(dve.tensor_tensor(x_lat[:], x_lat[:], ln2wb[:, 0:1, :].to_broadcast((P, TT, C)), ALU.mult))
            dve.tensor_tensor(x_lat[:], x_lat[:], ln2wb[:, 1:2, :].to_broadcast((P, TT, C)), ALU.add)\
                .then_inc(s_pln, 1)
            ctx_scale(0)
            dve.wait_ge(s_platt, 1)
            dve.tensor_copy(latt[:], TWO).then_inc(s_pevac, 1)
            dve.wait_ge(s_pevac, 2)
            dve.tensor_tensor(latt_lo[:], TWO, latt_hi[:].bitcast(F32), ALU.subtract).then_inc(s_plo, 1)
            for m in range(MISC):
                misc_lo(0, 0, m)

            def tail_lo(part, now):
                b, slot, hp = now
                u = hp % 2
                high, low, where, t0, t1 = {"A": (s_hA, s_lA, TP[0], 0, 4), "B": (s_hB, s_lB, TP[1], 4, 8),
                                            "C": (s_hC, s_lC, TP[0], 8, 9)}[part]
                dve.wait_ge(high, count(b, hp))
                rows = slice(0, P) if part != "C" else half(slot)
                dve.tensor_tensor(pt_lo[u][rows, t0:t1, :],
                                  where[rows, 0:(t1 - t0) * P].rearrange("p (t m) -> p t m", m=P),
                                  pt_hi[u][rows, t0:t1, :].bitcast(F32), ALU.subtract).then_inc(low, 1)

            def step(b, slot, hp, live, more, pair):
                p1, p3 = back(b, slot, hp, 1), back(b, slot, hp, 3)
                if live:
                    dve.wait_ge(s_lg, count(b, hp))
                    dve.tensor_reduce(rowmax[slot][:, hp:hp + 1], LG, X, ALU.max).then_inc(s_mx, 1)
                    dve.wait_ge(s_mx, count(b, hp))
                    apart(dve)
                    dve.tensor_scalar(nbias[slot][:, hp:hp + 1], rowmax[slot][:, hp:hp + 1], -SCALE, None,
                                      ALU.mult).then_inc(s_nb, 1)
                if p1:
                    tail_lo("A", p1)
                    tail_lo("B", p1)
                    b1_, sl1, hp1 = p1
                    dve.wait_ge(s_exp, count(b1_, hp1))
                    dve.reciprocal(rden[sl1][:, hp1:hp1 + 1], den[sl1][:, hp1:hp1 + 1]).then_inc(s_rd, 1)
                if p3:
                    dve.wait_ge(s_yt, count(p3[0], p3[2]))
                    dve.tensor_copy(y_t[:], OC[:, 0:C].rearrange("p (k m) -> p k m", k=CK)).then_inc(s_yte, 1)
                if slot == 0 and hp == 3 and pair is not None:
                    dve.wait_ge(s_wo, pair + 1)
                    dve.tensor_tensor(x1[:, ds(pair, 1), :], x1[:, ds(pair, 1), :], MB[:, 0:C].unsqueeze(1),
                                      ALU.add).then_inc(s_woe, 1)
                if p1:
                    tail_lo("C", p1)
                if more:
                    if hp < 2:
                        ctx_stats(b + 1, hp)
                    misc_lo(b + 1, 1 - slot, hp)
                    if hp == 2:
                        ctx_scale(b + 1)

            def body(b, slot, more, pair):
                for hp in range(HP):
                    step(b, slot, hp, True, more, pair)

            def drain(b, slot, pair):
                step(b, slot, 0, False, False, pair)
                for hp in (1, 2, 3):
                    p3 = back(b, slot, hp, 3)
                    if p3[0] is not b:
                        dve.wait_ge(s_yt, count(p3[0], p3[2]))
                        dve.tensor_copy(y_t[:], OC[:, 0:C].rearrange("p (k m) -> p k m", k=CK)).then_inc(s_yte, 1)
                    if hp == 3:
                        dve.wait_ge(s_wo, pair + 1)
                        dve.tensor_tensor(x1[:, ds(pair, 1), :], x1[:, ds(pair, 1), :], MB[:, 0:C].unsqueeze(1),
                                          ALU.add).then_inc(s_woe, 1)

            dve.wait_ge(ld_wvo, 48)
            all_steps(dve, body, drain)

            dve.wait_ge(ld_idx, 16)
            index = idx_rows[:].bitcast(I32)
            dve.tensor_scalar(index[:, 1, :], index[:, 0, :], P - 1, None, ALU.bitwise_and)
            link(dve.tensor_scalar(index[:, 2, :], index[:, 0, :], P.bit_length() - 1, None, ALU.arith_shift_right))
            dve.wait_ge(s_woe, B // 2)
            dve.tensor_copy(place_f[:], index[:, 1, :])
            dve.tensor_copy(tile_f[:], index[:, 2, :]).then_inc(r_idx, 1)
            stats(x1, tstat, tmv, TT).then_inc(m_stat, 1)
            dve.wait_ge(r_tab, 1)
            dve.wait_ge(r_idx, 1)
            dve.tensor_tensor(onetile[:], iota_f[:, 0:TT].unsqueeze(1).to_broadcast((P, SC * E, TT)),
                              tile_f[:].unsqueeze(2).to_broadcast((P, SC * E, TT)), ALU.is_equal)
            dve.tensor_tensor(onehot[:], iota_f[:].unsqueeze(1).to_broadcast((P, SC * E, P)),
                              place_f[:].unsqueeze(2).to_broadcast((P, SC * E, P)), ALU.is_equal).then_inc(r_oh, 1)
            dve.wait_ge(m_rs, 1)
            for rstd, dst in ((trstd2, xn), (trstd, mres)):
                for t in range(TT):
                    last = dve.tensor_scalar(dst[:, t, :], x1[:, t, :], tmv[:, t, 0:1], rstd[:, t:t + 1],
                                             ALU.subtract, ALU.mult)
            link(last)
            dve.wait_ge(ld_mam, 16 * 11)
            link(dve.tensor_tensor(xn[:], xn[:], nwb[:, 0:1, :].to_broadcast((P, TT, C)), ALU.mult))
            dve.tensor_tensor(xn[:], xn[:], nwb[:, 1:2, :].to_broadcast((P, TT, C)), ALU.add).then_inc(m_ln, 1)
            dve.wait_ge(m_xt, 1)
            link(dve.tensor_copy(xn_t[:], TWO))
            dve.sem_inc(m_xte, 1)
            for d in range(DT):
                dve.wait_ge(m_xze, d + 1)
                o = conv[:, d, :].rearrange("p (b l) -> p b l", l=L)
                link(dve.tensor_scalar(o, xpad[:, d, :, 0:L], convw[:, d, 0:1], dvec[:, 0, d:d + 1],
                                       ALU.mult, ALU.add))
                for k in range(1, TAPS):
                    ins = dve.scalar_tensor_tensor(out=o, in0=xpad[:, d, :, k:k + L], scalar=convw[:, d, k:k + 1],
                                                   in1=o, op0=ALU.mult, op1=ALU.add)
                    if k < TAPS - 1:
                        link(ins)
                ins.then_inc(m_conv, 1)
            dve.wait_ge(r_cnt, 1)
            counts = psum[:, 7, 0:TT * E].rearrange("p (e t) -> p t e", t=TT)
            dve.tensor_scalar(valid[:], counts, 1.0, None, ALU.min).then_inc(r_val, 1)
            dve.wait_ge(ld_comb, 32)
            dve.tensor_tensor(coef[:], counts, comb[:], ALU.mult).then_inc(r_val, 1)
            dve.wait_ge(m_dhi, 1)
            dve.tensor_tensor(dbc_lo[:], psum[0:NX, 2, :], dbc_hi[:].bitcast(F32), ALU.subtract).then_inc(m_dlo, 1)
            dve.wait_ge(r_pre, 1)
            link(dve.tensor_tensor(slot_of[:], psum[:, 7, 64:64 + TT * E].rearrange("p (t e) -> p t e", e=E),
                                   valid[:], ALU.mult))
            dve.tensor_scalar(slot_of[:], slot_of[:], 1.0, None, ALU.subtract).then_inc(r_pos, 1)
            link(dve.tensor_reduce(most[:], psum[:, 7, 128:128 + E], X, ALU.max))
            dve.tensor_copy(most_i[:], most[:]).then_inc(r_pos, 1)
            dve.wait_ge(m_dt0, 1)
            for d in range(DT):
                dve.tensor_scalar(state[0][:, d, :], psum[:, 3, :], dvec[:, 1, d:d + 1], dvec[:, 2, d:d + 1],
                                  ALU.mult, ALU.add).then_inc(m_dtu, 1)

            def picks(r):
                if not isinstance(r, int):
                    dve.wait_ge(f_cs, r)
                    dve.wait_ge(f_gat, EG * CK * r)
                    apart(dve)
                    dve.tensor_scalar(slot_of[:], slot_of[:], -float(P), None, ALU.add).then_inc(f_shift, 1)
                    dve.wait_ge(f_shift, r)
                    apart(dve)
                dve.tensor_tensor(pick[:].rearrange("p t e s -> p (t e) s"),
                                  iota_f[:].unsqueeze(1).to_broadcast((P, TT * E, P)),
                                  slot_of[:].rearrange("p t e -> p (t e)").unsqueeze(2).to_broadcast((P, TT * E, P)),
                                  ALU.is_equal).then_inc(f_pick, 1)

            dve.wait_ge(r_pos, 2)
            picks(0)
            dve.wait_ge(m_dta, DT)
            link(dve.scalar_tensor_tensor(out=dts[:], in0=state[0][:], scalar=0.0, in1=read[1][:],
                                          op0=ALU.max, op1=ALU.add))
            dve.tensor_tensor(dtx[:], dts[:], xc[:], ALU.mult).then_inc(m_dtx, 1)
            for n in range(NS):
                i = n % 2
                dve.wait_ge(m_z0, n + 1)
                dve.wait_ge(m_drv, n + 1)
                flat = "p a b -> p (a b)"
                dve.tensor_tensor_scan(state[i][:].rearrange(flat), dec[i][:].rearrange(flat),
                                       drive[i][:].rearrange(flat), 0.0, ALU.mult, ALU.add).then_inc(m_scan, 1)
                dve.wait_ge(m_scan, n + 1)
                dve.wait_ge(m_c, n + 1)
                if n >= 2:
                    dve.wait_ge(m_acc, n - 1)
                dve.tensor_tensor(read[i][:], state[i][:], psum[:, 5 + i:6 + i, :].to_broadcast((P, DT, T)),
                                  ALU.mult).then_inc(m_rd, 1)
            dve.wait_ge(m_acc, NS)
            for d in range(DT):
                link(dve.scalar_tensor_tensor(out=conv[:, d, :], in0=xc[:, d, :], scalar=dvec[:, 3, d:d + 1],
                                              in1=psum[:, d, :], op0=ALU.mult, op1=ALU.add))
            dve.tensor_tensor(conv[:], conv[:], zs[:], ALU.mult).then_inc(m_y, 1)
            for t in range(TT):
                dve.wait_ge(m_y, 2 + t)
                link(dve.tensor_tensor(mres[:, t, :], mres[:, t, :], psum[:, 4 + t, 0:C], ALU.add))
                dve.tensor_tensor(x1[:, t, :], x1[:, t, :], mres[:, t, :], ALU.add).then_inc(m_out, 1)

            dve.wait_ge(m_out, TT)
            stats(x1, fstat, fmv, TT).then_inc(f_stat, 1)
            dve.wait_ge(f_rs, 1)
            for t in range(TT):
                last = dve.tensor_scalar(f_nat[:, t, :], x1[:, t, :], fmv[:, t, 0:1], frstd[:, t:t + 1],
                                         ALU.subtract, ALU.mult)
                last.then_inc(f_ln, 1)
            for t in range(TT):
                dve.wait_ge(f_hi_done, t + 1)
                dve.tensor_tensor(f_lo[:, t, :], f_nat[:, t, :], f_hi[:, t, :].bitcast(F32), ALU.subtract)\
                    .then_inc(f_lo_done, 1)
            for k in range(CK):
                dve.wait_ge(f_b2, k + 1)
                dve.tensor_copy(acc_t[:, k, :], psum[:, 6 + k, :]).then_inc(f_sce, 1)

            def expert_round(r):
                dve.wait_ge(f_cs, r + 1)
                apart(dve)
                dve.tensor_reduce(coef_slot[:], psum[:, 4, 0:2 * E].rearrange("p (e h) -> p e h", h=2), X, ALU.add)\
                    .then_inc(f_cse, 1)
                dve.wait_ge(f_cse, r + 1)
                apart(dve)
                with dve.Fori(0, EG) as q:
                    for i in range(RING):
                        e = E * r + RING * q + i
                        dve.wait_ge(f_o, e + 1)
                        dve.tensor_scalar(o_s[:], psum[:, 4 + i % 2, 0:C], coef_slot[:, ds(RING * q + i, 1)], None,
                                          ALU.mult).then_inc(f_os, 1)
                        dve.wait_ge(f_oh, e + 1)
                        dve.tensor_tensor(o_lo[:], o_s[:], o_hi[:].bitcast(F32), ALU.subtract).then_inc(f_ol, 1)
                    dve.wait_ge(f_sc, EG * r + q + 1)
                    dve.wait_ge(f_sce, CK * (EG * r + q + 1))
                    for k in range(CK):
                        dve.tensor_tensor(acc_t[:, k, :], acc_t[:, k, :], psum[:, 6 + k, :], ALU.add)\
                            .then_inc(f_sce, 1)
                dve.wait_ge(f_sce, CK * (EG * (r + 1) + 1))

            expert_round(0)

            def next_round(r):
                picks(r)
                expert_round(r)

            further_rounds(dve, next_round)
            dve.sem_inc(f_all, ROUNDS)
            for t in range(TT):
                dve.wait_ge(f_fin, t + 1)
                dve.tensor_tensor(res_nat[:, t, :], x1[:, t, :], psum[:, t, 0:C], ALU.add).then_inc(f_done, 1)

        @block.scalar
        def _(act):
            for g in range(HP // 2):
                act.wait_ge(s_pwk, g + 1)
                act.activation(wk_t[:, 2 * g:2 * g + 2, :], TP[g % 2].rearrange("p (a c) -> p a c", c=C), ACT.Copy)\
                    .then_inc(s_pwke, 1)
            act.wait_ge(s_pevac, 1)
            act.activation(latt_hi[:], TWO, ACT.Copy).then_inc(s_pevac, 1)
            for t in range(HP):
                act.wait_ge(s_pq, t + 1)
                act.activation(q_t[:, t, :], psum[:, 5 + t % 2, :], ACT.Copy).then_inc(s_pqe, 1)
            act.wait_ge(s_pqe, HP)
            act.wait_ge(s_id, 1)
            for h in range(2):
                rows = slice(h * DH, (h + 1) * DH)
                act.activation(q_cur[rows, :, h, :], q_t[rows, :, 0:L], ACT.Copy).then_inc(s_qcur, 1)

            def misc_hi(b, slot, m):
                act.wait_ge(s_misc, misc_count(b, m))
                act.activation(misc_dst(slot, m, True), MB, ACT.Copy).then_inc(s_mhi, 1)

            for m in range(MISC):
                misc_hi(0, 0, m)

            def tail_hi(part, now):
                b, slot, hp = now
                u = hp % 2
                turned, high, where, t0, t1 = {"A": (s_tA, s_hA, TP[0], 0, 4), "B": (s_tB, s_hB, TP[1], 4, 8),
                                               "C": (s_tC, s_hC, TP[0], 8, 9)}[part]
                act.wait_ge(turned, count(b, hp))
                rows = slice(0, P) if part != "C" else half(slot)
                act.activation(pt_hi[u][rows, t0:t1, :],
                               where[rows, 0:(t1 - t0) * P].rearrange("p (t m) -> p t m", m=P), ACT.Copy)\
                    .then_inc(high, 1)

            def mean_value(now):
                b, slot, hp = now
                act.wait_ge(s_pv, count(b, hp))
                act.wait_ge(s_rd, count(b, hp))
                before = back(b, slot, hp, 1)
                if before:
                    act.wait_ge(s_yt, count(before[0], before[2]))
                act.activation(y_n[:], PV, ACT.Copy, scale=rden[slot][:, hp:hp + 1]).then_inc(s_y, 1)

            def keep_out(now, pair):
                b, slot, hp = now
                act.wait_ge(s_o, count(b, hp))
                if slot == 0 and pair is not None:
                    act.wait_ge(s_wo, pair + 1)
                act.activation(o_t[:, hp, slot * L:(slot + 1) * L], OC[:, C:C + L], ACT.Copy).then_inc(s_oe, 1)

            def step(b, slot, hp, live, more, pair):
                p1, p2, p3 = (back(b, slot, hp, n) for n in (1, 2, 3))
                if p3:
                    mean_value(p3)
                if p1:
                    if p3:
                        act.wait_ge(s_pv, count(p3[0], p3[2]))
                    tail_hi("A", p1)
                    tail_hi("B", p1)
                if live:
                    act.wait_ge(s_nb, count(b, hp))
                    if p2:
                        act.wait_ge(s_tC, count(p2[0], p2[2]))
                    act.activation(prob[hp % 2][:], LG, ACT.Exp, bias=nbias[slot][:, hp:hp + 1], scale=SCALE,
                                   accum_out=den[slot][:, hp:hp + 1]).then_inc(s_exp, 1)
                if p1:
                    tail_hi("C", p1)
                if p3:
                    keep_out(p3, pair if hp >= 3 else None)
                if more:
                    misc_hi(b + 1, 1 - slot, hp)

            def body(b, slot, more, pair):
                for hp in range(HP):
                    step(b, slot, hp, True, more, pair)

            def drain(b, slot, pair):
                step(b, slot, 0, False, False, None)
                for hp in (1, 2):
                    p3 = back(b, slot, hp, 3)
                    mean_value(p3)
                    keep_out(p3, None)

            all_steps(act, body, drain)

            act.wait_ge(ld_mam, 16 * 11)
            act.activation(a_neg[:], a_neg[:], ACT.Exp).then_inc(m_aneg, 1)
            act.wait_ge(m_aneg, 1)
            act.activation(a_neg[:], a_neg[:], ACT.Copy, scale=-1.0).then_inc(m_aneg, 1)
            act.wait_ge(m_ln, 1)
            for t in range(2 * DT):
                act.wait_ge(m_xz, t + 1)
                if t < DT:
                    act.activation(xpad[:, t, :, TAPS - 1:], psum[:, t % 2, :].rearrange("p (b l) -> p b l", l=L),
                                   ACT.Copy).then_inc(m_xze, 1)
                else:
                    act.activation(zs[:, t - DT, :], psum[:, t % 2, :], ACT.Silu).then_inc(m_xze, 1)
            act.wait_ge(r_b1, 1)
            act.activation(b1_t[:], psum[:, 6, 0:E * FT], ACT.Copy).then_inc(r_b1e, 1)
            for d in range(DT):
                act.wait_ge(m_conv, d + 1)
                act.activation(xc[:, d, :], conv[:, d, :], ACT.Silu).then_inc(m_xc, 1)
            act.wait_ge(m_dbc, 1)
            act.activation(dbc_hi[:], psum[0:NX, 2, :], ACT.Copy).then_inc(m_dhi, 1)
            for d in range(DT):
                act.wait_ge(m_dtu, d + 1)
                act.activation(read[0][:, d, :], state[0][:, d, :], ACT.Abs).then_inc(s_act, 1)
            for d in range(DT):
                act.wait_ge(s_act, d + 1)
                act.activation(read[0][:, d, :], read[0][:, d, :], ACT.Exp, scale=-1.0).then_inc(s_act, 1)
            for d in range(DT):
                act.wait_ge(s_act, DT + d + 1)
                act.activation(read[1][:, d, :], read[0][:, d, :], ACT.Ln, bias=1.0).then_inc(m_dta, 1)
            act.wait_ge(m_dtx, 1)
            for n in range(NS):
                i = n % 2
                act.wait_ge(m_b, n + 1)
                if n >= 2:
                    act.wait_ge(m_drv, n - 1)
                act.activation(bmat[i][:], psum[:, 4 + 3 * i, :], ACT.Copy).then_inc(m_bs, 1)
                if n >= 2:
                    act.wait_ge(m_scan, n - 1)
                for d in range(DT):
                    last = act.activation(dec[i][:, d, :], dts[:, d, :], ACT.Exp, scale=a_neg[:, d, n:n + 1])
                last.then_inc(m_dec, 1)

            def turned(r, half):
                for e in range(half * RING, (half + 1) * RING):
                    act.wait_ge(f_turn, E * r + e + 1)
                    act.activation(pick_t[:, e, :], psum[:, 4 + e % RING, :], ACT.Copy).then_inc(f_turned, 1)

            def expert_round(r):
                for g in range(EG):
                    for k in range(CK):
                        act.wait_ge(f_gat, CK * EG * r + CK * g + k + 1)
                        act.activation(xg_t[:, k, g * RING:(g + 1) * RING, :],
                                       psum[:, CK * g + k, :].rearrange("p (e s) -> p e s", s=P), ACT.Copy)\
                            .then_inc(f_gate, 1)
                with act.Fori(0, EG) as q:
                    for i in range(RING):
                        e = E * r + RING * q + i
                        for f in range(FT):
                            act.wait_ge(f_h, FT * e + f + 1)
                            act.activation(hid[:, f, :], psum[:, f % 4, 0:P], ACT.Gelu_apprx_tanh,
                                           bias=b1_t[:, ds(FT * (RING * q + i) + f, 1)]).then_inc(f_he, 1)
                        act.wait_ge(f_os, e + 1)
                        act.activation(o_hi[:], o_s[:], ACT.Copy).then_inc(f_oh, 1)

            turned(0, 0)
            turned(0, 1)
            act.wait_ge(f_ct, 1)
            act.activation(coef_t[:], psum[0:E, 5, :], ACT.Copy).then_inc(f_cte, 1)
            for t in range(TT):
                act.wait_ge(f_ln, t + 1)
                act.activation(f_hi[:, t, :], f_nat[:, t, :], ACT.Copy).then_inc(f_hi_done, 1)
            expert_round(0)

            def next_round(r):
                turned(r, 0)
                turned(r, 1)
                expert_round(r)

            further_rounds(act, next_round)

        @block.tensor
        def _(pe):
            pe.wait_ge(s_id, 1)
            pe.wait_ge(ld_wk, 16)
            for g in range(HP // 2):
                if g >= 2:
                    pe.wait_ge(s_pwke, g - 1)
                for a in range(2):
                    for k in range(CK):
                        last = pe.transpose(TP[g % 2][:, (2 * a + k) * P:(2 * a + k + 1) * P],
                                            wk_nat[:, k, (2 * g + a) * P:(2 * g + a + 1) * P], ident[:])
                last.then_inc(s_pwk, 1)
            pe.wait_ge(s_pln, 1)
            for k in range(CK):
                for t in range(TT):
                    last = pe.transpose(psum[:, k, t * P:(t + 1) * P], x_lat[:, t, k * P:(k + 1) * P], ident[:])
            last.then_inc(s_platt, 1)
            pe.wait_ge(s_pevac, 1)
            pe.wait_ge(ld_wq, 16)
            for t in range(HP):
                if t >= 2:
                    pe.wait_ge(s_pqe, t - 1)
                for k in range(CK):
                    last = pe.matmul(psum[:, 5 + t % 2, :], wq_sb[:, k, t * P:(t + 1) * P], latt[:, k, :],
                                     start=(k == 0), stop=(k == CK - 1))
                last.then_inc(s_pq, 1)

            def misc(b, slot, m, after=None):
                if after is not None:
                    pe.wait_ge(s_woe, after)
                if not (isinstance(b, int) and b == 0 and m == 0):
                    pe.wait_ge(s_mlo, misc_count(b, m) - 1)
                if m < 4:
                    k, a = m // 2, m % 2
                    if m == 0:
                        pe.wait_ge(s_qcur, 2 * b + 2)
                    for n in range(HP // 2):
                        hp = a * HP // 2 + n
                        last = pe.matmul(MB[:, n * P:(n + 1) * P], wk_t[:, hp, k * P:(k + 1) * P],
                                         q_cur[:, hp].rearrange("p a l -> p (a l)"), start=True, stop=True)
                else:
                    h, k = m % 4 // 2, m % 2
                    if k == 0:
                        pe.wait_ge(s_cn, 2 * b + h + 1)
                    for j in range(4):
                        last = pe.transpose(MB[:, j * P:(j + 1) * P], ctx_nat[:, 4 * h + j, k * P:(k + 1) * P],
                                            ident[:])
                last.then_inc(s_misc, 1)

            pe.wait_ge(s_pwke, HP // 2)
            for m in range(MISC):
                misc(0, 0, m)

            def logits(b, slot, hp):
                for k in range(CK):
                    for q, x_, own in ((qk_hi, kvt_hi, latt_hi), (qk_hi, kvt_lo, latt_lo), (qk_lo, kvt_hi, latt_hi)):
                        w = q[slot][:, k, hp].rearrange("p a l -> p (a l)")
                        first, final = k == 0 and q is qk_hi and x_ is kvt_hi, k == CK - 1 and q is qk_lo
                        for n in range(2):
                            pe.matmul(psum[:, n, :], w, x_[slot][:, k, n * 512:(n + 1) * 512],
                                      start=first, stop=final)
                        last = pe.matmul(psum[:, 2, 0:L], w, own[:, k, ds(b * L, L)], start=first, stop=final)
                last.then_inc(s_lg, 1)

            def turn(now, part):
                b, slot, hp = now
                if part == "C":
                    pe.wait_ge(s_lA, count(b, hp))
                    apart(pe)
                    if slot == 0:
                        last = pe.transpose(TP[0][0:L, 0:P], prob[hp % 2][:, S:S + L], ident[:])
                    else:
                        last = pe.matmul(TP[0][half(slot), 0:P], prob[hp % 2][:, S:S + L], ident[:],
                                         start=True, stop=True)
                    last.then_inc(s_tC, 1)
                    return
                before = back(b, slot, hp, 1)
                if before:
                    pe.wait_ge(s_lC, count(before[0], before[2]))
                for n, done in ((0, s_tA), (1, s_tB)):
                    for j in range(4):
                        last = pe.transpose(TP[n][:, j * P:(j + 1) * P],
                                            prob[hp % 2][:, (4 * n + j) * P:(4 * n + j + 1) * P], ident[:])
                    last.then_inc(done, 1)

            def times_rows(now):
                b, slot, hp = now
                pe.wait_ge(s_lC, count(b, hp))
                if hp == 0:
                    pe.wait_ge(s_klo, b + 1)
                    pe.wait_ge(s_lcur, 3 * b + 3)
                before = back(b, slot, hp, 1)
                if before:
                    pe.wait_ge(s_y, count(before[0], before[2]))
                u = hp % 2
                for j in range(SJ):
                    for w, x_ in ((pt_hi, kvn_hi), (pt_hi, kvn_lo), (pt_lo, kvn_hi)):
                        pe.matmul(PV, w[u][:, j, :], x_[slot][:, j, :],
                                  start=(j == 0 and w is pt_hi and x_ is kvn_hi), stop=False)
                rows = half(slot)
                for n, (w, x_) in enumerate(((pt_hi, cur_hi), (pt_hi, cur_lo), (pt_lo, cur_hi))):
                    last = pe.matmul(PV, w[u][rows, SJ, :], x_[rows], start=False, stop=(n == 2))
                last.then_inc(s_pv, 1)

            def turn_value(now):
                b, slot, hp = now
                pe.wait_ge(s_y, count(b, hp))
                before = back(b, slot, hp, 1)
                if before:
                    pe.wait_ge(s_oe, count(before[0], before[2]))
                for k in range(CK):
                    last = pe.transpose(OC[:, k * P:(k + 1) * P], y_n[:, k * P:(k + 1) * P], ident[:])
                last.then_inc(s_yt, 1)

            def head_out(now):
                b, slot, hp = now
                pe.wait_ge(s_yte, count(b, hp))
                for h in range(2):
                    for k in range(CK):
                        last = pe.matmul(OC[h * DH:(h + 1) * DH, C:C + L],
                                         wv[:, k, (2 * hp + h) * DH:(2 * hp + h + 1) * DH],
                                         y_t[:, k, h * L:(h + 1) * L], start=(k == 0), stop=(k == CK - 1))
                last.then_inc(s_o, 1)

            def out_proj(pair, seen):
                pe.wait_ge(s_oe, HP * 2 * (pair + 1))
                pe.wait_ge(s_mlo, seen)
                for hp in range(HP):
                    last = pe.matmul(MB[:, 0:C], o_t[:, hp, :], wo[:, hp, :], start=(hp == 0), stop=(hp == HP - 1))
                last.then_inc(s_wo, 1)

            def step(b, slot, hp, live, more, pair):
                p1, p2, p3 = (back(b, slot, hp, n) for n in (1, 2, 3))
                if live:
                    if hp == 0:
                        pe.wait_ge(s_mlo, MISC * (b + 1))
                    if p1:
                        pe.wait_ge(s_exp, count(p1[0], p1[2]))
                    logits(b, slot, hp)
                if p1:
                    if not live:
                        pe.wait_ge(s_exp, count(p1[0], p1[2]))
                    turn(p1, "AB")
                if p3:
                    turn_value(p3)
                if slot == 0 and hp == 3 and pair is not None:
                    out_proj(pair, misc_count(b + 1, hp) - 1)
                if p2:
                    times_rows(p2)
                if p1:
                    turn(p1, "C")
                if p3:
                    head_out(p3)
                if more:
                    misc(b + 1, 1 - slot, hp, pair + 1 if slot == 0 and hp == 3 and pair is not None else None)

            def body(b, slot, more, pair):
                for hp in range(HP):
                    step(b, slot, hp, True, more, pair)

            def drain(b, slot, pair):
                step(b, slot, 0, False, False, None)
                turn_value(back(b, slot, 1, 3))
                times_rows(back(b, slot, 1, 2))
                head_out(back(b, slot, 1, 3))
                turn_value(back(b, slot, 2, 3))
                head_out(back(b, slot, 2, 3))
                out_proj(pair, MISC * B)

            pe.wait_ge(ld_wvo, 48)
            pe.wait_ge(s_plo, 1)
            all_steps(pe, body, drain)

            pe.wait_ge(m_ln, 1)
            for k in range(CK):
                for t in range(TT):
                    last = pe.transpose(psum[:, k, t * P:(t + 1) * P], xn[:, t, k * P:(k + 1) * P], ident[:])
            last.then_inc(m_xt, 1)
            pe.wait_ge(m_xte, 1)
            for t in range(2 * DT):
                if t >= 2:
                    pe.wait_ge(m_xze, t - 1)
                for k in range(CK):
                    last = pe.matmul(psum[:, t % 2, :], win[:, k, t * P:(t + 1) * P], xn_t[:, k, :],
                                     start=(k == 0), stop=(k == CK - 1))
                last.then_inc(m_xz, 1)
            pe.wait_ge(ld_comb, 32)
            pe.transpose(psum[:, 6, 0:E * FT], b1_rows[:], ident[0:E * FT, 0:E * FT]).then_inc(r_b1, 1)
            pe.wait_ge(r_oh, 1)
            for e in range(E):
                for j in range(SC):
                    last = pe.matmul(psum[:, 7, e * TT:(e + 1) * TT], onehot[:, j * E + e, :],
                                     onetile[:, j * E + e, :], start=(j == 0), stop=(j == SC - 1))
            last.then_inc(r_cnt, 1)
            for d in range(DT):
                pe.wait_ge(m_xc, d + 1)
                last = pe.matmul(psum[0:NX, 2, :], wxp[:, d, :], xc[:, d, :], start=(d == 0), stop=(d == DT - 1))
            last.then_inc(m_dbc, 1)
            pe.wait_ge(r_val, 2)
            upto = psum[:, 7, 64:64 + TT * E].rearrange("p (t e) -> p t e", e=E)
            pe.matmul(upto, before[:], valid[:], start=True, stop=False)
            for t in range(TT - 1):
                pe.matmul(upto[:, t + 1:, :], ones[:], valid[:, t:t + 1, :].to_broadcast((P, TT - 1 - t, E)),
                          start=False, stop=(t == TT - 2))
            for t in range(TT):
                last = pe.matmul(psum[:, 7, 128:128 + E], ones[:], valid[:, t, :], start=(t == 0),
                                 stop=(t == TT - 1))
            last.then_inc(r_pre, 1)
            pe.wait_ge(m_dlo, 1)
            pe.wait_ge(m_sel, 1)

            def spread(where, r):
                same = ident_r[:, r:r + 1].to_broadcast((NX, P))
                pe.matmul(where, same, dbc_hi[:], start=True, stop=False)
                return pe.matmul(where, same, dbc_lo[:], start=False, stop=True)

            spread(psum[:, 3, :], 0).then_inc(m_dt0, 1)
            pe.wait_ge(m_xze, 2 * DT)
            pe.wait_ge(m_dtx, 1)
            def spread_in(n):
                if n >= 2:
                    pe.wait_ge(m_bs, n - 1)
                spread(psum[:, 4 + 3 * (n % 2), :], 1 + n).then_inc(m_b, 1)

            def spread_out(n):
                if n >= 2:
                    pe.wait_ge(m_rd, n - 1)
                spread(psum[:, 5 + n % 2, :], 1 + NS + n).then_inc(m_c, 1)

            pe.wait_ge(r_pos, 2)
            pe.wait_ge(r_b1e, 1)
            for n in range(2):
                spread_in(n)
                spread_out(n)
            for n in range(NS):
                if n + 2 < NS:
                    spread_in(n + 2)
                pe.wait_ge(m_rd, n + 1)
                for d in range(DT):
                    last = pe.matmul(psum[:, d, :], ident[:], read[n % 2][:, d, :], start=(n == 0),
                                     stop=(n == NS - 1))
                last.then_inc(m_acc, 1)
                if n + 2 < NS:
                    spread_out(n + 2)

            def turn_picks(r, half):
                for e in range(half * RING, (half + 1) * RING):
                    if half == 1:
                        pe.wait_ge(f_turned, E * r + e - RING + 1)
                    for t in range(TT):
                        last = pe.transpose(psum[:, 4 + e % RING, t * P:(t + 1) * P], pick[:, t, e, :].bitcast(F32),
                                            ident[:])
                    last.then_inc(f_turn, 1)

            pe.wait_ge(f_pick, 1)
            pe.wait_ge(m_bs, NS)
            pe.wait_ge(m_rd, NS)
            turn_picks(0, 0)
            pe.wait_ge(m_y, 1)
            for t in range(TT):
                pe.wait_ge(f_turned, t + 1)
                for d in range(DT):
                    last = pe.matmul(psum[:, 4 + t, 0:C], conv[:, d, t * P:(t + 1) * P], wout[:, d, :],
                                     start=(d == 0), stop=(d == DT - 1))
                last.then_inc(m_y, 1)

            def slot_weights(r):
                pe.wait_ge(f_hl, 1)
                pe.wait_ge(f_turned, E * r + RING + 1)
                for e in range(E):
                    for t in range(TT):
                        last = pe.matmul(psum[:, 4, 2 * e:2 * e + 2], pick[:, t, e, :], coef_hl[:, t, e, :],
                                         start=(t == 0), stop=(t == TT - 1))
                last.then_inc(f_cs, 1)

            def expert_round(r):
                for g in range(EG):
                    for k in range(CK):
                        for t in range(TT):
                            for part in (f_hi, f_lo):
                                last = pe.matmul(psum[:, CK * g + k, :], part[:, t, k * P:(k + 1) * P],
                                                 pick[:, t, g * RING:(g + 1) * RING, :].rearrange("p e s -> p (e s)"),
                                                 start=(t == 0 and part is f_hi), stop=(t == TT - 1 and part is f_lo))
                        last.then_inc(f_gat, 1)
                pe.wait_ge(f_gate, CK * EG * (r + 1))

                def to_tokens(q, i):
                    pe.wait_ge(f_ol, E * r + RING * q + i + 1)
                    if i == 0:
                        pe.wait_ge(f_sce, CK * (EG * r + q + 1))
                    for k in range(CK):
                        for part in (o_hi, o_lo):
                            last = pe.matmul(psum[:, 6 + k, :], part[:, k * P:(k + 1) * P],
                                             pick_t[:, ds(RING * q + i, 1), :].rearrange("p e t -> p (e t)"),
                                             start=(i == 0 and part is o_hi), stop=(i == RING - 1 and part is o_lo))
                    return last

                apart(pe)
                with pe.Fori(0, EG) as q:
                    for i in range(RING):
                        e = E * r + RING * q + i
                        pe.wait_ge(ld_e[i], 32 * (EG * r + q + 1))
                        for f in range(FT):
                            if f >= 4:
                                pe.wait_ge(f_he, FT * e + f - 3)
                            for k in range(CK):
                                last = pe.matmul(psum[:, f % 4, 0:P], w1[i][:, k, f * P:(f + 1) * P],
                                                 xg_t[:, k, ds(RING * q + i, 1), :].rearrange("p e s -> p (e s)"),
                                                 start=(k == 0), stop=(k == CK - 1))
                            last.then_inc(f_h, 1)
                        if i > 0:
                            to_tokens(q, i - 1)
                        pe.wait_ge(f_he, FT * (e + 1))
                        if i == 0:
                            pe.wait_ge(f_cse, r + 1)
                        for f in range(FT):
                            last = pe.matmul(psum[:, 4 + i % 2, 0:C], hid[:, f, :], w2[i][:, f, :],
                                             start=(f == 0), stop=(f == FT - 1))
                        last.then_inc(f_o, 1)
                    to_tokens(q, RING - 1).then_inc(f_sc, 1)

            pe.wait_ge(m_out, TT)
            turn_picks(0, 1)
            slot_weights(0)
            pe.wait_ge(f_turned, E)
            for t in range(TT):
                last = pe.transpose(psum[0:E, 5, t * P:(t + 1) * P], coef[:, t, :], ident[:])
            last.then_inc(f_ct, 1)
            pe.wait_ge(f_cte, 1)
            pe.wait_ge(ld_b2, 16)
            for k in range(CK):
                pe.matmul(psum[:, 6 + k, :], b2_sb[:, k * P:(k + 1) * P], coef_t[:], start=True, stop=True)\
                    .then_inc(f_b2, 1)
            pe.wait_ge(f_lo_done, TT)
            expert_round(0)

            def next_round(r):
                pe.wait_ge(f_pick, r + 1)
                pe.wait_ge(f_sce, CK * (EG * r + 1))
                turn_picks(r, 0)
                turn_picks(r, 1)
                slot_weights(r)
                expert_round(r)

            further_rounds(pe, next_round)
            pe.wait_ge(f_all, ROUNDS)
            for t in range(TT):
                for k in range(CK):
                    last = pe.transpose(psum[:, t, k * P:(k + 1) * P], acc_t[:, k, t * P:(t + 1) * P], ident[:])
                last.then_inc(f_fin, 1)


_INS = ['x', 'ctx_1024', 'L0_xattn_Wq', 'L0_xattn_Wkv', 'L0_xattn_Wo', 'L0_xattn_ln1_w', 'L0_xattn_ln1_b',
        'L0_xattn_ln2_w', 'L0_xattn_ln2_b', 'L0_attn_norm_w', 'L0_attn_norm_b', 'L0_attn_W_in', 'L0_attn_conv_w',
        'L0_attn_conv_b', 'L0_attn_x_proj_w', 'L0_attn_dt_w', 'L0_attn_dt_b', 'L0_attn_A_log', 'L0_attn_D',
        'L0_attn_W_out', 'L0_ffn_combine_weights', 'L0_ffn_top_idx', 'L0_ffn_W1', 'L0_ffn_b1', 'L0_ffn_W2',
        'L0_ffn_b2']
_OUTS = [((8, 64, 256), 'float32')]


def kernel(**inputs):
    import numpy as _np
    import concourse.bacc as _bacc
    from concourse import mybir as _mybir
    from concourse.bass_utils import run_bass_kernel_spmd as _run

    nc = _bacc.Bacc("TRN2", target_bir_lowering=False, num_devices=1)
    arrays, args = {}, []
    for name in _INS:
        a = _np.ascontiguousarray(inputs[name])
        arrays[f"in_{name}_dram"] = a
        args.append(nc.dram_tensor(f"in_{name}_dram", a.shape, _mybir.dt.from_np(a.dtype), kind="ExternalInput").ap())
    for i, (shape, dtype) in enumerate(_OUTS):
        dt = _mybir.dt.from_np(_np.dtype(dtype))
        args.append(nc.dram_tensor(f"out_{i}_dram", shape, dt, kind="ExternalOutput").ap())
    perceiver_kernel(nc, *args)
    r = _run(nc, [arrays], core_ids=[0])
    got = tuple(r.results[0][f"out_{i}_dram"] for i in range(len(_OUTS)))
    return got[0]
```

```python
from contextlib import ExitStack

import concourse.bass as bass
from concourse import mybir

F32 = mybir.dt.float32
F32R = mybir.dt.float32r
BF16 = mybir.dt.bfloat16
I32 = mybir.dt.int32
ALU = mybir.AluOpType
ACT = mybir.ActivationFunctionType
X = mybir.AxisListType.X
XY = mybir.AxisListType.XY
ds = bass.ds

P = 128
EPS = 1e-5


def perceiver_kernel(nc, x, ctx_in, Wq, Wkv, Wo, ln1_w, ln1_b, ln2_w, ln2_b,
                     norm_w, norm_b, W_in, conv_w, conv_b, x_proj_w, dt_w, dt_b, A_log, D_skip, W_out,
                     combine_w, top_idx, W1, b1, W2, b2, out):
    B, L, C = x.shape
    S = ctx_in.shape[1]
    INNER = Wq.shape[1]
    DH = 64
    HP = INNER // (2 * DH)
    CK = C // P
    SJ = S // P
    T = B * L
    TT = T // P
    BP = P // L
    DI = conv_w.shape[0]
    DT = DI // P
    TAPS = conv_w.shape[1]
    NS = A_log.shape[1]
    NX = x_proj_w.shape[1]
    E, _, FF = W1.shape
    FT = FF // P
    SC = top_idx.shape[0] // P
    RING = 4
    EG = E // RING
    ROUNDS = T // P
    SCALE = float(DH) ** -0.5
    GT = 4
    MISC = 8
    assert HP == MISC and C == 2 * P and P == 2 * L and SJ == 8 and TT * P == T == 512

    top = ExitStack()
    with top:
        def sem(name):
            return top.enter_context(nc.semaphore(name))

        def sb(stack, name, shape, dt=F32):
            return stack.enter_context(nc.sbuf_tensor(name, shape, dt))

        def row(v):
            return v.rearrange("(a d) -> a d", a=1)

        ident = sb(top, "ident", [P, P])
        x1 = sb(top, "x1", [P, TT, C])
        q_t = sb(top, "q_t", [P, HP, T])
        psum = top.enter_context(nc.psum_tensor("psum", [P, 8, 512], F32))

        att = ExitStack()
        ctx_nat = sb(att, "ctx_nat", [P, SJ, C])
        kvn_hi = [sb(att, "kvn_hi0", [P, SJ, C], F32R), None]
        kvn_lo = [sb(att, "kvn_lo0", [P, SJ, C], F32R), None]
        kvt_hi = [sb(att, f"kvt_hi{i}", [P, CK, S + L], F32R) for i in range(2)]
        kvt_lo = [sb(att, f"kvt_lo{i}", [P, CK, S + L], F32R) for i in range(2)]
        qk_hi = [sb(att, f"qk_hi{i}", [P, CK, HP, 2, L], F32R) for i in range(2)]
        qk_lo = [sb(att, f"qk_lo{i}", [P, CK, HP, 2, L], F32R) for i in range(2)]
        x_lat = sb(att, "x_lat", [P, TT, C])
        lat_cur = sb(att, "lat_cur", [P, C])
        cur_hi = sb(att, "cur_hi", [P, C], F32R)
        cur_lo = sb(att, "cur_lo", [P, C], F32R)
        latt_hi = sb(att, "latt_hi", [P, CK, T], F32R)
        latt_lo = sb(att, "latt_lo", [P, CK, T], F32R)
        q_cur = sb(att, "q_cur", [P, HP, 2, L])
        wk_t = sb(att, "wk_t", [P, HP, C])
        wv = sb(att, "wv", [P, CK, INNER])
        wo = sb(att, "wo", [P, HP, C])
        prob = [sb(att, f"prob{i}", [P, S + L]) for i in range(2)]
        y_n = sb(att, "y_n", [P, C])
        y_t = sb(att, "y_t", [P, CK, P])
        o_t = sb(att, "o_t", [P, HP, P])
        ln1wb = sb(att, "ln1wb", [P, 2, C])
        cstat = sb(att, "cstat", [P, SJ, 6])
        cmv = sb(att, "cmv", [P, SJ, 2])
        cvar = sb(att, "cvar", [P, SJ])
        crstd = sb(att, "crstd", [P, SJ])
        cnm = sb(att, "cnm", [P, SJ])
        cshift = sb(att, "cshift", [P, SJ])
        mhalf = sb(att, "mhalf", [P, SJ])
        lvar = sb(att, "lvar", [P, TT])
        lstat = sb(att, "lstat", [P, TT, 6])
        lmv = sb(att, "lmv", [P, TT, 2])
        lscale = sb(att, "lscale", [P, TT])
        lnm = sb(att, "lnm", [P, TT])
        lshift = sb(att, "lshift", [P, TT])
        rowmax = [sb(att, f"rowmax{i}", [P, HP, 2]) for i in range(2)]
        den_part = [sb(att, f"den_part{i}", [P, HP, 2]) for i in range(2)]
        nbias = [sb(att, f"nbias{i}", [P, HP]) for i in range(2)]
        den = [sb(att, f"den{i}", [P, HP]) for i in range(2)]
        rden = [sb(att, f"rden{i}", [P, HP]) for i in range(2)]
        pro = ExitStack()
        wq_sb = sb(pro, "wq_sb", [P, CK, INNER])
        wk_nat = sb(pro, "wk_nat", [P, CK, INNER])
        latt = sb(pro, "latt", [P, CK, T])
        ln2wb = sb(pro, "ln2wb", [P, 2, C])
        pro.close()
        kvn_hi[1] = sb(att, "kvn_hi1", [P, SJ, C], F32R)
        kvn_lo[1] = sb(att, "kvn_lo1", [P, SJ, C], F32R)
        pt_hi = [sb(att, f"pt_hi{i}", [P, SJ + 1, P], F32R) for i in range(2)]
        pt_lo = [sb(att, f"pt_lo{i}", [P, SJ + 1, P], F32R) for i in range(2)]
        att.close()

        mam = ExitStack()
        room = q_t[:].rearrange("p h t -> p (h t)")
        used = [0]

        def part(*shape):
            size = 1
            for n in shape:
                size *= n
            view = room[:, used[0]:used[0] + size]
            used[0] += size
            return view.rearrange("p (a b) -> p a b", b=shape[-1])

        win = part(CK, 2 * DI)
        wout = part(DT, C)
        NR = 64 + NX
        wxp = part(DT, NR)
        convw = part(DT, TAPS)
        dvec = part(4, DT)
        nwb = part(2, CK)
        a_neg = part(DT, NS)
        idx_rows = part(3, SC * E)
        warm_out = sb(mam, "warm_out", [P, 1])
        pick = sb(mam, "pick", [P, TT, E, P], F32R)
        pick_t = sb(mam, "pick_t", [P, E, T], F32R)
        lists = ExitStack()
        onehot = sb(lists, "onehot", [P, SC * E, P], BF16)
        lists.close()
        acc_t = sb(mam, "acc_t", [P, CK, T])
        coef_t = sb(mam, "coef_t", [E, T])
        b2_sb = sb(mam, "b2_sb", [E, C])
        sb(mam, "rest_of_lists", [P, C])
        onetile = sb(mam, "onetile", [P, SC * E, TT], BF16)
        place_f = sb(mam, "place_f", [P, SC * E])
        tile_f = sb(mam, "tile_f", [P, SC * E])
        iota_i = sb(mam, "iota_i", [P, P], I32)
        iota_f = sb(mam, "iota_f", [P, P])
        upto_ones = sb(mam, "upto_ones", [P, P], BF16)
        ones = sb(mam, "ones", [P, P], BF16)
        valid = sb(mam, "valid", [P, TT, E], BF16)
        slot_of = sb(mam, "slot_of", [P, TT, E])
        most = sb(mam, "most", [P, 1])
        most_i = sb(mam, "most_i", [P, 1], I32)
        comb = sb(mam, "comb", [P, TT, E])
        coef = sb(mam, "coef", [P, TT, E])
        coef_hl = sb(mam, "coef_hl", [P, TT, E, 2], F32R)
        b1_rows = sb(mam, "b1_rows", [E * FT, P])
        b1_t = sb(mam, "b1_t", [P, E * FT])
        mres = sb(mam, "mres", [P, TT, C])
        conv = sb(mam, "conv", [P, DT, T])
        pair_r = sb(mam, "pair_r", [NR, NX], F32R)
        dbc = sb(mam, "dbc", [NR, T], F32R)
        bmat = [sb(mam, f"bmat{i}", [P, T]) for i in range(2)]
        tstat = sb(mam, "tstat", [P, TT, 6])
        tmv = sb(mam, "tmv", [P, TT, 2])
        tvar = sb(mam, "tvar", [P, TT])
        trstd = sb(mam, "trstd", [P, TT])
        tvar2 = sb(mam, "tvar2", [P, TT])
        trstd2 = sb(mam, "trstd2", [P, TT])
        thalf = sb(mam, "thalf", [P, TT])
        front = ExitStack()
        xn = sb(front, "xn", [P, TT, C])
        xn_t = sb(front, "xn_t", [P, CK, T])
        xpad = sb(front, "xpad", [P, DT, B, L + TAPS - 1])
        front.close()
        w1, w2 = [sb(mam, "w1_0", [P, CK, FF])], [sb(mam, "w2_0", [P, FT, C])]
        sb(mam, "rest_of_front", [P, DT * B * (L + TAPS - 1) + TT * C + CK * T - CK * FF - FT * C])
        steps = ExitStack()
        dec = [sb(steps, f"dec{i}", [P, DT, T]) for i in range(2)]
        drive = [sb(steps, f"drive{i}", [P, DT, T]) for i in range(2)]
        steps.close()
        for i in (1, 2):
            w1.append(sb(mam, f"w1_{i}", [P, CK, FF]))
            w2.append(sb(mam, f"w2_{i}", [P, FT, C]))
        res = ExitStack()
        state = [sb(res, f"state{i}", [P, DT, T]) for i in range(2)]
        read = [sb(res, f"read{i}", [P, DT, T]) for i in range(2)]
        res.close()
        w1.append(sb(mam, "w1_3", [P, CK, FF]))
        w2.append(sb(mam, "w2_3", [P, FT, C]))
        xg_t = sb(mam, "xg_t", [P, CK, E, P])
        hid = sb(mam, "hid", [P, FT, P])
        sb(mam, "rest_of_res", [P, FT, P])
        oper = ExitStack()
        dts = sb(oper, "dts", [P, DT, T])
        dtx = sb(oper, "dtx", [P, DT, T])
        xc = sb(oper, "xc", [P, DT, T])
        zs = sb(oper, "zs", [P, DT, T])
        oper.close()
        coef_slot = sb(mam, "coef_slot", [P, E])
        o_s = sb(mam, "o_s", [P, C])
        o_hi = sb(mam, "o_hi", [P, C], F32R)
        o_lo = sb(mam, "o_lo", [P, C], F32R)
        f_nat = sb(mam, "f_nat", [P, TT, C])
        f_hi = sb(mam, "f_hi", [P, TT, C], F32R)
        f_lo = sb(mam, "f_lo", [P, TT, C], F32R)
        res_nat = sb(mam, "res_nat", [P, TT, C])
        fstat = sb(mam, "fstat", [P, TT, 6])
        fmv = sb(mam, "fmv", [P, TT, 2])
        fvar = sb(mam, "fvar", [P, TT])
        frstd = sb(mam, "frstd", [P, TT])
        fhalf = sb(mam, "fhalf", [P, TT])
        mam.close()

        TWO = psum[:, 0:2, :]
        CUT = 364
        LG_A, LG_B = psum[:, 0:2, 0:CUT], psum[:, 2, 0:S + L - 2 * CUT]
        TP, PV, OC, MB = [psum[:, 3, :], psum[:, 4, :]], psum[:, 5, 0:C], psum[:, 6, :], psum[:, 7, :]

        XB = (0, 1, 3, 6)
        GB = (0, 6)

        ld_xlat, ld_vec, ld_wq, ld_wk, ld_wvo, ld_ctx = (sem(n) for n in (
            "ld_xlat", "ld_vec", "ld_wq", "ld_wk", "ld_wvo", "ld_ctx"))
        ld_vec2 = sem("ld_vec2")
        ld_mam, ld_idx, ld_comb, ld_b2, ld_out = (sem(n) for n in ("ld_mam", "ld_idx", "ld_comb", "ld_b2", "ld_out"))
        ld_e = [sem(f"ld_e{i}") for i in range(RING)]
        s_dve, s_pool, s_act = sem("s_dve"), sem("s_pool"), sem("s_act")
        s_apart, s_psc, s_lcur, m_rs, f_rs = (sem(n) for n in ("s_apart", "s_psc", "s_lcur", "m_rs", "f_rs"))
        s_id, s_pstat, s_pln, s_platt, s_pevac, s_pq, s_pqe, s_pwk, s_pwke, s_plo = (sem(n) for n in (
            "s_id", "s_pstat", "s_pln", "s_platt", "s_pevac", "s_pq", "s_pqe", "s_pwk", "s_pwke", "s_plo"))
        s_cst, s_cmv, s_cvar, s_crs, s_cnm, s_csh, s_cz, s_cw, s_cn, s_khi, s_klo, s_qcur = (sem(n) for n in (
            "s_cst", "s_cmv", "s_cvar", "s_crs", "s_cnm", "s_csh", "s_cz", "s_cw", "s_cn", "s_khi", "s_klo",
            "s_qcur"))
        s_misc, s_mhi, s_mlo = sem("s_misc"), sem("s_mhi"), sem("s_mlo")
        (s_lg, s_mx, s_nb, s_exp, s_tA, s_tB, s_tC, s_hA, s_hB, s_hC, s_lA, s_lB, s_lC,
         s_rd, s_pv, s_y, s_yt, s_yte, s_o, s_oe) = (sem("s_" + n) for n in (
             "lg mx nb exp tA tB tC hA hB hC lA lB lC rd pv y yt yte o oe").split())
        s_own = sem("s_own")
        s_den = sem("s_den")
        s_wo, s_woe = sem("s_wo"), sem("s_woe")
        (m_stat, m_ln, m_xt, m_xte, m_pad, m_xz, m_xze, m_tap, m_conv, m_xc, m_dbc, m_dhi, m_dlo, m_dt0, m_dtu, m_dta,
         m_dts, m_dtx, m_sel, m_aneg, m_b, m_bs, m_c, m_dec, m_z0, m_drv0, m_drv, m_scan, m_rd, m_acc, m_y, m_yo,
         m_x1m, m_res, m_zs, m_out) = (sem("m_" + n) for n in (
             "stat ln xt xte pad xz xze tap conv xc dbc dhi dlo dt0 dtu dta dts dtx sel aneg b bs c dec z0 drv0 drv "
             "scan rd acc y yo x1m res zs out").split())
        r_idx, r_tab, r_oh, r_cnt, r_val, r_pre, r_pos, r_b1, r_b1e = (sem("r_" + n) for n in (
            "idx tab oh cnt val pre pos b1 b1e").split())
        (f_bn, f_stat, f_ln, f_hi_done, f_lo_done, f_hl, f_ct, f_cte, f_pick, f_turn, f_turned, f_cs, f_cse, f_gat,
         f_gate, f_h, f_he, f_o, f_os, f_oh, f_ol, f_sc, f_sce, f_b2, f_b2e, f_shift, f_all, f_fin, f_done) = (
            sem("f_" + n) for n in (
                "bn stat ln hi lo hl ct cte pick turn turned cs cse gat gate h he o os oh ol sc sce b2 b2e shift all "
                "fin done").split())

        def count(b, hp):
            return HP * b + hp + 1

        def back(b, slot, hp, n):
            if hp >= n:
                return b, slot, hp - n
            if isinstance(b, int) and b == 0:
                return None
            return b - 1, 1 - slot, hp - n + HP

        def apart(eng):
            eng.sem_inc(s_apart, 1)

        def misc_count(b, m):
            return MISC * b + m + 1

        def misc_dst(slot, m, hi):
            if m < 4:
                k, a = m // 2, m % 2
                return (qk_hi if hi else qk_lo)[slot][:, k, a * HP // 2:(a + 1) * HP // 2]\
                    .rearrange("p h a l -> p (h a l)")
            h, k = m % 4 // 2, m % 2
            return (kvt_hi if hi else kvt_lo)[slot][:, k, h * 512:(h + 1) * 512]

        first_groups = list(zip(list(range(4, MISC)) + list(range(4)), (7, 2, 0, 1, 3, 4, 5, 6)))

        def half(slot):
            return slice(slot * L, (slot + 1) * L)

        def all_steps(loops, body, drain):
            body(0, 0, True, None)
            with loops.Fori(0, B // 2 - 1) as p:
                body(2 * p + 1, 1, True, None)
                body(2 * p + 2, 0, True, p)
            body(B - 1, 1, False, None)
            drain(B, 0, B // 2 - 1)

        def further_rounds(eng, do_round):
            eng.wait_ge(r_pos, 2)
            longest = eng.value_load(most_i[0:1, 0:1], min_val=0, max_val=T)
            with eng.If(longest > P):
                with eng.Fori(1, ROUNDS) as r:
                    do_round(r)

        block = top.enter_context(nc.Block())

        @block.sync
        def _(sp):
            sp.dma_start(x_lat[:], x.rearrange("(t b) l c -> (b l) t c", b=BP)).then_inc(ld_xlat, 16)
            wkv = Wkv.rearrange("(k p) n -> p k n", p=P)
            sp.dma_start(wk_nat[:], wkv[:, :, 0:INNER]).then_inc(ld_wk, 16)
            for i, v in enumerate((ln2_w, ln2_b)):
                sp.dma_start(ln2wb[:, i, :], row(v).to_broadcast((P, C))).then_inc(ld_vec2, 16)
            sp.dma_start(ctx_nat[:], ctx_in[0].rearrange("(p j) c -> p j c", j=SJ)).then_inc(ld_ctx, 16)
            for i, v in enumerate((ln1_w, ln1_b)):
                sp.dma_start(ln1wb[:, i, :], row(v).to_broadcast((P, C))).then_inc(ld_vec, 16)
            sp.dma_start(wq_sb[:], Wq.rearrange("(k p) n -> p k n", p=P)).then_inc(ld_wq, 16)
            sp.dma_start(wv[:], wkv[:, :, INNER:2 * INNER]).then_inc(ld_wvo, 16)
            sp.dma_start(wo[:], Wo.rearrange("(h p) n -> p h n", p=P)).then_inc(ld_wvo, 16)
            sp.dma_start(x1[:], x.rearrange("(t b) l c -> (b l) t c", b=BP)).then_inc(ld_wvo, 16)
            with sp.Fori(1, B) as b:
                sp.wait_ge(s_misc, MISC * b)
                sp.wait_ge(s_klo, b)
                sp.dma_start(ctx_nat[:], ctx_in[ds(b, 1)].rearrange("a (p j) c -> p (a j) c", j=SJ))\
                    .then_inc(ld_ctx, 16)
            sp.wait_ge(s_qcur, 2 * B)
            sp.dma_start(win[:], W_in.rearrange("(k p) n -> p k n", p=P)).then_inc(ld_mam, 16)
            sp.dma_start(wout[:], W_out.rearrange("(k p) n -> p k n", p=P)).then_inc(ld_mam, 16)
            sp.wait_ge(m_pad, 1)
            for first in (0, 64):
                sp.dma_start(wxp[:, :, first:first + NX], x_proj_w.rearrange("(k p) n -> p k n", p=P))\
                    .then_inc(ld_mam, 16)
            sp.dma_start(convw[:], conv_w.rearrange("(k p) n -> p k n", p=P)).then_inc(ld_mam, 16)
            with nc.allow_non_contiguous_dma(reason="four short vectors"):
                for i, v in enumerate((conv_b, dt_w, dt_b, D_skip)):
                    sp.dma_start(dvec[:, i, :], v.rearrange("(k p) -> p k", p=P)).then_inc(ld_mam, 16)
            sp.dma_start(a_neg[:], A_log.rearrange("(k p) n -> p k n", p=P)).then_inc(ld_mam, 16)
            with nc.allow_non_contiguous_dma(reason="two short vectors"):
                for i, v in enumerate((norm_w, norm_b)):
                    sp.dma_start(nwb[:, i, :], v.rearrange("(k p) -> p k", p=P)).then_inc(ld_mam, 16)
            with nc.allow_non_contiguous_dma(reason="a short table"):
                sp.dma_start(idx_rows[:, 0, :].bitcast(I32).rearrange("p (j e) -> p j e", e=E),
                             top_idx.rearrange("(j p) e -> p j e", p=P)).then_inc(ld_idx, 16)

            def load_expert(e, i):
                sp.dma_start(w1[i][:], W1[ds(e, 1)].rearrange("a (k p) n -> p (a k) n", p=P)).then_inc(ld_e[i], 16)
                sp.dma_start(w2[i][:], W2[ds(e, 1)].rearrange("a (k p) n -> p (a k) n", p=P)).then_inc(ld_e[i], 16)

            sp.wait_ge(s_woe, B // 2)
            sp.dma_start(comb[:], combine_w[0:T, :].rearrange("(t p) e -> p t e", p=P)).then_inc(ld_comb, 16)
            sp.dma_start(b1_rows[:], b1.rearrange("e (f p) -> (e f) p", p=P)).then_inc(ld_comb, 16)
            sp.wait_ge(r_cnt, 1)
            sp.dma_start(b2_sb[:], b2).then_inc(ld_b2, 16)
            sp.wait_ge(m_conv, DT)
            sp.wait_ge(m_xz, 2 * DT)
            load_expert(0, 0)
            sp.wait_ge(m_scan, NS)
            load_expert(1, 1)
            load_expert(2, 2)
            sp.wait_ge(m_rd, NS)
            load_expert(3, 3)
            for e in range(RING, E):
                sp.wait_ge(f_o, e - RING + 1)
                load_expert(e, e % RING)

            def more_loads(r):
                for e in range(E):
                    sp.wait_ge(f_o, E * r + e - RING + 1)
                    load_expert(e, e % RING)

            further_rounds(sp, more_loads)
            for t in range(TT):
                sp.wait_ge(f_done, t + 1)
                sp.dma_start(out.rearrange("(t b) l c -> t (b l) c", b=BP)[t], res_nat[:, t, :]).then_inc(ld_out, 16)
            sp.wait_ge(ld_out, 16 * TT)

        @block.gpsimd
        def _(pool):
            done = [0]

            def link(ins):
                done[0] += 1
                ins.then_inc(s_pool, 1)
                pool.wait_ge(s_pool, done[0])

            link(pool.memset(ident[:], 0.0))
            link(pool.memset(q_cur[:], 0.0))
            pool.affine_select(out=ident[:], in_=ident[:], compare_op=ALU.not_equal, fill=1.0, base=0,
                               pattern=[[-1, P]], channel_multiplier=1).then_inc(s_id, 1)
            link(pool.memset(mhalf[:], -0.5))
            pool.wait_ge(s_pstat, 1)
            link(pool.tensor_scalar(lvar[:], lmv[:, :, 1], 1.0 + EPS, EPS * EPS, ALU.mult, ALU.add))
            link(pool.tensor_tensor(lscale[:], lvar[:], mhalf[:, 0:TT], ALU.pow))
            link(pool.tensor_tensor(lnm[:], lmv[:, :, 0], lscale[:], ALU.mult))
            pool.tensor_scalar(lshift[:], lnm[:], -1.0, 0.0, ALU.mult, ALU.add).then_inc(s_psc, 1)

            def queries(b):
                pool.wait_ge(s_misc, MISC * (b - 1) + 4)
                apart(pool)
                pool.wait_ge(s_lcur, 3 * b)
                apart(pool)
                for h in range(2):
                    rows = slice(h * DH, (h + 1) * DH)
                    pool.tensor_copy(q_cur[rows, :, h, :], q_t[rows, :, ds(b * L, L)]).then_inc(s_qcur, 1)
                    pool.wait_ge(s_qcur, 2 * b + h + 1)

            def latents(b, slot):
                rows = half(slot)
                flat = x_lat[:].rearrange("p t c -> p (t c)")
                pool.wait_ge(s_klo, b + 1)
                apart(pool)
                pool.tensor_copy(lat_cur[rows], flat[rows, ds((b - slot) * (C // BP), C)]).then_inc(s_lcur, 1)
                pool.wait_ge(s_lcur, 3 * b + 1)
                apart(pool)
                pool.tensor_scalar(cur_hi[rows], lat_cur[rows], 1.0, 0.0, ALU.mult, ALU.add).then_inc(s_lcur, 1)
                pool.wait_ge(s_lcur, 3 * b + 2)
                pool.tensor_tensor(cur_lo[rows], lat_cur[rows], cur_hi[rows].bitcast(F32), ALU.subtract)\
                    .then_inc(s_lcur, 1)

            def context(b, slot):
                pool.wait_ge(s_cmv, b + 1)
                apart(pool)
                pool.tensor_scalar(cvar[:], cmv[:, :, 1], 1.0, EPS, ALU.mult, ALU.add).then_inc(s_cvar, 1)
                pool.wait_ge(s_cvar, b + 1)
                pool.tensor_tensor(crstd[:], cvar[:], mhalf[:], ALU.pow).then_inc(s_crs, 1)
                pool.wait_ge(s_crs, b + 1)
                pool.tensor_tensor(cnm[:], cmv[:, :, 0], crstd[:], ALU.mult).then_inc(s_cnm, 1)
                pool.wait_ge(s_cnm, b + 1)
                apart(pool)
                pool.tensor_scalar(cshift[:], cnm[:], -1.0, 0.0, ALU.mult, ALU.add).then_inc(s_csh, 1)
                pool.wait_ge(s_cz, b + 1)
                if isinstance(b, int) and b == 0:
                    pool.wait_ge(ld_vec, 32)
                shape = (P, SJ // 2, C)
                for h in range(2):
                    rows = ctx_nat[:, h * SJ // 2:(h + 1) * SJ // 2, :]
                    pool.tensor_tensor(rows, rows, ln1wb[:, 0:1, :].to_broadcast(shape), ALU.mult).then_inc(s_cw, 1)
                    pool.wait_ge(s_cw, 2 * b + h + 1)
                    pool.tensor_tensor(rows, rows, ln1wb[:, 1:2, :].to_broadcast(shape), ALU.add).then_inc(s_cn, 1)
                pool.wait_ge(s_cn, 2 * b + 2)
                if not (isinstance(b, int) and b < 2):
                    pool.wait_ge(s_pv, HP * (b - 1))
                apart(pool)
                pool.tensor_scalar(kvn_hi[slot][:], ctx_nat[:], 1.0, 0.0, ALU.mult, ALU.add).then_inc(s_khi, 1)
                pool.wait_ge(s_khi, b + 1)
                pool.tensor_tensor(kvn_lo[slot][:], ctx_nat[:], kvn_hi[slot][:].bitcast(F32), ALU.subtract)\
                    .then_inc(s_klo, 1)

            context(0, 0)
            pool.wait_ge(s_pln, 1)
            latents(0, 0)
            pool.wait_ge(s_misc, MISC)

            def body(b, slot, more, pair):
                if more:
                    queries(b + 1)
                    context(b + 1, 1 - slot)
                    latents(b + 1, 1 - slot)
                    pool.wait_ge(s_lcur, 3 * (b + 2))

            all_steps(pool, body, lambda b, slot, pair: None)

            link(pool.memset(wxp[:, :, NX:64], 0.0))
            pool.sem_inc(m_pad, 1)
            pool.wait_ge(s_woe, B // 2)
            link(pool.memset(thalf[:], -0.5))
            pool.memset(xpad[:, :, :, 0:TAPS - 1], 0.0).then_inc(m_pad, 1)
            pool.tensor_tensor(pair_r[:], ident[0:NR, 0:NX], ident[0:NR, 64:NR], ALU.add).then_inc(m_sel, 1)
            pool.wait_ge(m_stat, 1)
            link(pool.tensor_scalar(tvar2[:], tmv[:, :, 1], 1.0 + EPS, EPS * EPS, ALU.mult, ALU.add))
            pool.tensor_tensor(trstd2[:], tvar2[:], thalf[:], ALU.pow).then_inc(m_rs, 1)
            link(pool.tensor_scalar(tvar[:], tmv[:, :, 1], 1.0, EPS, ALU.mult, ALU.add))
            pool.tensor_tensor(trstd[:], tvar[:], thalf[:], ALU.pow).then_inc(m_rs, 1)
            link(pool.memset(ones[:], 1.0))
            link(pool.affine_select(out=upto_ones[:], in_=ones[:], compare_op=ALU.is_ge, fill=0.0, base=0,
                                    pattern=[[1, P]], channel_multiplier=-1))
            link(pool.iota(iota_i[:], pattern=[[1, P]], base=0, channel_multiplier=0))
            link(pool.tensor_copy(iota_f[:], iota_i[:]))
            pool.sem_inc(r_tab, 1)
            pool.wait_ge(r_pos, 2)
            link(pool.tensor_scalar(coef_hl[:, :, :, 0], coef[:], 1.0, 0.0, ALU.mult, ALU.add))
            pool.tensor_tensor(coef_hl[:, :, :, 1], coef[:], coef_hl[:, :, :, 0].bitcast(F32), ALU.subtract)\
                .then_inc(f_hl, 1)
            for n in range(NS):
                i = n % 2
                if n > 0:
                    pool.wait_ge(m_bs, n + 1)
                    if n == 1:
                        pool.wait_ge(m_dtx, DT)
                    else:
                        pool.wait_ge(m_scan, n - 1)
                    pool.tensor_tensor(drive[i][:], dtx[:], bmat[i][:].unsqueeze(1).to_broadcast((P, DT, T)),
                                       ALU.mult).then_inc(m_drv, 1)
                pool.wait_ge(m_dec, n + 1)
                pool.memset(dec[i][:].rearrange("p a (b l) -> p (a b) l", l=L)[:, :, 0:1], 0.0).then_inc(m_z0, 1)
            pool.wait_ge(m_res, 1)
            pool.tensor_tensor(x1[:], x1[:], mres[:], ALU.add).then_inc(m_x1m, 1)
            pool.wait_ge(m_out, TT)
            link(pool.memset(fhalf[:], -0.5))
            pool.wait_ge(f_stat, 1)
            link(pool.tensor_scalar(fvar[:], fmv[:, :, 1], 1.0, EPS, ALU.mult, ALU.add))
            pool.tensor_tensor(frstd[:], fvar[:], fhalf[:], ALU.pow).then_inc(f_rs, 1)

        @block.vector
        def _(dve):
            done = [0]

            def link(ins):
                done[0] += 1
                ins.then_inc(s_dve, 1)
                dve.wait_ge(s_dve, done[0])

            def stats(src, st, mv, j_n):
                for j in range(j_n):
                    last = dve.bn_stats(st[:, j, :], src[:, j, :])
                link(last)
                for j in range(j_n):
                    last = dve.bn_aggr(mv[:, j, :], st[:, j, :])
                return last

            def ctx_stats(b, part):
                if part == 0:
                    dve.wait_ge(ld_ctx, 16 * (b + 1))
                for j in range(part * SJ // 2, (part + 1) * SJ // 2):
                    last = dve.bn_stats(cstat[:, j, :], ctx_nat[:, j, :])
                if part == 1:
                    last.then_inc(s_cst, 1)
                    dve.wait_ge(s_cst, b + 1)
                    apart(dve)
                    for j in range(SJ):
                        last = dve.bn_aggr(cmv[:, j, :], cstat[:, j, :])
                    last.then_inc(s_cmv, 1)

            def misc_lo(b, slot, m, turn=None, where=MB):
                dve.wait_ge(s_mhi, misc_count(b, m if turn is None else turn))
                dve.tensor_tensor(misc_dst(slot, m, False), where,
                                  misc_dst(slot, m, True).bitcast(F32), ALU.subtract).then_inc(s_mlo, 1)

            def ctx_scale(b):
                dve.wait_ge(s_csh, b + 1)
                for j in range(SJ):
                    last = dve.tensor_scalar(ctx_nat[:, j, :], ctx_nat[:, j, :], crstd[:, j:j + 1],
                                             cshift[:, j:j + 1], ALU.mult, ALU.add)
                last.then_inc(s_cz, 1)

            dve.wait_ge(ld_xlat, 16)
            stats(x_lat, lstat, lmv, TT).then_inc(s_pstat, 1)
            dve.wait_ge(s_psc, 1)
            for t in range(TT):
                last = dve.tensor_scalar(x_lat[:, t, :], x_lat[:, t, :], lscale[:, t:t + 1], lshift[:, t:t + 1],
                                         ALU.mult, ALU.add)
            link(last)
            dve.wait_ge(ld_vec2, 32)
            link(dve.tensor_tensor(x_lat[:], x_lat[:], ln2wb[:, 0:1, :].to_broadcast((P, TT, C)), ALU.mult))
            dve.tensor_tensor(x_lat[:], x_lat[:], ln2wb[:, 1:2, :].to_broadcast((P, TT, C)), ALU.add)\
                .then_inc(s_pln, 1)
            ctx_stats(0, 0)
            ctx_stats(0, 1)
            ctx_scale(0)
            dve.wait_ge(s_pevac, 2)
            dve.tensor_tensor(latt_lo[:], TWO, latt_hi[:].bitcast(F32), ALU.subtract).then_inc(s_plo, 1)
            for n, (m, bank) in enumerate(first_groups):
                misc_lo(0, 0, m, n, psum[:, bank, :])

            def tail_lo(part, now):
                b, slot, hp = now
                u = hp % 2
                high, low, where, t0, t1 = {"A": (s_hA, s_lA, TP[0], 0, 4), "B": (s_hB, s_lB, TP[1], 4, 8),
                                            "C": (s_hC, s_lC, TP[0], 8, 9)}[part]
                dve.wait_ge(high, count(b, hp))
                rows = slice(0, P) if part != "C" else half(slot)
                dve.tensor_tensor(pt_lo[u][rows, t0:t1, :],
                                  where[rows, 0:(t1 - t0) * P].rearrange("p (t m) -> p t m", m=P),
                                  pt_hi[u][rows, t0:t1, :].bitcast(F32), ALU.subtract).then_inc(low, 1)

            def step(b, slot, hp, live, more, pair):
                p1, p3 = back(b, slot, hp, 1), back(b, slot, hp, 3)
                if live:
                    dve.wait_ge(s_lg, count(b, hp))
                    dve.tensor_reduce(rowmax[slot][:, hp, 0:1], LG_A, XY, ALU.max)
                    dve.tensor_reduce(rowmax[slot][:, hp, 1:2], LG_B, X, ALU.max).then_inc(s_mx, 1)
                    dve.wait_ge(s_mx, count(b, hp))
                    apart(dve)
                    dve.tensor_scalar(nbias[slot][:, hp:hp + 1], rowmax[slot][:, hp, 0:1], rowmax[slot][:, hp, 1:2],
                                      -SCALE, ALU.max, ALU.mult).then_inc(s_nb, 1)
                if p1:
                    tail_lo("A", p1)
                    tail_lo("B", p1)
                    b1_, sl1, hp1 = p1
                    dve.wait_ge(s_exp, count(b1_, hp1))
                    dve.tensor_tensor(den[sl1][:, hp1:hp1 + 1], den_part[sl1][:, hp1, 0:1],
                                      den_part[sl1][:, hp1, 1:2], ALU.add).then_inc(s_den, 1)
                    dve.wait_ge(s_den, count(b1_, hp1))
                    dve.reciprocal(rden[sl1][:, hp1:hp1 + 1], den[sl1][:, hp1:hp1 + 1]).then_inc(s_rd, 1)
                if p3:
                    dve.wait_ge(s_yt, count(p3[0], p3[2]))
                    dve.tensor_copy(y_t[:], OC[:, 0:C].rearrange("p (k m) -> p k m", k=CK)).then_inc(s_yte, 1)
                if slot == 0 and hp == 3 and pair is not None:
                    dve.wait_ge(s_wo, pair + 1)
                    dve.tensor_tensor(x1[:, ds(pair, 1), :], x1[:, ds(pair, 1), :], MB[:, 0:C].unsqueeze(1),
                                      ALU.add).then_inc(s_woe, 1)
                if more and hp == MISC - 1:
                    misc_lo(b + 1, 1 - slot, hp)
                if p1:
                    tail_lo("C", p1)
                if more and hp < MISC - 1:
                    if hp < 2:
                        ctx_stats(b + 1, hp)
                    misc_lo(b + 1, 1 - slot, hp)
                    if hp == 2:
                        ctx_scale(b + 1)

            def body(b, slot, more, pair):
                for hp in range(HP):
                    step(b, slot, hp, True, more, pair)

            def drain(b, slot, pair):
                step(b, slot, 0, False, False, pair)
                for hp in (1, 2, 3):
                    p3 = back(b, slot, hp, 3)
                    if p3[0] is not b:
                        dve.wait_ge(s_yt, count(p3[0], p3[2]))
                        dve.tensor_copy(y_t[:], OC[:, 0:C].rearrange("p (k m) -> p k m", k=CK)).then_inc(s_yte, 1)
                    if hp == 3:
                        dve.wait_ge(s_wo, pair + 1)
                        dve.tensor_tensor(x1[:, ds(pair, 1), :], x1[:, ds(pair, 1), :], MB[:, 0:C].unsqueeze(1),
                                          ALU.add).then_inc(s_woe, 1)

            dve.wait_ge(ld_wvo, 48)
            all_steps(dve, body, drain)

            dve.wait_ge(ld_idx, 16)
            index = idx_rows[:].bitcast(I32)
            dve.tensor_scalar(index[:, 1, :], index[:, 0, :], P - 1, None, ALU.bitwise_and)
            link(dve.tensor_scalar(index[:, 2, :], index[:, 0, :], P.bit_length() - 1, None, ALU.arith_shift_right))
            dve.wait_ge(s_woe, B // 2)
            dve.tensor_copy(place_f[:], index[:, 1, :])
            dve.tensor_copy(tile_f[:], index[:, 2, :]).then_inc(r_idx, 1)
            stats(x1, tstat, tmv, TT).then_inc(m_stat, 1)
            dve.wait_ge(m_rs, 1)
            for t in range(TT):
                dve.tensor_scalar(xn[:, t, :], x1[:, t, :], tmv[:, t, 0:1], trstd2[:, t:t + 1],
                                  ALU.subtract, ALU.mult).then_inc(m_ln, 1)
            dve.wait_ge(ld_mam, 16 * 12)
            dve.wait_ge(m_xt, 1)
            dve.tensor_scalar(xn_t[:, 0, :], psum[:, 0, :], nwb[:, 0, 0:1], nwb[:, 1, 0:1], ALU.mult, ALU.add)\
                .then_inc(m_xte, 1)
            dve.wait_ge(m_rs, 2)
            for t in range(TT):
                last = dve.tensor_scalar(mres[:, t, :], x1[:, t, :], tmv[:, t, 0:1], trstd[:, t:t + 1],
                                         ALU.subtract, ALU.mult)
            last.then_inc(m_res, 1)
            dve.wait_ge(r_tab, 1)
            dve.wait_ge(r_idx, 1)
            dve.tensor_tensor(onetile[:], iota_f[:, 0:TT].unsqueeze(1).to_broadcast((P, SC * E, TT)),
                              tile_f[:].unsqueeze(2).to_broadcast((P, SC * E, TT)), ALU.is_equal)
            dve.tensor_tensor(onehot[:], iota_f[:].unsqueeze(1).to_broadcast((P, SC * E, P)),
                              place_f[:].unsqueeze(2).to_broadcast((P, SC * E, P)), ALU.is_equal).then_inc(r_oh, 1)
            for d in range(DT):
                dve.wait_ge(m_tap, d + 1)
                o = conv[:, d, :].rearrange("p (b l) -> p b l", l=L)
                for k in range(1, TAPS):
                    ins = dve.scalar_tensor_tensor(out=o, in0=xpad[:, d, :, k:k + L], scalar=convw[:, d, k:k + 1],
                                                   in1=o, op0=ALU.mult, op1=ALU.add)
                    if k < TAPS - 1:
                        link(ins)
                ins.then_inc(m_conv, 1)
            dve.wait_ge(r_cnt, 1)
            counts = psum[:, 7, 0:TT * E].rearrange("p (e t) -> p t e", t=TT)
            dve.tensor_scalar(valid[:], counts, 1.0, None, ALU.min).then_inc(r_val, 1)
            dve.wait_ge(ld_comb, 32)
            dve.tensor_tensor(coef[:], counts, comb[:], ALU.mult).then_inc(r_val, 1)
            def picks(r):
                if not isinstance(r, int):
                    dve.wait_ge(f_cs, r)
                    dve.wait_ge(f_gat, EG * CK * r)
                    apart(dve)
                    dve.tensor_scalar(slot_of[:], slot_of[:], -float(P), None, ALU.add).then_inc(f_shift, 1)
                    dve.wait_ge(f_shift, r)
                    apart(dve)
                dve.tensor_tensor(pick[:].rearrange("p t e s -> p (t e) s"),
                                  iota_f[:].unsqueeze(1).to_broadcast((P, TT * E, P)),
                                  slot_of[:].rearrange("p t e -> p (t e)").unsqueeze(2).to_broadcast((P, TT * E, P)),
                                  ALU.is_equal).then_inc(f_pick, 1)

            dve.wait_ge(m_dhi, 1)
            dve.tensor_tensor(dbc[64:NR, :], psum[64:NR, 2, :], dbc[64:NR, :].bitcast(F32), ALU.subtract)\
                .then_inc(m_dlo, 1)
            dve.wait_ge(r_pre, 1)
            link(dve.tensor_tensor(slot_of[:], psum[:, 7, 64:64 + TT * E].rearrange("p (t e) -> p t e", e=E),
                                   valid[:], ALU.mult))
            dve.tensor_scalar(slot_of[:], slot_of[:], 1.0, None, ALU.subtract).then_inc(r_pos, 1)
            link(dve.tensor_reduce(most[:], psum[:, 7, 128:128 + E], X, ALU.max))
            dve.tensor_copy(most_i[:], most[:]).then_inc(r_pos, 1)
            dve.wait_ge(r_pos, 2)
            picks(0)
            dve.wait_ge(m_dt0, 1)
            for d in range(DT):
                last = dve.tensor_scalar(state[0][:, d, :], psum[:, 5, :], dvec[:, 1, d:d + 1], dvec[:, 2, d:d + 1],
                                         ALU.mult, ALU.add)
            last.then_inc(m_dtu, 1)
            dve.wait_ge(m_dtu, 1)
            for d in range(DT):
                dve.wait_ge(m_dta, d + 1)
                dve.scalar_tensor_tensor(out=dts[:, d, :], in0=state[0][:, d, :], scalar=0.0, in1=read[1][:, d, :],
                                         op0=ALU.max, op1=ALU.add).then_inc(m_dts, 1)
                dve.wait_ge(m_dts, d + 1)
                dve.tensor_tensor(dtx[:, d, :], dts[:, d, :], xc[:, d, :], ALU.mult).then_inc(m_dtx, 1)
            dve.wait_ge(m_dtx, DT)
            dve.wait_ge(m_bs, 1)
            dve.tensor_tensor(drive[0][:], dtx[:], bmat[0][:].unsqueeze(1).to_broadcast((P, DT, T)), ALU.mult)\
                .then_inc(m_drv0, 1)
            for n in range(NS):
                i = n % 2
                dve.wait_ge(m_z0, n + 1)
                if n == 0:
                    dve.wait_ge(m_drv0, 1)
                else:
                    dve.wait_ge(m_drv, n)
                flat = "p a b -> p (a b)"
                dve.tensor_tensor_scan(state[i][:].rearrange(flat), dec[i][:].rearrange(flat),
                                       drive[i][:].rearrange(flat), 0.0, ALU.mult, ALU.add).then_inc(m_scan, 1)
                dve.wait_ge(m_scan, n + 1)
                dve.wait_ge(m_c, n + 1)
                if n >= 2:
                    dve.wait_ge(m_acc, n - 1)
                dve.tensor_tensor(read[i][:], state[i][:], psum[:, 5 + i:6 + i, :].to_broadcast((P, DT, T)),
                                  ALU.mult).then_inc(m_rd, 1)
            dve.wait_ge(m_zs, 1)
            for d in range(DT):
                dve.wait_ge(m_acc, NS + d)
                link(dve.scalar_tensor_tensor(out=conv[:, d, :], in0=xc[:, d, :], scalar=dvec[:, 3, d:d + 1],
                                              in1=psum[:, d, :], op0=ALU.mult, op1=ALU.add))
                dve.tensor_tensor(conv[:, d, :], conv[:, d, :], zs[:, d, :], ALU.mult).then_inc(m_y, 1)
            dve.wait_ge(m_x1m, 1)
            for t in range(TT):
                dve.wait_ge(m_yo, t + 1)
                dve.tensor_tensor(x1[:, t, :], x1[:, t, :], psum[:, 4 + t, 0:C], ALU.add).then_inc(m_out, 1)

            for t in range(TT):
                dve.wait_ge(m_out, t + 1)
                dve.bn_stats(fstat[:, t, :], x1[:, t, :]).then_inc(f_bn, 1)
            for t in range(TT):
                dve.wait_ge(f_bn, t + 1)
                last = dve.bn_aggr(fmv[:, t, :], fstat[:, t, :])
            last.then_inc(f_stat, 1)
            dve.wait_ge(f_rs, 1)
            for t in range(TT):
                last = dve.tensor_scalar(f_nat[:, t, :], x1[:, t, :], fmv[:, t, 0:1], frstd[:, t:t + 1],
                                         ALU.subtract, ALU.mult)
                last.then_inc(f_ln, 1)
            for t in range(TT):
                dve.wait_ge(f_hi_done, t + 1)
                dve.tensor_tensor(f_lo[:, t, :], f_nat[:, t, :], f_hi[:, t, :].bitcast(F32), ALU.subtract)\
                    .then_inc(f_lo_done, 1)
            def expert_round(r):
                dve.wait_ge(f_cs, r + 1)
                apart(dve)
                dve.tensor_reduce(coef_slot[:], psum[:, 4, 0:2 * E].rearrange("p (e h) -> p e h", h=2), X, ALU.add)\
                    .then_inc(f_cse, 1)
                dve.wait_ge(f_cse, r + 1)
                apart(dve)
                with dve.Fori(0, EG) as q:
                    for i in range(RING):
                        e = E * r + RING * q + i
                        dve.wait_ge(f_o, e + 1)
                        dve.tensor_scalar(o_s[:], psum[:, 4 + i % 2, 0:C], coef_slot[:, ds(RING * q + i, 1)], None,
                                          ALU.mult).then_inc(f_os, 1)
                        dve.wait_ge(f_oh, e + 1)
                        dve.tensor_tensor(o_lo[:], o_s[:], o_hi[:].bitcast(F32), ALU.subtract).then_inc(f_ol, 1)
                    dve.wait_ge(f_sc, EG * r + q + 1)
                    for k in range(CK):
                        dve.tensor_tensor(acc_t[:, k, :], acc_t[:, k, :], psum[:, 6 + k, :], ALU.add)\
                            .then_inc(f_sce, 1)
                    dve.wait_ge(f_sce, CK * (EG * r + q + 2))

            dve.wait_ge(f_b2e, CK)
            dve.sem_inc(f_sce, CK)
            expert_round(0)

            def next_round(r):
                picks(r)
                expert_round(r)

            further_rounds(dve, next_round)
            dve.sem_inc(f_all, ROUNDS)
            for t in range(TT):
                dve.wait_ge(f_fin, t + 1)
                dve.tensor_tensor(res_nat[:, t, :], x1[:, t, :], psum[:, t, 0:C], ALU.add).then_inc(f_done, 1)

        @block.scalar
        def _(act):
            for g in range(HP // 2):
                act.wait_ge(s_pwk, g + 1)
                act.activation(wk_t[:, 2 * g:2 * g + 2, :], TP[g % 2].rearrange("p (a c) -> p a c", c=C), ACT.Copy)\
                    .then_inc(s_pwke, 1)
            act.wait_ge(s_platt, 1)
            act.activation(latt[:], TWO, ACT.Copy).then_inc(s_pevac, 1)
            act.activation(latt_hi[:], TWO, ACT.Copy).then_inc(s_pevac, 1)
            for t in range(HP):
                act.wait_ge(s_pq, t + 1)
                act.activation(q_t[:, t, :], psum[:, 5 + t % 2, :], ACT.Copy).then_inc(s_pqe, 1)
            act.wait_ge(s_pqe, HP)
            act.wait_ge(s_id, 1)
            for h in range(2):
                rows = slice(h * DH, (h + 1) * DH)
                act.activation(q_cur[rows, :, h, :], q_t[rows, :, 0:L], ACT.Copy).then_inc(s_qcur, 1)

            def misc_hi(b, slot, m, turn=None, where=MB):
                act.wait_ge(s_misc, misc_count(b, m if turn is None else turn))
                act.activation(misc_dst(slot, m, True), where, ACT.Copy).then_inc(s_mhi, 1)

            def own_rows(b, slot):
                for src, dst in ((latt_hi, kvt_hi), (latt_lo, kvt_lo)):
                    act.activation(dst[slot][:, :, S:], src[:, :, ds(b * L, L)].bitcast(F32), ACT.Copy)\
                        .then_inc(s_own, 1)

            for n, (m, bank) in enumerate(first_groups):
                misc_hi(0, 0, m, n, psum[:, bank, :])
            act.wait_ge(s_pevac, 2)
            act.wait_ge(s_plo, 1)
            own_rows(0, 0)

            def tail_hi(part, now):
                b, slot, hp = now
                u = hp % 2
                turned, high, where, t0, t1 = {"A": (s_tA, s_hA, TP[0], 0, 4), "B": (s_tB, s_hB, TP[1], 4, 8),
                                               "C": (s_tC, s_hC, TP[0], 8, 9)}[part]
                act.wait_ge(turned, count(b, hp))
                rows = slice(0, P) if part != "C" else half(slot)
                act.activation(pt_hi[u][rows, t0:t1, :],
                               where[rows, 0:(t1 - t0) * P].rearrange("p (t m) -> p t m", m=P), ACT.Copy)\
                    .then_inc(high, 1)

            def mean_value(now):
                b, slot, hp = now
                act.wait_ge(s_pv, count(b, hp))
                act.wait_ge(s_rd, count(b, hp))
                before = back(b, slot, hp, 1)
                if before:
                    act.wait_ge(s_yt, count(before[0], before[2]))
                act.activation(y_n[:], PV, ACT.Copy, scale=rden[slot][:, hp:hp + 1]).then_inc(s_y, 1)

            def keep_out(now, pair):
                b, slot, hp = now
                act.wait_ge(s_o, count(b, hp))
                if slot == 0 and pair is not None:
                    act.wait_ge(s_wo, pair + 1)
                act.activation(o_t[:, hp, slot * L:(slot + 1) * L], OC[:, C:C + L], ACT.Copy).then_inc(s_oe, 1)

            def step(b, slot, hp, live, more, pair):
                p1, p2, p3 = (back(b, slot, hp, n) for n in (1, 2, 3))
                if p3:
                    mean_value(p3)
                if p1:
                    if p3:
                        act.wait_ge(s_pv, count(p3[0], p3[2]))
                    tail_hi("A", p1)
                    tail_hi("B", p1)
                if live:
                    act.wait_ge(s_nb, count(b, hp))
                    if p2:
                        act.wait_ge(s_tC, count(p2[0], p2[2]))
                    act.activation(prob[hp % 2][:, 0:2 * CUT].rearrange("p (a n) -> p a n", n=CUT), LG_A, ACT.Exp,
                                   bias=nbias[slot][:, hp:hp + 1], scale=SCALE,
                                   accum_out=den_part[slot][:, hp, 0:1])
                    act.activation(prob[hp % 2][:, 2 * CUT:], LG_B, ACT.Exp, bias=nbias[slot][:, hp:hp + 1],
                                   scale=SCALE, accum_out=den_part[slot][:, hp, 1:2]).then_inc(s_exp, 1)
                if more and hp == MISC - 1:
                    misc_hi(b + 1, 1 - slot, hp)
                    own_rows(b + 1, 1 - slot)
                if p1:
                    tail_hi("C", p1)
                if p3:
                    keep_out(p3, pair if hp >= 3 else None)
                if more and hp < MISC - 1:
                    misc_hi(b + 1, 1 - slot, hp)

            def body(b, slot, more, pair):
                for hp in range(HP):
                    step(b, slot, hp, True, more, pair)

            def drain(b, slot, pair):
                step(b, slot, 0, False, False, None)
                for hp in (1, 2):
                    p3 = back(b, slot, hp, 3)
                    mean_value(p3)
                    keep_out(p3, None)

            all_steps(act, body, drain)

            act.wait_ge(ld_mam, 16 * 12)
            act.activation(a_neg[:], a_neg[:], ACT.Exp).then_inc(m_aneg, 1)
            act.wait_ge(m_aneg, 1)
            act.activation(a_neg[:], a_neg[:], ACT.Copy, scale=-1.0).then_inc(m_aneg, 1)
            act.wait_ge(m_xt, 2)
            act.activation(xn_t[:, 1, :], psum[:, 1, :], ACT.Identity, scale=nwb[:, 0, 1:2], bias=nwb[:, 1, 1:2])\
                .then_inc(m_xte, 1)
            act.wait_ge(m_pad, 2)
            for d in range(DT):
                act.wait_ge(m_xz, d + 1)
                act.activation(xpad[:, d, :, TAPS - 1:], psum[:, XB[d % 4], :].rearrange("p (b l) -> p b l", l=L),
                               ACT.Copy).then_inc(m_xze, 1)
                act.wait_ge(m_xze, d + 1)
                act.activation(conv[:, d, :].rearrange("p (b l) -> p b l", l=L), xpad[:, d, :, 0:L], ACT.Identity,
                               scale=convw[:, d, 0:1], bias=dvec[:, 0, d:d + 1]).then_inc(m_tap, 1)

            for d in range(DT):
                act.wait_ge(m_conv, d + 1)
                act.activation(xc[:, d, :], conv[:, d, :], ACT.Silu).then_inc(m_xc, 1)
            act.wait_ge(r_b1, 1)
            act.activation(b1_t[:], psum[:, 5, 0:E * FT], ACT.Copy).then_inc(r_b1e, 1)
            act.wait_ge(m_dbc, 1)
            act.activation(dbc[:], psum[0:NR, 2, :], ACT.Copy).then_inc(m_dhi, 1)
            act.activation(warm_out[:], a_neg[:, 0, 0:1], ACT.Exp)
            act.wait_ge(m_dt0, 2)
            for d in range(DT):
                act.activation(read[0][:, d, :], psum[:, 2, :], ACT.Abs, scale=dvec[:, 1, d:d + 1],
                               bias=dvec[:, 2, d:d + 1]).then_inc(s_act, 1)
            for d in range(DT):
                act.wait_ge(s_act, d + 1)
                act.activation(read[0][:, d, :], read[0][:, d, :], ACT.Exp, scale=-1.0).then_inc(s_act, 1)
            for d in range(DT):
                act.wait_ge(s_act, DT + d + 1)
                act.activation(read[1][:, d, :], read[0][:, d, :], ACT.Ln, bias=1.0).then_inc(m_dta, 1)

            def b_row(n):
                act.wait_ge(m_b, n + 1)
                if n == 2:
                    act.wait_ge(m_drv0, 1)
                elif n > 2:
                    act.wait_ge(m_drv, n - 2)
                act.activation(bmat[n % 2][:], psum[:, 4, :], ACT.Copy).then_inc(m_bs, 1)

            act.activation(warm_out[:], a_neg[:, 0, 0:1], ACT.Exp)
            for n in range(2):
                b_row(n)
            for n in range(NS):
                i = n % 2
                if n >= 2:
                    act.wait_ge(m_scan, n - 1)
                for d in range(DT):
                    if n == 0:
                        act.wait_ge(m_dts, d + 1)
                    last = act.activation(dec[i][:, d, :], dts[:, d, :], ACT.Exp, scale=a_neg[:, d, n:n + 1])
                last.then_inc(m_dec, 1)
                if n == 1:
                    for d in range(DT):
                        act.wait_ge(m_xz, DT + d + 1)
                        act.activation(zs[:, d, :], psum[:, XB[d % 4], :], ACT.Copy).then_inc(m_xze, 1)
                job = n - 5
                if 0 <= job < E:
                    act.wait_ge(f_turn, job + 1)
                    act.activation(pick_t[:, job, :], psum[:, 7, :], ACT.Copy).then_inc(f_turned, 1)
                elif job == E:
                    act.wait_ge(f_ct, 1)
                    act.activation(coef_t[:], psum[0:E, 7, :], ACT.Copy).then_inc(f_cte, 1)
                elif job == E + 1:
                    act.wait_ge(f_b2, 1)
                    act.activation(acc_t[:, 0, :], psum[:, 7, :], ACT.Copy).then_inc(f_b2e, 1)
                elif job == E + 2:
                    act.wait_ge(f_b2, 2)
                    act.activation(acc_t[:, 1, :], psum[:, 7, :], ACT.Copy).then_inc(f_b2e, 1)
                if n + 2 < NS:
                    b_row(n + 2)
            act.wait_ge(m_xze, 2 * DT)
            act.activation(zs[:], zs[:], ACT.Silu).then_inc(m_zs, 1)

            def turned(r, side):
                for e in range(side * RING, (side + 1) * RING):
                    act.wait_ge(f_turn, E * r + e + 1)
                    act.activation(pick_t[:, e, :], psum[:, 4 + e % RING, :], ACT.Copy).then_inc(f_turned, 1)

            def expert_round(r):
                for g in range(EG):
                    for k in range(CK):
                        act.wait_ge(f_gat, CK * EG * r + CK * g + k + 1)
                        act.activation(xg_t[:, k, g * RING:(g + 1) * RING, :],
                                       psum[:, GB[g] + k, :].rearrange("p (e s) -> p e s", s=P), ACT.Copy)\
                            .then_inc(f_gate, 1)
                with act.Fori(0, EG) as q:
                    act.activation(warm_out[:], a_neg[:, 0, 0:1], ACT.Gelu_apprx_tanh)
                    for i in range(RING):
                        e = E * r + RING * q + i
                        for f in range(FT):
                            act.wait_ge(f_h, FT * e + f + 1)
                            act.activation(hid[:, f, :], psum[:, f % 4, 0:P], ACT.Gelu_apprx_tanh,
                                           bias=b1_t[:, ds(FT * (RING * q + i) + f, 1)]).then_inc(f_he, 1)
                        act.wait_ge(f_os, e + 1)
                        act.activation(o_hi[:], o_s[:], ACT.Copy).then_inc(f_oh, 1)

            for t in range(TT):
                act.wait_ge(f_ln, t + 1)
                act.activation(f_hi[:, t, :], f_nat[:, t, :], ACT.Copy).then_inc(f_hi_done, 1)
            expert_round(0)

            def next_round(r):
                turned(r, 0)
                turned(r, 1)
                expert_round(r)

            further_rounds(act, next_round)

        @block.tensor
        def _(pe):
            pe.wait_ge(s_id, 1)
            pe.wait_ge(ld_wk, 16)
            for g in range(HP // 2):
                if g >= 2:
                    pe.wait_ge(s_pwke, g - 1)
                for a in range(2):
                    for k in range(CK):
                        last = pe.transpose(TP[g % 2][:, (2 * a + k) * P:(2 * a + k + 1) * P],
                                            wk_nat[:, k, (2 * g + a) * P:(2 * g + a + 1) * P], ident[:])
                last.then_inc(s_pwk, 1)
            pe.wait_ge(s_pln, 1)
            for k in range(CK):
                for t in range(TT):
                    last = pe.transpose(psum[:, k, t * P:(t + 1) * P], x_lat[:, t, k * P:(k + 1) * P], ident[:])
            last.then_inc(s_platt, 1)
            pe.wait_ge(s_pevac, 1)
            pe.wait_ge(ld_wq, 16)
            for t in range(HP):
                if t >= 2:
                    pe.wait_ge(s_pqe, t - 1)
                for k in range(CK):
                    last = pe.matmul(psum[:, 5 + t % 2, :], wq_sb[:, k, t * P:(t + 1) * P], latt[:, k, :],
                                     start=(k == 0), stop=(k == CK - 1))
                last.then_inc(s_pq, 1)

            def misc(b, slot, m, after=None, where=MB):
                if after is not None:
                    pe.wait_ge(s_woe, after)
                if not (isinstance(b, int) and b == 0):
                    pe.wait_ge(s_mlo, misc_count(b, m) - 1)
                if m < 4:
                    k, a = m // 2, m % 2
                    if m == 0:
                        pe.wait_ge(s_qcur, 2 * b + 2)
                    for n in range(HP // 2):
                        hp = a * HP // 2 + n
                        last = pe.matmul(where[:, n * P:(n + 1) * P], wk_t[:, hp, k * P:(k + 1) * P],
                                         q_cur[:, hp].rearrange("p a l -> p (a l)"), start=True, stop=True)
                else:
                    h, k = m % 4 // 2, m % 2
                    if k == 0:
                        pe.wait_ge(s_cn, 2 * b + h + 1)
                    for j in range(4):
                        last = pe.transpose(where[:, j * P:(j + 1) * P], ctx_nat[:, 4 * h + j, k * P:(k + 1) * P],
                                            ident[:])
                last.then_inc(s_misc, 1)

            pe.wait_ge(s_pwke, HP // 2)
            for n, (m, bank) in enumerate(first_groups):
                if n == 2:
                    pe.wait_ge(s_plo, 1)
                if bank == 5:
                    pe.wait_ge(s_pqe, HP)
                misc(0, 0, m, where=psum[:, bank, :])

            def logits(b, slot, hp):
                for k in range(CK):
                    for q, x_ in ((qk_hi, kvt_hi), (qk_hi, kvt_lo), (qk_lo, kvt_hi)):
                        w = q[slot][:, k, hp].rearrange("p a l -> p (a l)")
                        first, final = k == 0 and q is qk_hi and x_ is kvt_hi, k == CK - 1 and q is qk_lo
                        for n in range(3):
                            x0, x1_ = n * CUT, min((n + 1) * CUT, S + L)
                            last = pe.matmul(psum[:, n, 0:x1_ - x0], w, x_[slot][:, k, x0:x1_],
                                             start=first, stop=final)
                last.then_inc(s_lg, 1)

            def turn(now, part):
                b, slot, hp = now
                if part == "C":
                    pe.wait_ge(s_lA, count(b, hp))
                    apart(pe)
                    if slot == 0:
                        last = pe.transpose(TP[0][0:L, 0:P], prob[hp % 2][:, S:S + L], ident[:])
                    else:
                        last = pe.matmul(TP[0][half(slot), 0:P], prob[hp % 2][:, S:S + L], ident[:],
                                         start=True, stop=True)
                    last.then_inc(s_tC, 1)
                    return
                before = back(b, slot, hp, 1)
                if before:
                    pe.wait_ge(s_lC, count(before[0], before[2]))
                for n, done in ((0, s_tA), (1, s_tB)):
                    for j in range(4):
                        last = pe.transpose(TP[n][:, j * P:(j + 1) * P],
                                            prob[hp % 2][:, (4 * n + j) * P:(4 * n + j + 1) * P], ident[:])
                    last.then_inc(done, 1)

            def times_rows(now):
                b, slot, hp = now
                pe.wait_ge(s_lC, count(b, hp))
                if hp == 0:
                    pe.wait_ge(s_klo, b + 1)
                    pe.wait_ge(s_lcur, 3 * b + 3)
                before = back(b, slot, hp, 1)
                if before:
                    pe.wait_ge(s_y, count(before[0], before[2]))
                u = hp % 2
                for j in range(SJ):
                    for w, x_ in ((pt_hi, kvn_hi), (pt_hi, kvn_lo), (pt_lo, kvn_hi)):
                        pe.matmul(PV, w[u][:, j, :], x_[slot][:, j, :],
                                  start=(j == 0 and w is pt_hi and x_ is kvn_hi), stop=False)
                rows = half(slot)
                for n, (w, x_) in enumerate(((pt_hi, cur_hi), (pt_hi, cur_lo), (pt_lo, cur_hi))):
                    last = pe.matmul(PV, w[u][rows, SJ, :], x_[rows], start=False, stop=(n == 2))
                last.then_inc(s_pv, 1)

            def turn_value(now):
                b, slot, hp = now
                pe.wait_ge(s_y, count(b, hp))
                before = back(b, slot, hp, 1)
                if before:
                    pe.wait_ge(s_oe, count(before[0], before[2]))
                for k in range(CK):
                    last = pe.transpose(OC[:, k * P:(k + 1) * P], y_n[:, k * P:(k + 1) * P], ident[:])
                last.then_inc(s_yt, 1)

            def head_out(now):
                b, slot, hp = now
                pe.wait_ge(s_yte, count(b, hp))
                for h in range(2):
                    for k in range(CK):
                        last = pe.matmul(OC[h * DH:(h + 1) * DH, C:C + L],
                                         wv[:, k, (2 * hp + h) * DH:(2 * hp + h + 1) * DH],
                                         y_t[:, k, h * L:(h + 1) * L], start=(k == 0), stop=(k == CK - 1))
                last.then_inc(s_o, 1)

            def out_proj(pair, seen, first=0, final=HP):
                pe.wait_ge(s_oe, HP * (2 * pair + 1) + final)
                pe.wait_ge(s_mlo, seen)
                for hp in range(first, final):
                    last = pe.matmul(MB[:, 0:C], o_t[:, hp, :], wo[:, hp, :], start=(hp == 0), stop=(hp == HP - 1))
                if final == HP:
                    last.then_inc(s_wo, 1)

            def step(b, slot, hp, live, more, pair):
                p1, p2, p3 = (back(b, slot, hp, n) for n in (1, 2, 3))
                if live:
                    if hp == 0:
                        pe.wait_ge(s_mlo, MISC * (b + 1))
                        pe.wait_ge(s_own, 2 * (b + 1))
                    if p1:
                        pe.wait_ge(s_exp, count(p1[0], p1[2]))
                    logits(b, slot, hp)
                if p1:
                    if not live:
                        pe.wait_ge(s_exp, count(p1[0], p1[2]))
                    turn(p1, "AB")
                if p3:
                    turn_value(p3)
                if slot == 0 and hp == 3 and pair is not None:
                    out_proj(pair, misc_count(b + 1, hp) - 1)
                if more and hp == MISC - 1:
                    misc(b + 1, 1 - slot, hp)
                if p2:
                    times_rows(p2)
                if p1:
                    turn(p1, "C")
                if p3:
                    head_out(p3)
                if more and hp < MISC - 1:
                    misc(b + 1, 1 - slot, hp, pair + 1 if slot == 0 and hp == 3 and pair is not None else None)

            def body(b, slot, more, pair):
                for hp in range(HP):
                    step(b, slot, hp, True, more, pair)

            def drain(b, slot, pair):
                step(b, slot, 0, False, False, None)
                turn_value(back(b, slot, 1, 3))
                times_rows(back(b, slot, 1, 2))
                head_out(back(b, slot, 1, 3))
                out_proj(pair, MISC * B, 0, HP - 2)
                turn_value(back(b, slot, 2, 3))
                head_out(back(b, slot, 2, 3))
                out_proj(pair, MISC * B, HP - 2, HP)

            pe.wait_ge(ld_wvo, 48)
            all_steps(pe, body, drain)

            for t in range(TT):
                pe.wait_ge(m_ln, t + 1)
                for k in range(CK):
                    last = pe.transpose(psum[:, k, t * P:(t + 1) * P], xn[:, t, k * P:(k + 1) * P], ident[:])
                    if t == TT - 1:
                        last.then_inc(m_xt, 1)
            pe.wait_ge(m_xte, 2)

            def in_proj(t):
                if t >= 4:
                    pe.wait_ge(m_xze, t - 3)
                for k in range(CK):
                    last = pe.matmul(psum[:, XB[t % 4], :], win[:, k, t * P:(t + 1) * P], xn_t[:, k, :],
                                     start=(k == 0), stop=(k == CK - 1))
                last.then_inc(m_xz, 1)

            for t in range(DT):
                in_proj(t)
            pe.wait_ge(r_oh, 1)
            for e in range(E):
                for j in range(SC):
                    last = pe.matmul(psum[:, 7, e * TT:(e + 1) * TT], onehot[:, j * E + e, :],
                                     onetile[:, j * E + e, :], start=(j == 0), stop=(j == SC - 1))
            last.then_inc(r_cnt, 1)
            in_proj(DT)
            in_proj(DT + 1)

            def list_slots():
                pe.wait_ge(r_val, 2)
                upto = psum[:, 7, 64:64 + TT * E].rearrange("p (t e) -> p t e", e=E)
                pe.matmul(upto, upto_ones[:], valid[:], start=True, stop=False)
                for t in range(TT - 1):
                    pe.matmul(upto[:, t + 1:, :], ones[:], valid[:, t:t + 1, :].to_broadcast((P, TT - 1 - t, E)),
                              start=False, stop=(t == TT - 2))
                for t in range(TT):
                    last = pe.matmul(psum[:, 7, 128:128 + E], ones[:], valid[:, t, :], start=(t == 0),
                                     stop=(t == TT - 1))
                last.then_inc(r_pre, 1)

            pe.wait_ge(ld_comb, 32)
            pe.transpose(psum[:, 5, 0:E * FT], b1_rows[:], ident[0:E * FT, 0:E * FT]).then_inc(r_b1, 1)
            for d in range(DT):
                pe.wait_ge(m_xc, d + 1)
                last = pe.matmul(psum[0:NR, 2, :], wxp[:, d, :], xc[:, d, :], start=(d == 0), stop=(d == DT - 1))
            last.then_inc(m_dbc, 1)
            list_slots()
            def spread(where, r):
                same = pair_r[:, r:r + 1].to_broadcast((NR, P))
                return pe.matmul(where, same, dbc[:], start=True, stop=True)

            pe.wait_ge(m_dlo, 1)
            pe.wait_ge(m_sel, 1)
            spread(psum[:, 2, :], 0)
            pe.wait_ge(r_b1e, 1)
            spread(psum[:, 5, :], 0).then_inc(m_dt0, 2)
            for t in range(DT + 2, 2 * DT):
                in_proj(t)

            def spread_in(n):
                if n >= 1:
                    pe.wait_ge(m_bs, n)
                spread(psum[:, 4, :], 1 + n).then_inc(m_b, 1)

            def spread_out(n):
                if n >= 2:
                    pe.wait_ge(m_rd, n - 1)
                spread(psum[:, 5 + n % 2, :], 1 + NS + n).then_inc(m_c, 1)

            def turn_pick(e, bank):
                for t in range(TT):
                    last = pe.transpose(psum[:, bank, t * P:(t + 1) * P], pick[:, t, e, :].bitcast(F32), ident[:])
                last.then_inc(f_turn, 1)

            spread_in(0)
            spread_in(1)
            pe.wait_ge(m_dtu, 1)
            spread_out(0)
            spread_in(2)
            pe.wait_ge(m_xze, 2 * DT)
            spread_out(1)
            for n in range(NS):
                if n + 3 < NS:
                    spread_in(n + 3)
                if n + 2 < NS:
                    spread_out(n + 2)
                pe.wait_ge(m_rd, n + 1)
                for d in range(DT):
                    last = pe.matmul(psum[:, d, :], ident[:], read[n % 2][:, d, :], start=(n == 0),
                                     stop=(n == NS - 1))
                    if n == NS - 1:
                        last.then_inc(m_acc, 1)
                if n < NS - 1:
                    last.then_inc(m_acc, 1)
                job = n - 2
                if 0 <= job < E:
                    if job == 0:
                        pe.wait_ge(f_pick, 1)
                        pe.wait_ge(r_pos, 2)
                    else:
                        pe.wait_ge(f_turned, job)
                    turn_pick(job, 7)
                elif job == E:
                    pe.wait_ge(f_turned, E)
                    for t in range(TT):
                        last = pe.transpose(psum[0:E, 7, t * P:(t + 1) * P], coef[:, t, :], ident[:])
                    last.then_inc(f_ct, 1)
                elif job == E + 1:
                    pe.wait_ge(f_cte, 1)
                    pe.wait_ge(ld_b2, 16)
                    pe.matmul(psum[:, 7, :], b2_sb[:, 0:P], coef_t[:], start=True, stop=True).then_inc(f_b2, 1)
                elif job == E + 2:
                    pe.wait_ge(f_b2e, 1)
                    pe.matmul(psum[:, 7, :], b2_sb[:, P:2 * P], coef_t[:], start=True, stop=True).then_inc(f_b2, 1)

            def turn_picks(r, side):
                for e in range(side * RING, (side + 1) * RING):
                    if side == 1:
                        pe.wait_ge(f_turned, E * r + e - RING + 1)
                    turn_pick(e, 4 + e % RING)

            pe.wait_ge(m_bs, NS)
            pe.wait_ge(m_rd, NS)
            pe.wait_ge(f_b2e, CK)
            for d in range(DT):
                pe.wait_ge(m_y, d + 1)
                for t in range(TT):
                    last = pe.matmul(psum[:, 4 + t, 0:C], conv[:, d, t * P:(t + 1) * P], wout[:, d, :],
                                     start=(d == 0), stop=(d == DT - 1))
                    if d == DT - 1:
                        last.then_inc(m_yo, 1)

            def slot_weights(r):
                pe.wait_ge(f_hl, 1)
                if not isinstance(r, int):
                    pe.wait_ge(f_turned, E * r + RING + 1)
                for e in range(E):
                    for t in range(TT):
                        last = pe.matmul(psum[:, 4, 2 * e:2 * e + 2], pick[:, t, e, :], coef_hl[:, t, e, :],
                                         start=(t == 0), stop=(t == TT - 1))
                last.then_inc(f_cs, 1)

            def expert_round(r):
                for g in range(EG):
                    if g == 1 and not isinstance(r, int):
                        pe.wait_ge(f_turned, E * (r + 1))
                    for k in range(CK):
                        for t in range(TT):
                            for part in (f_hi, f_lo):
                                last = pe.matmul(psum[:, GB[g] + k, :], part[:, t, k * P:(k + 1) * P],
                                                 pick[:, t, g * RING:(g + 1) * RING, :].rearrange("p e s -> p (e s)"),
                                                 start=(t == 0 and part is f_hi), stop=(t == TT - 1 and part is f_lo))
                        last.then_inc(f_gat, 1)
                pe.wait_ge(f_gate, CK * (EG * r + 1))

                def to_tokens(q, i):
                    pe.wait_ge(f_ol, E * r + RING * q + i + 1)
                    if i == 0:
                        pe.wait_ge(f_gate, CK * EG * (r + 1))
                        pe.wait_ge(f_sce, CK * (EG * r + q + 1))
                    for k in range(CK):
                        for part in (o_hi, o_lo):
                            last = pe.matmul(psum[:, 6 + k, :], part[:, k * P:(k + 1) * P],
                                             pick_t[:, ds(RING * q + i, 1), :].rearrange("p e t -> p (e t)"),
                                             start=(i == 0 and part is o_hi), stop=(i == RING - 1 and part is o_lo))
                    return last

                apart(pe)
                with pe.Fori(0, EG) as q:
                    for i in range(RING):
                        e = E * r + RING * q + i
                        pe.wait_ge(ld_e[i], 32 * (EG * r + q + 1))
                        for f in range(FT):
                            if f >= 4:
                                pe.wait_ge(f_he, FT * e + f - 3)
                            for k in range(CK):
                                last = pe.matmul(psum[:, f % 4, 0:P], w1[i][:, k, f * P:(f + 1) * P],
                                                 xg_t[:, k, ds(RING * q + i, 1), :].rearrange("p e s -> p (e s)"),
                                                 start=(k == 0), stop=(k == CK - 1))
                            last.then_inc(f_h, 1)
                        if i > 0:
                            to_tokens(q, i - 1)
                        pe.wait_ge(f_he, FT * (e + 1))
                        if i == 0:
                            pe.wait_ge(f_cse, r + 1)
                        for f in range(FT):
                            last = pe.matmul(psum[:, 4 + i % 2, 0:C], hid[:, f, :], w2[i][:, f, :],
                                             start=(f == 0), stop=(f == FT - 1))
                        last.then_inc(f_o, 1)
                    to_tokens(q, RING - 1).then_inc(f_sc, 1)

            pe.wait_ge(m_out, TT)
            slot_weights(0)
            pe.wait_ge(f_lo_done, TT)
            expert_round(0)

            def next_round(r):
                pe.wait_ge(f_pick, r + 1)
                pe.wait_ge(f_sce, CK * (EG * r + 1))
                turn_picks(r, 0)
                turn_picks(r, 1)
                slot_weights(r)
                expert_round(r)

            further_rounds(pe, next_round)
            pe.wait_ge(f_all, ROUNDS)
            for t in range(TT):
                for k in range(CK):
                    last = pe.transpose(psum[:, t, k * P:(k + 1) * P], acc_t[:, k, t * P:(t + 1) * P], ident[:])
                last.then_inc(f_fin, 1)


_INS = ['x', 'ctx_1024', 'L0_xattn_Wq', 'L0_xattn_Wkv', 'L0_xattn_Wo', 'L0_xattn_ln1_w', 'L0_xattn_ln1_b',
        'L0_xattn_ln2_w', 'L0_xattn_ln2_b', 'L0_attn_norm_w', 'L0_attn_norm_b', 'L0_attn_W_in', 'L0_attn_conv_w',
        'L0_attn_conv_b', 'L0_attn_x_proj_w', 'L0_attn_dt_w', 'L0_attn_dt_b', 'L0_attn_A_log', 'L0_attn_D',
        'L0_attn_W_out', 'L0_ffn_combine_weights', 'L0_ffn_top_idx', 'L0_ffn_W1', 'L0_ffn_b1', 'L0_ffn_W2',
        'L0_ffn_b2']
_OUTS = [((8, 64, 256), 'float32')]


def kernel(**inputs):
    import numpy as _np
    import concourse.bacc as _bacc
    from concourse import mybir as _mybir
    from concourse.bass_utils import run_bass_kernel_spmd as _run

    nc = _bacc.Bacc("TRN2", target_bir_lowering=False, num_devices=1)
    arrays, args = {}, []
    for name in _INS:
        a = _np.ascontiguousarray(inputs[name])
        arrays[f"in_{name}_dram"] = a
        args.append(nc.dram_tensor(f"in_{name}_dram", a.shape, _mybir.dt.from_np(a.dtype), kind="ExternalInput").ap())
    for i, (shape, dtype) in enumerate(_OUTS):
        dt = _mybir.dt.from_np(_np.dtype(dtype))
        args.append(nc.dram_tensor(f"out_{i}_dram", shape, dt, kind="ExternalOutput").ap())
    perceiver_kernel(nc, *args)
    r = _run(nc, [arrays], core_ids=[0])
    got = tuple(r.results[0][f"out_{i}_dram"] for i in range(len(_OUTS)))
    return got[0]
```
